# Optimizing a Trainium2 kernel written in Bass

```python
import numpy as np
import jax
import jax.numpy as jnp

def _softmax(x, axis=-1):
    return jax.nn.softmax(x, axis=axis)

def _gelu(x):
    return jax.nn.gelu(x, approximate=True)

def _silu(x):
    return jax.nn.silu(x)

def _sigmoid(x):
    return jax.nn.sigmoid(x)

def _layernorm(x, axis=-1, eps=1e-05):
    m = jnp.mean(x, axis=axis, keepdims=True)
    v = jnp.var(x, axis=axis, keepdims=True)
    return (x - m) / jnp.sqrt(v + eps)

def _scatter_add(tgt, idx, src, axis=0):
    return tgt.at[idx].add(src)

def _segment_sum(src, seg, n):
    return jax.ops.segment_sum(src, seg, n)
kernel_name = 'mk_cond_seq_d2_seqx_r4_060ba0'

def setup_inputs(seed: int=0):
    np.random.seed(seed)
    _w = jnp.asarray

    def _rec_inputs():
        import jax
        import jax.numpy as jnp
        _rk = jax.random.key(seed)
        x = 7.22e-05 + 1 * jax.random.normal(jax.random.fold_in(_rk, 1), (4, 512, 256), jnp.float32)
        _lenS = 512 - jax.random.randint(jax.random.fold_in(_rk, 7), (4,), 0, max(1, 512 // 4) + 1, jnp.int32)
        _lenS2 = 512 - jax.random.randint(jax.random.fold_in(_rk, 8), (4,), 0, max(1, 512 // 4) + 1, jnp.int32)
        cond_2048 = 0.00386106 + 1.00199 * jax.random.normal(jax.random.fold_in(_rk, 11), (4, 512), jnp.float32)
        _validS = jnp.arange(512)[None, :] < _lenS[:, None]
        _validS2 = jnp.arange(512)[None, :] < _lenS2[:, None]
        _causal = jnp.tril(jnp.ones((512, 512), dtype=bool))
        mask_BxS_ff1 = jnp.where(jnp.ones((4, 512), dtype=bool), 1.0, 0.0).astype(jnp.float32)
        mask_BxS_ik0 = jnp.where(jnp.broadcast_to(_validS[:, :], (4, 512)), 0, 1).astype(jnp.int32)
        return (x, cond_2048, mask_BxS_ff1, mask_BxS_ik0)
    x, cond_2048, mask_BxS_ff1, mask_BxS_ik0 = _rec_inputs()

    def _L0_cond_setup():
        import jax, jax.numpy as jnp
        import numpy as np
        B, T, D, H, TE = (8, 256, 256, 16, 512)
        LN_EPS = 1e-05

        def layer_norm(x, w, b):
            m = jnp.mean(x, axis=-1, keepdims=True)
            v = jnp.var(x, axis=-1, keepdims=True)
            return (x - m) / jnp.sqrt(v + LN_EPS) * w + b
        key = jax.random.key(seed)
        ks = jax.random.split(key, 8)
        s = lambda k, sh: jax.random.normal(k, sh, jnp.float32) * 0.02
        return dict(x=jax.random.normal(ks[0], (B, T, D), jnp.float32), emb=jax.random.normal(ks[1], (B, TE), jnp.float32), src_mask=jnp.ones((B, T), jnp.float32), norm_w=jnp.ones((D,), jnp.float32), norm_b=jnp.zeros((D,), jnp.float32), q_w=s(ks[2], (D, D)), q_b=jnp.zeros((D,), jnp.float32), k_w=s(ks[3], (D, D)), k_b=jnp.zeros((D,), jnp.float32), v_w=s(ks[4], (D, D)), v_b=jnp.zeros((D,), jnp.float32), emb_w=s(ks[5], (TE, 2 * D)), emb_b=jnp.zeros((2 * D,), jnp.float32), sb_norm_w=jnp.ones((D,), jnp.float32), sb_norm_b=jnp.zeros((D,), jnp.float32), out_w=s(ks[6], (D, D)), out_b=jnp.zeros((D,), jnp.float32))
    _L0_cond_all = _L0_cond_setup()
    _L0_cond_in = {k: v for k, v in _L0_cond_all.items() if k in ('norm_w', 'norm_b', 'q_w', 'q_b', 'k_w', 'k_b', 'v_w', 'v_b', 'emb_w', 'emb_b', 'sb_norm_w', 'sb_norm_b', 'out_w', 'out_b')}
    del _L0_cond_all

    def _L1_cond_setup():
        import jax, jax.numpy as jnp
        import numpy as np
        H = 16
        LN_EPS = 1e-05

        def _layernorm(x, scale, bias):
            mu = jnp.mean(x, axis=-1, keepdims=True)
            var = jnp.var(x, axis=-1, keepdims=True)
            return (x - mu) * jax.lax.rsqrt(var + LN_EPS) * scale + bias
        key = jax.random.key(seed)
        ks = jax.random.split(key, 8)
        B, T, D, E = (4, 1024, 256, 512)
        s = 0.02
        return {'x': jax.random.normal(ks[0], (B, T, D), jnp.float32), 'emb': jax.random.normal(ks[1], (B, E), jnp.float32), 'src_mask': jax.random.randint(ks[2], (B, T), 0, 2).astype(jnp.int32), 'norm_scale': jnp.ones((D,), jnp.float32), 'norm_bias': jnp.zeros((D,), jnp.float32), 'Wq': jax.random.normal(ks[3], (D, D), jnp.float32) * s, 'bq': jnp.zeros((D,), jnp.float32), 'Wk': jax.random.normal(ks[4], (D, D), jnp.float32) * s, 'bk': jnp.zeros((D,), jnp.float32), 'Wv': jax.random.normal(ks[5], (D, D), jnp.float32) * s, 'bv': jnp.zeros((D,), jnp.float32), 'film_emb_W': jax.random.normal(ks[6], (E, 2 * D), jnp.float32) * s, 'film_emb_b': jnp.zeros((2 * D,), jnp.float32), 'film_norm_scale': jnp.ones((D,), jnp.float32), 'film_norm_bias': jnp.zeros((D,), jnp.float32), 'film_out_W': jax.random.normal(ks[7], (D, D), jnp.float32) * s, 'film_out_b': jnp.zeros((D,), jnp.float32)}
    _L1_cond_all = _L1_cond_setup()
    _L1_cond_in = {k: v for k, v in _L1_cond_all.items() if k in ('norm_scale', 'norm_bias', 'Wq', 'bq', 'Wk', 'bk', 'Wv', 'bv', 'film_emb_W', 'film_emb_b', 'film_norm_scale', 'film_norm_bias', 'film_out_W', 'film_out_b')}
    del _L1_cond_all
    return {'x': x, 'cond_2048': cond_2048, 'mask_BxS_ff1': mask_BxS_ff1, 'mask_BxS_ik0': mask_BxS_ik0, 'L0_cond_norm_w': _L0_cond_in['norm_w'], 'L0_cond_norm_b': _L0_cond_in['norm_b'], 'L0_cond_q_w': _L0_cond_in['q_w'], 'L0_cond_q_b': _L0_cond_in['q_b'], 'L0_cond_k_w': _L0_cond_in['k_w'], 'L0_cond_k_b': _L0_cond_in['k_b'], 'L0_cond_v_w': _L0_cond_in['v_w'], 'L0_cond_v_b': _L0_cond_in['v_b'], 'L0_cond_emb_w': _L0_cond_in['emb_w'], 'L0_cond_emb_b': _L0_cond_in['emb_b'], 'L0_cond_sb_norm_w': _L0_cond_in['sb_norm_w'], 'L0_cond_sb_norm_b': _L0_cond_in['sb_norm_b'], 'L0_cond_out_w': _L0_cond_in['out_w'], 'L0_cond_out_b': _L0_cond_in['out_b'], 'L1_cond_norm_scale': _L1_cond_in['norm_scale'], 'L1_cond_norm_bias': _L1_cond_in['norm_bias'], 'L1_cond_Wq': _L1_cond_in['Wq'], 'L1_cond_bq': _L1_cond_in['bq'], 'L1_cond_Wk': _L1_cond_in['Wk'], 'L1_cond_bk': _L1_cond_in['bk'], 'L1_cond_Wv': _L1_cond_in['Wv'], 'L1_cond_bv': _L1_cond_in['bv'], 'L1_cond_film_emb_W': _L1_cond_in['film_emb_W'], 'L1_cond_film_emb_b': _L1_cond_in['film_emb_b'], 'L1_cond_film_norm_scale': _L1_cond_in['film_norm_scale'], 'L1_cond_film_norm_bias': _L1_cond_in['film_norm_bias'], 'L1_cond_film_out_W': _L1_cond_in['film_out_W'], 'L1_cond_film_out_b': _L1_cond_in['film_out_b']}

def reference(x, cond_2048, mask_BxS_ff1, mask_BxS_ik0, L0_cond_norm_w, L0_cond_norm_b, L0_cond_q_w, L0_cond_q_b, L0_cond_k_w, L0_cond_k_b, L0_cond_v_w, L0_cond_v_b, L0_cond_emb_w, L0_cond_emb_b, L0_cond_sb_norm_w, L0_cond_sb_norm_b, L0_cond_out_w, L0_cond_out_b, L1_cond_norm_scale, L1_cond_norm_bias, L1_cond_Wq, L1_cond_bq, L1_cond_Wk, L1_cond_bk, L1_cond_Wv, L1_cond_bv, L1_cond_film_emb_W, L1_cond_film_emb_b, L1_cond_film_norm_scale, L1_cond_film_norm_bias, L1_cond_film_out_W, L1_cond_film_out_b):
    import jax
    import jax.numpy as jnp

    def _L0_cond_ref(x, emb, src_mask, norm_w, norm_b, q_w, q_b, k_w, k_b, v_w, v_b, emb_w, emb_b, sb_norm_w, sb_norm_b, out_w, out_b):
        import jax, jax.numpy as jnp
        import numpy as np
        B, T, D, H, TE = (8, 256, 256, 16, 512)
        LN_EPS = 1e-05

        def layer_norm(x, w, b):
            m = jnp.mean(x, axis=-1, keepdims=True)
            v = jnp.var(x, axis=-1, keepdims=True)
            return (x - m) / jnp.sqrt(v + LN_EPS) * w + b
        Bx, Tx, Dx = x.shape
        xn = layer_norm(x, norm_w, norm_b)
        q = (xn @ q_w + q_b).reshape(Bx, Tx, H, -1)
        k = (xn @ k_w + k_b).reshape(Bx, Tx, H, -1)
        att = jnp.einsum('bnhl,bmhl->bnmh', q, k)
        mask = src_mask.reshape(Bx, 1, Tx, 1)
        att = att + (1.0 - mask) * -1000000.0
        att = jax.nn.softmax(att, axis=2)
        v = ((xn @ v_w + v_b) * src_mask[:, :, None]).reshape(Bx, Tx, H, -1)
        y = jnp.einsum('bnmh,bmhl->bnhl', att, v).reshape(Bx, Tx, Dx)
        e = jax.nn.silu(emb) @ emb_w + emb_b
        scale, shift = jnp.split(e[:, None, :], 2, axis=2)
        h = layer_norm(y, sb_norm_w, sb_norm_b) * (1.0 + scale) + shift
        h = jax.nn.silu(h) @ out_w + out_b
        return x + h

    def _L1_cond_ref(x, emb, src_mask, norm_scale, norm_bias, Wq, bq, Wk, bk, Wv, bv, film_emb_W, film_emb_b, film_norm_scale, film_norm_bias, film_out_W, film_out_b):
        import jax, jax.numpy as jnp
        import numpy as np
        H = 16
        LN_EPS = 1e-05

        def _layernorm(x, scale, bias):
            mu = jnp.mean(x, axis=-1, keepdims=True)
            var = jnp.var(x, axis=-1, keepdims=True)
            return (x - mu) * jax.lax.rsqrt(var + LN_EPS) * scale + bias
        B, T, D = x.shape
        dh = D // H
        xn = _layernorm(x, norm_scale, norm_bias)
        q = xn @ Wq + bq
        k = xn @ Wk + bk
        v = xn @ Wv + bv
        mask = (src_mask == 1)[:, :, None]
        k = jnp.where(mask, -jnp.inf, k)
        v = jnp.where(mask, 0.0, v)
        q = q.reshape(B, T, H, dh).transpose(0, 2, 1, 3)
        k = k.reshape(B, T, H, dh).transpose(0, 2, 1, 3)
        v = v.reshape(B, T, H, dh).transpose(0, 2, 1, 3)
        q = jax.nn.softmax(q, axis=-1)
        k = jax.nn.softmax(k, axis=2)
        attn = jnp.einsum('bhse,bhsd->bhed', k, v)
        y = jnp.einsum('bhtd,bhed->bhte', q, attn)
        y = y.transpose(0, 2, 1, 3).reshape(B, T, D)
        emb_out = jax.nn.silu(emb) @ film_emb_W + film_emb_b
        scale, shift = jnp.split(emb_out, 2, axis=-1)
        h = _layernorm(y, film_norm_scale, film_norm_bias) * (1.0 + scale[:, None, :]) + shift[:, None, :]
        h = jax.nn.silu(h) @ film_out_W + film_out_b
        return x + h
    x = _L0_cond_ref(x, cond_2048, mask_BxS_ff1, L0_cond_norm_w, L0_cond_norm_b, L0_cond_q_w, L0_cond_q_b, L0_cond_k_w, L0_cond_k_b, L0_cond_v_w, L0_cond_v_b, L0_cond_emb_w, L0_cond_emb_b, L0_cond_sb_norm_w, L0_cond_sb_norm_b, L0_cond_out_w, L0_cond_out_b)
    x = _L1_cond_ref(x, cond_2048, mask_BxS_ik0, L1_cond_norm_scale, L1_cond_norm_bias, L1_cond_Wq, L1_cond_bq, L1_cond_Wk, L1_cond_bk, L1_cond_Wv, L1_cond_bv, L1_cond_film_emb_W, L1_cond_film_emb_b, L1_cond_film_norm_scale, L1_cond_film_norm_bias, L1_cond_film_out_W, L1_cond_film_out_b)
    return x

_drawn_inputs = setup_inputs


def setup_inputs(seed=0):
    import zlib

    import numpy as np

    out = dict(_drawn_inputs(seed))
    spreads = {'L0_cond_norm_w': (1.0, 0.6),
     'L0_cond_norm_b': (0.0, 0.1),
     'L0_cond_q_b': (0.0, 0.8),
     'L0_cond_k_b': (0.0, 0.8),
     'L0_cond_v_b': (0.0, 0.1),
     'L0_cond_emb_b': (0.0, 0.1),
     'L0_cond_sb_norm_w': (1.0, 0.2),
     'L0_cond_sb_norm_b': (0.0, 0.303),
     'L0_cond_out_b': (0.0, 0.1),
     'L1_cond_norm_scale': (1.0, 0.2),
     'L1_cond_norm_bias': (0.0, 0.1),
     'L1_cond_bq': (0.0, 0.451),
     'L1_cond_bk': (0.0, 0.8),
     'L1_cond_bv': (0.0, 0.1),
     'L1_cond_film_emb_b': (0.0, 0.1),
     'L1_cond_film_norm_scale': (1.0, 0.2),
     'L1_cond_film_norm_bias': (0.0, 0.382),
     'L1_cond_film_out_b': (0.0, 0.1)}
    factors = {'L0_cond_q_w': 2.698, 'L1_cond_Wk': 3.318}
    for name, (base, spread) in spreads.items():
        noise = np.random.default_rng([zlib.crc32(name.encode()), seed]).standard_normal(out[name].shape)
        drawn = base * np.exp(spread * noise) if base else spread * noise
        out[name] = jnp.asarray(drawn.astype(out[name].dtype))
    for name, factor in factors.items():
        out[name] = (out[name] * factor).astype(out[name].dtype)
    return out
```

```python
import concourse.bass as bass
from concourse import mybir
from contextlib import ExitStack

F32 = mybir.dt.float32
F32R = mybir.dt.float32r
BF16 = mybir.dt.bfloat16
I32 = mybir.dt.int32
ALU = mybir.AluOpType
ACT = mybir.ActivationFunctionType
AX = mybir.AxisListType

P = 128
LN_EPS = 1e-5
MASK_PENALTY = 1e6
HIDDEN_KEY = -1e30
RSQRT_GUESS = 1597463007.0
NEWTON_STEPS = 3

ROW_MASK = 64
ROW_MAX = 96
ROWS_SCORE = 96
ROWS_SHIFTED = 98

PLACES = {
    0: [[], [], [], [("v", 0)]],
    1: [[("v", 1), ("ln_next", 0)], [("ln_a", 0)], [("z_next", 0)], [("z_a", 0)]],
    2: [[("c", 1)], [("zt", 0)], [("zt", 1)], [("film_a", 0)]],
    3: [[("film_a", 1)], [("qk", 0)], [("qk", 1)], []],
    4: [[("out_a", 0)], [("out_a", 1)], [("ln_b", 0)], [("z_b", 0)]],
    5: [[("qk", 2)], [("qk", 3)], [], []],
    6: [[("c", 2)], [("z1t", 0)], [("z1t", 1)], []],
    7: [[("k1", 0)], [("k1", 1)], [("qv", 0)], []],
    8: [[("qv", 1)], [("qv", 2)], [("qv", 3)], [("softmax_q", 0)]],
    9: [[("k1t", 0)], [("k1t", 1)], [], []],
    10: [[("c", 3)], [("q1t", 0)], [("q1t", 1)], []],
    11: [[("attn", 0)], [], [], []],
    12: [[("y1", 0)], [("y1", 1)], [("ln_c", 0)], [("z_c", 0)]],
    13: [[], [], [], []],
    14: [[("c", 0)], [("film_c", 0)], [("film_c", 1)], []],
    15: [[("out_c", 0)], [("out_c", 1)], [], []],
}
NEXT = ("zt", "qk", "ln_next", "z_next")
OWN = ("v", "c")


def film_seq_kernel(nc, x, cond_2048, mask_BxS_ff1, mask_BxS_ik0,
                    norm_w0, norm_b0, q_w0, q_b0, k_w0, k_b0, v_w0, v_b0, emb_w0, emb_b0,
                    film_w0, film_b0, out_w0, out_b0,
                    norm_w1, norm_b1, q_w1, q_b1, k_w1, k_b1, v_w1, v_b1, emb_w1, emb_b1,
                    film_w1, film_b1, out_w1, out_b1, out):
    B, T, D = x.shape
    E = cond_2048.shape[1]
    H, DH = 16, 16
    TT = T // P
    KC = D // P
    EC = E // P
    HG = 4
    G = H // HG
    LEAD = 6
    assert T == 512 and D == H * DH == 256 and B == 4 and 2 * D == E

    ctx = ExitStack()
    with ctx:
        def sb(name, shape, dt=F32, scope=ctx):
            return scope.enter_context(nc.sbuf_tensor(name, shape, dt))

        def sem(name):
            return ctx.enter_context(nc.semaphore(name))

        wh = sb("w_hi", [P, 8, KC, D], F32R)
        wl = sb("w_lo", [P, 8, KC, D], F32R)
        Q0, K0, V0, K1, Q1, V1, O0, O1 = range(8)
        ident = sb("ident", [P, P])
        blocks = sb("blocks", [P, P], BF16)
        ones_row = sb("ones_row", [1, P], F32R)
        cols = sb("cols", [P, 56])
        own_key = sb("own_key", [P, B * TT])
        bias_cols = sb("bias_cols", [P, 6])
        bias_hi = sb("bias_hi", [1, 3 * D], F32R)
        bias_lo = sb("bias_lo", [1, 3 * D], F32R)
        film_s = sb("film_s", [P, 2, KC, B])
        film_t = sb("film_t", [P, 2, KC, B])
        outb = sb("outb", [P, 2, D])
        film_now = sb("film_now", [P, 2, 2, KC])
        mcol_now = sb("mcol_now", [P, TT])
        own_now = sb("own_now", [P, TT])
        x_in = sb("x_in", [P, TT, D])
        mrow = sb("mrow", [1, T])
        mrow_hi = sb("mrow_hi", [1, T], F32R)
        mrow_lo = sb("mrow_lo", [1, T], F32R)
        zt_hi = sb("zt_hi", [P, KC, T], F32R)
        zt_lo = sb("zt_lo", [P, KC, T], F32R)
        qk_hi = sb("qk_hi", [P, 2, KC, T], F32R)
        qk_lo = sb("qk_lo", [P, 2, KC, T], F32R)
        v_aug = sb("v_aug", [P, TT, H, DH + 1])
        probs = sb("probs", [P, 2, TT, T])
        negmax = sb("negmax", [P, 2, HG * TT])
        crow_hi = sb("crow_hi", [HG * TT, P], F32R)
        crow_lo = sb("crow_lo", [HG * TT, P], F32R)
        recip = sb("recip", [P, HG * TT])
        y0 = sb("y0", [P, TT, D])
        yk = sb("yk", [P, TT, D])
        zn = sb("zn", [P, TT, D])
        x_res = sb("x_res", [P, TT, D])
        film_u = sb("film_u", [P, T])
        film_h = sb("film_h", [P, KC, T])
        at_hi = sb("at_hi", [P, KC, T], F32R)
        at_lo = sb("at_lo", [P, KC, T], F32R)
        q1 = sb("q1_sb", [P, TT, D])
        v1 = sb("v1_sb", [P, TT, D])
        k1 = sb("k1_sb", [P, KC, T])
        q1t = k1
        hide = sb("hide", [P, T])
        attn = sb("attn_sb", [P, KC, P])
        q1max = sb("q1max", [P, TT, H])
        q1sum = sb("q1sum", [P, TT * H])
        q1rec = sb("q1rec", [P, TT * H])
        k1max = sb("k1max", [P, KC])
        k1sum = sb("k1sum", [P, KC])
        k1rec = sb("k1rec", [P, KC])
        three_halves = sb("three_halves", [P, TT])
        ln = {n: dict(stats=sb(f"stats_{n}", [P, TT, 6]), sum=sb(f"sum_{n}", [P, TT, 2]),
                      diff=sb(f"diff_{n}", [P, TT]), mean=sb(f"mean_{n}", [P, TT]),
                      var=sb(f"var_{n}", [P, TT]), nhalf=sb(f"nhalf_{n}", [P, TT]), y=sb(f"rstd_{n}", [P, TT]),
                      t=sb(f"newton_{n}", [P, TT])) for n in ("next", "last")}

        s_ps = [ctx.enter_context(nc.psum_tensor(f"s_ps{i}", [P, 2 * T], F32)) for i in range(2)]
        m_ps = [ctx.enter_context(nc.psum_tensor(f"m_ps{i}", [P, T], F32)) for i in range(2)]
        y_ps = ctx.enter_context(nc.psum_tensor("y_ps", [P, 512], F32))
        w_ps = ctx.enter_context(nc.psum_tensor("w_ps", [P, 512], F32))
        y_v = y_ps[:, 0:HG * TT * (DH + 1)].rearrange("p (h t d) -> p h t d", h=HG, t=TT)

        vec_in, bias_in, outb_in, emb_in = sem("vec_in"), sem("bias_in"), sem("outb_in"), sem("emb_in")
        w_in = [sem(f"w_in{i}") for i in range(4)]
        const_set, ones_set, cols_mm, cols_set = sem("const_set"), sem("ones_set"), sem("cols_mm"), sem("cols_set")
        hid_rows, perm_set, bias_mm, bias_set = sem("hid_rows"), sem("perm_set"), sem("bias_mm"), sem("bias_set")
        cond_set, film_mm, film_set = sem("cond_set"), sem("film_mm"), sem("film_set")
        w_hi_set, w_lo_set, stack_set = sem("w_hi_set"), sem("w_lo_set"), sem("stack_set")

        PER = {}

        def batch_sem(name, per):
            s = sem(name)
            PER[name] = per
            return s

        def at(name, b, n):
            return PER[name] * b + n

        S = {name: batch_sem(name, per) for name, per in dict(
            x_in=16, mrow_in=16, mrow_shift=1, mrow_hi=1, mrow_lo=1, mcol=1, own=1, film_now=2,
            bn_next=12, newton_next=4 * NEWTON_STEPS, z_next=4,
            bn_a=12, newton_a=4 * NEWTON_STEPS, z_a=4,
            bn_b=12, newton_b=4 * NEWTON_STEPS, z_b=4,
            bn_c=12, newton_c=4 * NEWTON_STEPS, z_c=4,
            zt_mm=2, zt_hi=2, zt_lo=2, qk_mm=4, qk_hi=4, qk_lo=4, v_mm=2, v_set=4,
            m_mm=64, m_red=64, c_mm=4, c_hi=4, c_lo=4,
            s_mm=32, exp=32, pv=16, y_rec=4, y_set=4,
            res_in=16, res_b=1, hide_in=16, hide_set=1,
            fa_mm=2, fa_u=2, fa_t=2, fa_h=2, fa_hi=2, fa_lo=2,
            fc_mm=2, fc_u=2, fc_t=2, fc_h=2, fc_hi=2, fc_lo=2,
            oa_mm=2, oa_set=2, res_c=1, z1_mm=2, z1_hi=2, z1_lo=2,
            k1_mm=2, k1_b=2, k1_max=2, k1_exp=2, k1_rec=2, k1_n=2,
            qv_mm=4, v1_set=4, q1_max=4, q1_sub=4, q1_exp=1, q1_sum=1, q1_rec=1,
            kt_mm=2, kt_set=2, qt_mm=2, qt_set=2, at_mm=1, at_set=1, y1_mm=2, y1_set=4,
            oc_mm=2, oc_set=2, stored=16).items()}
        c_in = [sem("c_in0"), sem("c_in1")]
        fill = [sem(f"fill{g}") for g in range(G)]

        prep = ExitStack()
        wraw = sb("wraw", [P, 8, KC, D], F32, prep)
        wperm = sb("wperm", [P, 2, KC, D], F32, prep)
        embw = sb("embw", [P, 2, EC, 2 * D], F32, prep)
        vrows = sb("vrows", [56, P], F32, prep)
        hrows_i = sb("hrows_i", [B * TT, P], I32, prep)
        hrows = sb("hrows", [B * TT, P], F32, prep)
        brow = sb("brow", [1, 6, D], F32, prep)
        bperm = sb("bperm", [1, 2, D], F32, prep)
        one1 = sb("one1", [1, 1], F32, prep)
        cond_t = sb("cond_t", [P, B * EC], F32, prep)
        cond_h = sb("cond_h", [P, B * EC], F32, prep)
        cond_s = sb("cond_s", [P, B * EC], F32, prep)
        emb_e = sb("emb_e", [P, 2, 2, KC, B], F32, prep)
        emb_p = sb("emb_p", [P, 2, KC, B], F32, prep)
        emb_q = sb("emb_q", [P, 2, KC, B], F32, prep)
        prep.close()
        qs = sb("q_stack", [P, H, T], F32R)
        ks = sb("k_stack", [P, H, T], F32R)

        NW0, NB0, NW1, NB1, FW0, FB0, FW1, FB1 = range(0, 16, 2)
        EB = 16
        CD = 24
        MC = 40
        fcols = cols[:, FW0:FW0 + 8].rearrange("p (l w c) -> p l w c", l=2, w=2)

        def scale_col(w, c):
            n = NW0 if w in (Q0, K0, V0) else NW1
            return cols[:, n + c:n + c + 1]

        def tiles(ap):
            return ap.rearrange("(t p) d -> p t d", p=P)

        def regroup(ap):
            return ap.rearrange("p (g h d) -> p g d h", g=G, h=HG)

        block = ctx.enter_context(nc.Block())

        def batch_of(name, n, b, first, last):
            if name in NEXT or (name == "c" and n == 0):
                return None if last else b + 1
            if name in OWN:
                return b
            return None if first else b - 1

        def pieces(k, place, b, first, last):
            for name, n in PLACES[k][place]:
                bb = batch_of(name, n, b, first, last)
                if bb is not None:
                    yield name, n, bb

        LAST_ONLY = [(name, n) for k in range(H) for place in PLACES[k] for name, n in place
                     if name not in NEXT + OWN]

        def batches(eng, step, tail):
            for k in range(H):
                step(0, k, True, False)
            with eng.Fori(1, B - 1) as b:
                for k in range(H):
                    step(b, k, False, False)
            for k in range(H):
                step(B - 1, k, False, True)
            tail(B - 1)

        @block.sync
        def _(sp):
            def words(ap):
                return ap.bitcast(F32)

            row = 0
            for v, n in ((norm_w0, KC), (norm_b0, KC), (norm_w1, KC), (norm_b1, KC), (film_w0, KC),
                         (film_b0, KC), (film_w1, KC), (film_b1, KC), (emb_b0, EC), (emb_b1, EC)):
                sp.dma_start(vrows[row:row + n, :], v.rearrange("(c p) -> c p", p=P)).then_inc(vec_in, 16)
                row += n
            sp.dma_start(vrows[CD:CD + B * EC, :], cond_2048.rearrange("b (k p) -> (b k) p", p=P)).then_inc(vec_in, 16)
            sp.dma_start(vrows[MC:MC + B * TT, :], mask_BxS_ff1.rearrange("b (t p) -> (b t) p", p=P)).then_inc(vec_in, 16)
            sp.dma_start(hrows_i[:, :], mask_BxS_ik0.rearrange("b (t p) -> (b t) p", p=P)).then_inc(vec_in, 16)

            for i, v in enumerate((q_b0, k_b0, v_b0, k_b1, q_b1, v_b1)):
                sp.dma_start(brow[:, i, :], v.rearrange("(a n) -> a n", a=1)).then_inc(bias_in, 16)
            for i, w in enumerate((q_w0, k_w0, v_w0, k_w1, q_w1, v_w1, out_w0, out_w1)):
                sp.dma_start(wraw[:, i, :, :], w.rearrange("(c p) n -> p c n", p=P)).then_inc(w_in[i // 2], 16)
            for i, w in enumerate((emb_w0, emb_w1)):
                sp.dma_start(embw[:, i, :, :], w.rearrange("(c p) n -> p c n", p=P)).then_inc(emb_in, 16)
            for i, v in enumerate((out_b0, out_b1)):
                sp.dma_start(outb[:, i, :], v.rearrange("(a n) -> a n", a=1).broadcast_to([P, D])).then_inc(outb_in, 16)

            def fill_group(b, g):
                mc, part = g // 2, slice(64 * (g % 2), 64 * (g % 2) + 64)
                slots = slice(HG * g, HG * g + HG)
                for stack, i, order in ((qs, 0, (qk_hi, qk_hi, qk_lo, qk_lo)),
                                        (ks, 1, (qk_hi, qk_lo, qk_hi, qk_lo))):
                    for r, src in enumerate(order):
                        sp.dma_start(words(stack[DH * r:DH * r + DH, slots, :]), words(src[part, i, mc, :]))\
                          .then_inc(fill[g], 16)
                for r, src in enumerate((mrow_hi, mrow_lo)):
                    sp.dma_start(words(ks[ROW_MASK + r:ROW_MASK + r + 1, slots, :]),
                                 words(src[:, :]).unsqueeze(1).broadcast_to([1, HG, T])).then_inc(fill[g], 16)

            def shift_rows(b, g):
                sp.wait_ge(S["c_lo"], at("c_lo", b, g + 1))
                for r, src in enumerate((crow_hi, crow_lo)):
                    dst = qs[ROW_MAX + r:ROW_MAX + r + 1, HG * g:HG * g + HG, :]
                    sp.dma_start(words(dst).rearrange("a h (t p) -> a (h t) p", p=P), words(src[:, :]))\
                      .then_inc(c_in[g % 2], 16)

            def step(b, k, first, last):
                if k in (0, 7, 9, 13) and not (last and k > 0):
                    h = k + LEAD
                    sp.wait_ge(S["m_red"], at("m_red", b, TT * h + 1))
                    fill_group(*{0: (b, 3), 7: (b + 1, 0), 9: (b + 1, 1), 13: (b + 1, 2)}[k])
                if k in (2, 6, 10):
                    shift_rows(b, (k + 2) // 4)
                if not last and k == 14:
                    shift_rows(b + 1, 0)

            sp.wait_ge(stack_set, 3)
            for g in range(3):
                sp.wait_ge(S["mrow_lo"], 1)
                sp.wait_ge(S["qk_lo"], 2 * (g // 2) + 2)
                fill_group(0, g)
            shift_rows(0, 0)

            def tail(b):
                sp.wait_ge(S["stored"], at("stored", b, 16))

            batches(sp, step, tail)

        def newton(pool, which, name, b):
            t = ln[which]
            s, done = S[name], 0

            def after(ins):
                nonlocal done
                done += 1
                ins.then_inc(s, 1)
                pool.wait_ge(s, at(name, b, done))

            for _ in range(NEWTON_STEPS):
                after(pool.tensor_tensor(t["t"][:, :], t["y"][:, :], t["y"][:, :], ALU.mult))
                after(pool.tensor_tensor(t["t"][:, :], t["t"][:, :], t["nhalf"][:, :], ALU.mult))
                after(pool.tensor_tensor(t["t"][:, :], t["t"][:, :], three_halves[:, :], ALU.add))
                after(pool.tensor_tensor(t["y"][:, :], t["y"][:, :], t["t"][:, :], ALU.mult))

        NEWTON = 4 * NEWTON_STEPS
        STATS = TT + 8
        LN_OF = {"next": ("next", x_in, x_in), "a": ("last", y0, zn), "b": ("last", x_res, zn),
                 "c": ("last", yk, zn)}

        @block.gpsimd
        def _(pool):
            pool.memset(ident[:, :], 0.0).then_inc(const_set, 1)
            pool.memset(blocks[:, :], 1.0).then_inc(const_set, 1)
            pool.memset(one1[:, :], 1.0).then_inc(const_set, 1)
            pool.wait_ge(const_set, 3)
            pool.affine_select(out=ident[:, :], in_=ident[:, :], compare_op=ALU.not_equal, fill=1.0,
                               base=0, pattern=[[-1, P]], channel_multiplier=1).then_inc(const_set, 1)
            bview = blocks[:, :].rearrange("p (n e) -> p n e", e=DH)
            pool.affine_select(out=bview, in_=bview, compare_op=ALU.is_ge, fill=0.0,
                               base=0, pattern=[[-DH, P // DH], [0, DH]], channel_multiplier=1).then_inc(const_set, 1)
            pool.wait_ge(const_set, 5)
            pool.affine_select(out=bview, in_=bview, compare_op=ALU.is_ge, fill=0.0,
                               base=DH - 1, pattern=[[DH, P // DH], [0, DH]], channel_multiplier=-1).then_inc(const_set, 1)
            pool.memset(v_aug[:, :, :, DH:DH + 1], 1.0).then_inc(const_set, 1)

            def piece(name, n, b):
                if name.startswith("ln_"):
                    which = name[3:]
                    pool.wait_ge(S[f"bn_{which}"], at(f"bn_{which}", b, STATS))
                    newton(pool, LN_OF[which][0], f"newton_{which}", b)
                    if which == "a":
                        pool.wait_ge(S["res_in"], at("res_in", b, 16))
                        if isinstance(b, int) and b == 0:
                            pool.wait_ge(outb_in, 32)
                        pool.tensor_tensor(x_res[:, :, :], x_res[:, :, :],
                                           outb[:, 0:1, :].broadcast_to([P, TT, D]), ALU.add)\
                            .then_inc(S["res_b"], 1)
                if name == "z_b":
                    pool.wait_ge(S["z_b"], at("z_b", b, 4))
                    pool.tensor_tensor(x_res[:, :, :], x_res[:, :, :],
                                       outb[:, 1:2, :].broadcast_to([P, TT, D]), ALU.add)\
                        .then_inc(S["res_c"], 1)
                if name in ("film_a", "film_c"):
                    f = "f" + name[-1]
                    pool.wait_ge(S[f + "_hi"], at(f + "_hi", b, n + 1))
                    pool.tensor_tensor(at_lo[:, n, :], film_h[:, n, :], at_hi[:, n, :].bitcast(F32),
                                       ALU.subtract).then_inc(S[f + "_lo"], 1)

            def step(b, k, first, last):
                for place in range(4):
                    for name, n, bb in pieces(k, place, b, first, last):
                        piece(name, n, bb)

            def tail(b):
                for name, n in LAST_ONLY:
                    piece(name, n, b)

            pool.wait_ge(ones_set, 2)
            piece("ln_next", 0, 0)
            batches(pool, step, tail)

        @block.scalar
        def _(act):
            act.dma_start(x_in[:, :, :], tiles(x[0])).then_inc(S["x_in"], 16)
            act.dma_start(mrow[:, :], mask_BxS_ff1[0:1, :]).then_inc(S["mrow_in"], 16)
            act.wait_ge(cols_set, 1)
            act.activation(cond_t[:, :], cols[:, CD:CD + B * EC], ACT.Tanh, scale=0.5).then_inc(cond_set, 1)

            def weight_hi(w):
                for c in range(KC):
                    src = wperm[:, w, c, :] if w in (Q0, K0) else wraw[:, w, c, :]
                    if w in (O0, O1):
                        act.activation(wh[:, w, c, :], src, ACT.Copy).then_inc(w_hi_set, 1)
                    else:
                        act.activation(wh[:, w, c, :], src, ACT.Copy, scale=scale_col(w, c)).then_inc(w_hi_set, 1)

            act.wait_ge(perm_set, 2)
            weight_hi(Q0)
            weight_hi(K0)

            def piece(name, n, b):
                if name == "zt":
                    if n == 0 and not (isinstance(b, int) and b == 0):
                        act.wait_ge(S["v_mm"], at("v_mm", b - 1, 2))
                    act.wait_ge(S["zt_mm"], at("zt_mm", b, n + 1))
                    act.activation(zt_hi[:, n, :], w_ps[:, :], ACT.Copy).then_inc(S["zt_hi"], 1)
                elif name == "qk":
                    mc, i = n // 2, n % 2
                    if i == 0 and not (isinstance(b, int) and b == 0):
                        act.wait_ge(fill[2 * mc], 160 * b)
                        act.wait_ge(fill[2 * mc + 1], 160 * b)
                    act.wait_ge(S["qk_mm"], at("qk_mm", b, n + 1))
                    act.activation(qk_hi[:, i, mc, :], w_ps[:, :], ACT.Identity,
                                   bias=bias_cols[:, 2 * i + mc:2 * i + mc + 1]).then_inc(S["qk_hi"], 1)
                elif name == "v":
                    act.wait_ge(S["v_mm"], at("v_mm", b, n + 1))
                    if n == 0:
                        act.wait_ge(S["mcol"], at("mcol", b, 1))
                        if not (isinstance(b, int) and b == 0):
                            act.wait_ge(S["pv"], at("pv", b - 1, H))
                    for t in (2 * n, 2 * n + 1):
                        act.activation(v_aug[:, t, :, 0:DH],
                                       w_ps[:, D * (t % 2):D * (t % 2) + D].rearrange("p (h d) -> p h d", h=H),
                                       ACT.Copy, scale=mcol_now[:, t:t + 1]).then_inc(S["v_set"], 1)
                elif name in ("film_a", "film_c"):
                    f, layer = "f" + name[-1], 0 if name == "film_a" else 1
                    act.wait_ge(S[f + "_mm"], at(f + "_mm", b, n + 1))
                    if n == 0 and layer == 0:
                        act.wait_ge(S["film_now"], at("film_now", b, 2))
                    if n == 1:
                        act.wait_ge(S[f + "_h"], at(f + "_h", b, 1))
                    for which, func, dst in (("_u", ACT.Identity, film_u[:, :]), ("_t", ACT.Tanh, film_h[:, n, :])):
                        act.activation(dst, w_ps[:, :], func, scale=film_now[:, layer, 0, n:n + 1],
                                       bias=film_now[:, layer, 1, n:n + 1]).then_inc(S[f + which], 1)
                    act.wait_ge(S[f + "_h"], at(f + "_h", b, n + 1))
                    act.activation(at_hi[:, n, :], film_h[:, n, :], ACT.Copy).then_inc(S[f + "_hi"], 1)
                elif name == "z1t":
                    act.wait_ge(S["z1_mm"], at("z1_mm", b, n + 1))
                    act.activation(at_hi[:, n, :], w_ps[:, :], ACT.Copy).then_inc(S["z1_hi"], 1)
                elif name == "k1":
                    act.wait_ge(S["k1_max"], at("k1_max", b, n + 1))
                    act.activation(k1[:, n, :], k1[:, n, :], ACT.Exp, bias=k1max[:, n:n + 1],
                                   accum_out=k1sum[:, n:n + 1]).then_inc(S["k1_exp"], 1)
                elif name == "qv":
                    act.wait_ge(S["qv_mm"], at("qv_mm", b, n + 1))
                    if n == 0:
                        act.wait_ge(S["own"], at("own", b, 1))
                    act.activation(v1[:, n, :], w_ps[:, D:2 * D], ACT.Copy, scale=own_now[:, n:n + 1])\
                        .then_inc(S["v1_set"], 1)
                elif name == "softmax_q":
                    act.wait_ge(S["q1_sub"], at("q1_sub", b, 4))
                    act.activation(q1[:, :, :], q1[:, :, :], ACT.Exp).then_inc(S["q1_exp"], 1)
                elif name == "k1t":
                    act.wait_ge(S["kt_mm"], at("kt_mm", b, n + 1))
                    act.activation(yk[:, :, P * n:P * n + P], w_ps[:, :].rearrange("p (t f) -> p t f", t=TT),
                                   ACT.Copy).then_inc(S["kt_set"], 1)
                elif name == "q1t":
                    act.wait_ge(S["qt_mm"], at("qt_mm", b, n + 1))
                    act.activation(q1t[:, n, :], w_ps[:, :], ACT.Copy).then_inc(S["qt_set"], 1)

            def load_batch(b):
                if not isinstance(b, int) or b > 0:
                    act.wait_ge(S["zt_mm"], at("zt_mm", b - 1, 2))
                act.dma_start(x_in[:, :, :], tiles(x[b])).then_inc(S["x_in"], 16)

            def load_mask(b):
                if not isinstance(b, int) or b > 0:
                    act.wait_ge(fill[G - 1], 160 * b)
                act.dma_start(mrow[:, :], mask_BxS_ff1[bass.ds(b, 1), :]).then_inc(S["mrow_in"], 16)

            def load_last(b):
                act.dma_start(x_res[:, :, :], tiles(x[b])).then_inc(S["res_in"], 16)
                act.dma_start(hide[:, :].bitcast(I32), mask_BxS_ik0[bass.ds(b, 1), :].broadcast_to([P, T])).then_inc(S["hide_in"], 16)

            def store(b):
                act.wait_ge(S["oc_set"], at("oc_set", b, 2))
                act.dma_start(tiles(out[b]), x_res[:, :, :]).then_inc(S["stored"], 16)

            def exps(b, k):
                for half in range(2):
                    act.wait_ge(S["s_mm"], at("s_mm", b, 2 * k + half + 1))
                    if half == 0 and not (isinstance(b, int) and 16 * b + k < 2):
                        act.wait_ge(S["pv"], at("pv", b, k - 1))
                    act.activation(probs[:, k % 2, 2 * half:2 * half + 2, :],
                                   s_ps[half][:, :].rearrange("p (c q) -> p c q", c=2),
                                   ACT.Exp).then_inc(S["exp"], 1)

            def step(b, k, first, last):
                if k == 0:
                    if not last:
                        load_batch(b + 1)
                    if not first:
                        load_last(b - 1)
                if k == 2 and not last:
                    load_mask(b + 1)
                for place in range(4):
                    for name, n, bb in pieces(k, place, b, first, last):
                        piece(name, n, bb)
                if k == H - 1 and not first:
                    store(b - 1)
                exps(b, k)
                if k == H - 1 and not first:
                    act.wait_ge(S["stored"], at("stored", b - 1, 16))

            def tail(b):
                load_last(b)
                for name, n in LAST_ONLY:
                    piece(name, n, b)
                store(b)

            piece("zt", 0, 0)
            piece("zt", 1, 0)
            act.wait_ge(bias_set, 1)
            for n in range(4):
                piece("qk", n, 0)
            act.wait_ge(w_in[1], 32)
            act.wait_ge(w_in[2], 32)
            act.wait_ge(w_in[3], 32)
            for w in (V0, K1, Q1, V1, O0, O1):
                weight_hi(w)
            batches(act, step, tail)

        @block.vector
        def _(dve):
            nm = nc.vector

            def statistics(which, b, wait):
                scratch, src, _ = LN_OF[which]
                t = ln[scratch]
                s, name, done = S[f"bn_{which}"], f"bn_{which}", 0

                def then(ins):
                    nonlocal done
                    done += 1
                    ins.then_inc(s, 1)

                def settled():
                    dve.wait_ge(s, at(name, b, done))

                wait()
                for i in range(TT):
                    then(dve.bn_stats(t["stats"][:, i, :], src[:, i, :]))
                settled()
                even, odd = t["stats"][:, :, 1:3], t["stats"][:, :, 4:6]
                then(dve.tensor_tensor(t["sum"][:, :, :], even, odd, ALU.add))
                then(dve.tensor_tensor(t["diff"][:, :], even[:, :, 0], odd[:, :, 0], ALU.subtract))
                settled()
                then(dve.tensor_scalar(t["mean"][:, :], t["sum"][:, :, 0], 0.5, None, ALU.mult))
                then(dve.tensor_scalar(t["var"][:, :], t["sum"][:, :, 1], 1.0 / D, LN_EPS, ALU.mult, ALU.add))
                then(dve.scalar_tensor_tensor(t["diff"][:, :], t["diff"][:, :], 0.25, t["diff"][:, :],
                                              ALU.mult, ALU.mult))
                settled()
                then(dve.tensor_tensor(t["var"][:, :], t["var"][:, :], t["diff"][:, :], ALU.add))
                settled()
                then(dve.tensor_scalar(t["nhalf"][:, :], t["var"][:, :], -0.5, None, ALU.mult))
                then(dve.tensor_scalar(t["y"][:, :].bitcast(I32), t["var"][:, :].bitcast(I32), -0.5,
                                       RSQRT_GUESS, ALU.mult, ALU.add))

            def normalise(which, b):
                scratch, src, dst = LN_OF[which]
                t = ln[scratch]
                dve.wait_ge(S[f"newton_{which}"], at(f"newton_{which}", b, NEWTON))
                for i in range(TT):
                    dve.tensor_scalar(dst[:, i, :], src[:, i, :], t["mean"][:, i:i + 1], t["y"][:, i:i + 1],
                                      ALU.subtract, ALU.mult).then_inc(S[f"z_{which}"], 1)

            dve.memset(three_halves[:, :], 1.5).then_inc(ones_set, 1)
            dve.memset(ones_row[:, :].bitcast(F32), 1.0).then_inc(ones_set, 1)
            dve.wait_ge(vec_in, 16 * 13)
            dve.tensor_scalar(hrows[:, :], hrows_i[:, :], 1.0, None, ALU.is_equal).then_inc(hid_rows, 1)
            dve.wait_ge(cols_mm, 2)
            dve.tensor_copy(cols[:, :], w_ps[:, 0:56]).then_inc(cols_set, 1)
            dve.tensor_scalar(own_key[:, :], w_ps[:, 56:56 + B * TT], -1.0, 1.0, ALU.mult, ALU.add)\
               .then_inc(cols_set, 1)
            statistics("next", 0, lambda: dve.wait_ge(S["x_in"], 16))
            dve.wait_ge(w_in[0], 32)
            dve.tensor_copy(wperm[:, Q0, :, :].rearrange("p c (g d h) -> p (c g) d h", g=G, d=DH),
                            wraw[:, Q0, :, :].rearrange("p c (g h d) -> p (c g) d h", g=G, h=HG)).then_inc(perm_set, 1)
            dve.tensor_copy(wperm[:, K0, :, :].rearrange("p c (g d h) -> p (c g) d h", g=G, d=DH),
                            wraw[:, K0, :, :].rearrange("p c (g h d) -> p (c g) d h", g=G, h=HG)).then_inc(perm_set, 1)
            dve.wait_ge(bias_in, 16 * 6)
            for i in range(2):
                dve.tensor_copy(bperm[:, i, :].rearrange("p (g d h) -> p g d h", g=G, d=DH),
                                regroup(brow[:, i, :])).then_inc(perm_set, 1)
            normalise("next", 0)

            def weight_lo(w):
                for c in range(KC):
                    src = wperm[:, w, c, :] if w in (Q0, K0) else wraw[:, w, c, :]
                    if w in (O0, O1):
                        dve.tensor_tensor(wl[:, w, c, :], src, wh[:, w, c, :].bitcast(F32), ALU.subtract)\
                           .then_inc(w_lo_set, 1)
                    else:
                        dve.scalar_tensor_tensor(wl[:, w, c, :], src, scale_col(w, c),
                                                 wh[:, w, c, :].bitcast(F32), ALU.mult, ALU.subtract)\
                           .then_inc(w_lo_set, 1)

            dve.wait_ge(cols_set, 1)
            for w in (Q0, K0):
                dve.wait_ge(w_hi_set, 2 * w + 2)
                weight_lo(w)

            def piece(name, n, b):
                if name.startswith("ln_"):
                    which = name[3:]
                    ready = {"next": lambda: dve.wait_ge(S["x_in"], at("x_in", b, 16)),
                             "a": lambda: dve.wait_ge(S["y_set"], at("y_set", b, G)),
                             "b": lambda: dve.wait_ge(S["oa_set"], at("oa_set", b, 2)),
                             "c": lambda: dve.wait_ge(S["y1_set"], at("y1_set", b, 4))}[which]
                    statistics(which, b, ready)
                elif name in ("z_a", "z_b", "z_c", "z_next"):
                    normalise(name[2:], b)
                    if name == "z_a":
                        dve.tensor_copy(film_now[:, :, 0, :].unsqueeze(3), film_s[:, :, :, bass.ds(b, 1)]).then_inc(S["film_now"], 1)
                        dve.tensor_copy(film_now[:, :, 1, :].unsqueeze(3), film_t[:, :, :, bass.ds(b, 1)]).then_inc(S["film_now"], 1)
                        dve.tensor_copy(own_now[:, :], own_key[:, bass.ds(b * TT, TT)]).then_inc(S["own"], 1)
                        dve.wait_ge(S["hide_in"], at("hide_in", b, 16))
                        dve.tensor_scalar(hide[:, :], hide[:, :].bitcast(I32), 1.0, HIDDEN_KEY, ALU.is_equal, ALU.mult)\
                           .then_inc(S["hide_set"], 1)
                elif name == "zt":
                    dve.wait_ge(S["zt_hi"], at("zt_hi", b, n + 1))
                    dve.tensor_tensor(zt_lo[:, n, :], w_ps[:, :], zt_hi[:, n, :].bitcast(F32), ALU.subtract)\
                       .then_inc(S["zt_lo"], 1)
                elif name == "qk":
                    mc, i = n // 2, n % 2
                    dve.wait_ge(S["qk_hi"], at("qk_hi", b, n + 1))
                    dve.scalar_tensor_tensor(qk_lo[:, i, mc, :], w_ps[:, :],
                                             bias_cols[:, 2 * i + mc:2 * i + mc + 1],
                                             qk_hi[:, i, mc, :].bitcast(F32), ALU.add, ALU.subtract)\
                       .then_inc(S["qk_lo"], 1)
                elif name == "c":
                    dve.wait_ge(S["c_mm"], at("c_mm", b, n + 1))
                    if not (isinstance(b, int) and b == 0 and n == 0):
                        prev = 2 * b + (n - 1) // 2 + 1
                        dve.wait_ge(c_in[(n - 1) % 2], 32 * prev)
                    dve.tensor_copy(crow_hi[:, :], w_ps[0:HG * TT, 0:P]).then_inc(S["c_hi"], 1)
                    dve.wait_ge(S["c_hi"], at("c_hi", b, n + 1))
                    dve.tensor_tensor(crow_lo[:, :], w_ps[0:HG * TT, 0:P], crow_hi[:, :].bitcast(F32),
                                      ALU.subtract).then_inc(S["c_lo"], 1)
                elif name in ("film_a", "film_c"):
                    f = "f" + name[-1]
                    dve.wait_ge(S[f + "_t"], at(f + "_t", b, n + 1))
                    dve.scalar_tensor_tensor(film_h[:, n, :], film_h[:, n, :], 1.0, film_u[:, :],
                                             ALU.add, ALU.mult).then_inc(S[f + "_h"], 1)
                elif name == "out_a":
                    dve.wait_ge(S["oa_mm"], at("oa_mm", b, n + 1))
                    dve.wait_ge(S["res_b"], at("res_b", b, 1))
                    xr = x_res[:, 2 * n:2 * n + 2, :].rearrange("p t d -> p (t d)")
                    dve.tensor_tensor(xr, w_ps[:, :], xr, ALU.add).then_inc(S["oa_set"], 1)
                elif name == "z1t":
                    dve.wait_ge(S["z1_hi"], at("z1_hi", b, n + 1))
                    dve.tensor_tensor(at_lo[:, n, :], w_ps[:, :], at_hi[:, n, :].bitcast(F32), ALU.subtract)\
                       .then_inc(S["z1_lo"], 1)
                elif name == "k1":
                    dve.wait_ge(S["k1_mm"], at("k1_mm", b, n + 1))
                    dve.wait_ge(S["hide_set"], at("hide_set", b, 1))
                    dve.scalar_tensor_tensor(k1[:, n, :], w_ps[:, :], bias_cols[:, 4 + n:5 + n], hide[:, :],
                                             ALU.add, ALU.add).then_inc(S["k1_b"], 1)
                    dve.wait_ge(S["k1_b"], at("k1_b", b, n + 1))
                    dve.tensor_reduce(k1max[:, n:n + 1], k1[:, n, :], AX.X, ALU.max, negate=True)\
                       .then_inc(S["k1_max"], 1)
                elif name == "qv":
                    dve.wait_ge(S["v1_set"], at("v1_set", b, n + 1))
                    qv = w_ps[:, 0:D].rearrange("p (h d) -> p h d", h=H)
                    dve.tensor_reduce(q1max[:, n, :], qv, AX.X, ALU.max).then_inc(S["q1_max"], 1)
                    dve.wait_ge(S["q1_max"], at("q1_max", b, n + 1))
                    dve.tensor_tensor(q1[:, n, :].rearrange("p (h d) -> p h d", h=H), qv,
                                      q1max[:, n, :].unsqueeze(2).broadcast_to([P, H, DH]), ALU.subtract)\
                       .then_inc(S["q1_sub"], 1)
                elif name == "softmax_q":
                    for c in range(KC):
                        dve.wait_ge(S["k1_exp"], at("k1_exp", b, c + 1))
                        dve.reciprocal(k1rec[:, c:c + 1], k1sum[:, c:c + 1]).then_inc(S["k1_rec"], 1)
                        dve.wait_ge(S["k1_rec"], at("k1_rec", b, c + 1))
                        dve.tensor_scalar(k1[:, c, :], k1[:, c, :], k1rec[:, c:c + 1], None, ALU.mult)\
                           .then_inc(S["k1_n"], 1)
                    dve.wait_ge(S["q1_exp"], at("q1_exp", b, 1))
                    dve.tensor_reduce(q1sum[:, :], q1[:, :, :].rearrange("p t (h d) -> p (t h) d", h=H),
                                      AX.X, ALU.add).then_inc(S["q1_sum"], 1)
                    dve.wait_ge(S["q1_sum"], at("q1_sum", b, 1))
                    dve.reciprocal(q1rec[:, :], q1sum[:, :]).then_inc(S["q1_rec"], 1)
                elif name == "attn":
                    dve.wait_ge(S["at_mm"], at("at_mm", b, 1))
                    dve.tensor_tensor(attn[:, :, :], w_ps[:, 0:KC * P].rearrange("p (c e) -> p c e", c=KC),
                                      blocks[:, :].unsqueeze(1).broadcast_to([P, KC, P]), ALU.mult)\
                       .then_inc(S["at_set"], 1)
                elif name == "y1":
                    dve.wait_ge(S["y1_mm"], at("y1_mm", b, n + 1))
                    dve.wait_ge(S["q1_rec"], at("q1_rec", b, 1))
                    for t in (2 * n, 2 * n + 1):
                        dve.tensor_tensor(yk[:, t, :].rearrange("p (h d) -> p h d", h=H),
                                          w_ps[:, D * (t % 2):D * (t % 2) + D].rearrange("p (h d) -> p h d", h=H),
                                          q1rec[:, H * t:H * t + H].unsqueeze(2).broadcast_to([P, H, DH]),
                                          ALU.mult).then_inc(S["y1_set"], 1)
                elif name == "out_c":
                    dve.wait_ge(S["oc_mm"], at("oc_mm", b, n + 1))
                    dve.wait_ge(S["res_c"], at("res_c", b, 1))
                    xr = x_res[:, 2 * n:2 * n + 2, :].rearrange("p t d -> p (t d)")
                    dve.tensor_tensor(xr, w_ps[:, :], xr, ALU.add).then_inc(S["oc_set"], 1)

            def mask_row(b):
                dve.wait_ge(S["mrow_in"], at("mrow_in", b, 16))
                dve.tensor_scalar(mrow[:, :], mrow[:, :], -1.0, MASK_PENALTY, ALU.add, ALU.mult)\
                   .then_inc(S["mrow_shift"], 1)
                dve.wait_ge(S["mrow_shift"], at("mrow_shift", b, 1))
                dve.tensor_copy(mrow_hi[:, :], mrow[:, :]).then_inc(S["mrow_hi"], 1)
                dve.wait_ge(S["mrow_hi"], at("mrow_hi", b, 1))
                dve.tensor_tensor(mrow_lo[:, :], mrow[:, :], mrow_hi[:, :].bitcast(F32), ALU.subtract)\
                   .then_inc(S["mrow_lo"], 1)

            def mask_cols(b):
                dve.wait_ge(cols_set, 2)
                if not (isinstance(b, int) and b == 0):
                    dve.wait_ge(S["v_set"], at("v_set", b - 1, 4))
                dve.tensor_copy(mcol_now[:, :], cols[:, bass.ds(b * TT + MC, TT)]).then_inc(S["mcol"], 1)

            def maxima(b, h, part):
                g, j = h // HG, h % HG
                if j == 0 and part == 0 and not (isinstance(b, int) and HG * b + g < 2):
                    dve.wait_ge(S["c_mm"], at("c_mm", b, g - 1))
                for t in (2 * part, 2 * part + 1):
                    dve.wait_ge(S["m_mm"], at("m_mm", b, TT * h + t + 1))
                    dve.tensor_reduce(negmax[:, g % 2, TT * j + t:TT * j + t + 1], m_ps[t % 2][:, :], AX.X,
                                      ALU.max, negate=True).then_inc(S["m_red"], 1)

            def outputs(b, g):
                dve.wait_ge(S["pv"], at("pv", b, HG * g + HG))
                dve.reciprocal(recip[:, :].rearrange("p (h t) -> p h t", h=HG), y_v[:, :, :, DH])\
                   .then_inc(S["y_rec"], 1)
                dve.wait_ge(S["y_rec"], at("y_rec", b, g + 1))
                rc = recip[:, :].rearrange("p (h t) -> p t h", h=HG)
                for t in range(TT):
                    ins = dve.tensor_tensor(yout(g)[:, t, :, :], y_v[:, :, t, 0:DH],
                                            rc[:, t, :].unsqueeze(2).broadcast_to([P, HG, DH]), ALU.mult)
                ins.then_inc(S["y_set"], 1)

            def yout(g):
                return y0[:, :, HG * DH * g:HG * DH * g + HG * DH].rearrange("p t (h d) -> p t h d", h=HG)

            def step(b, k, first, last):
                i = (k + LEAD) % H
                nb = b + (k + LEAD) // H
                for place in range(4):
                    for name, n, bb in pieces(k, place, b, first, last):
                        piece(name, n, bb)
                    if place < 2 and not (last and k + LEAD >= H):
                        maxima(nb, i, place)
                    if place == 3 and k % HG == 0:
                        if k > 0:
                            outputs(b, k // HG - 1)
                        elif not first:
                            outputs(b - 1, G - 1)

            def full_step(b, k, first, last):
                if k == 0:
                    mask_cols(b)
                step(b, k, first, last)
                if k == 3 and not last:
                    mask_row(b + 1)

            def tail(b):
                outputs(b, G - 1)
                for name, n in LAST_ONLY:
                    piece(name, n, b)

            mask_row(0)
            piece("zt", 0, 0)
            piece("zt", 1, 0)
            dve.wait_ge(bias_mm, 6)
            dve.tensor_copy(bias_cols[:, :], m_ps[0][:, 0:6]).then_inc(bias_set, 1)
            for n in range(4):
                piece("qk", n, 0)
                if n == 0:
                    dve.wait_ge(w_lo_set, 4)
            for w, (ps, off, wd) in enumerate(((m_ps[1], 0, D), (s_ps[0], 0, D), (s_ps[0], 512, D))):
                dve.wait_ge(bias_mm, 7 + w)
                dve.tensor_tensor(brow[:, (2, 4, 5)[w], :], ps[0:1, off:off + wd], brow[:, (2, 4, 5)[w], :], ALU.add)\
                   .then_inc(bias_set, 1)
                dve.wait_ge(bias_set, 2 + 3 * w)
                dve.tensor_copy(bias_hi[:, D * w:D * w + D], brow[:, (2, 4, 5)[w], :]).then_inc(bias_set, 1)
                dve.wait_ge(bias_set, 3 + 3 * w)
                dve.tensor_tensor(bias_lo[:, D * w:D * w + D], brow[:, (2, 4, 5)[w], :],
                                  bias_hi[:, D * w:D * w + D].bitcast(F32), ALU.subtract).then_inc(bias_set, 1)
            dve.wait_ge(cond_set, 1)
            dve.tensor_scalar(cond_h[:, :], cols[:, CD:CD + B * EC], 0.5, None, ALU.mult).then_inc(cond_set, 1)
            dve.wait_ge(cond_set, 2)
            dve.scalar_tensor_tensor(cond_s[:, :], cond_t[:, :], 1.0, cond_h[:, :], ALU.add, ALU.mult)\
               .then_inc(cond_set, 1)
            dve.wait_ge(film_mm, 1)
            dve.tensor_tensor(emb_e[:, :, :, :, :].rearrange("p l w c b -> p (l w c) b"),
                              s_ps[1][:, 0:32].rearrange("p (f b) -> p f b", b=B),
                              cols[:, EB:EB + 2 * EC].unsqueeze(2).broadcast_to([P, 2 * EC, B]),
                              ALU.add).then_inc(film_set, 1)
            dve.wait_ge(film_set, 1)
            for l in range(2):
                dve.tensor_scalar(emb_p[:, l, :, :], emb_e[:, l, 0, :, :], 1.0, 0.5, ALU.add, ALU.mult)\
                   .then_inc(film_set, 1)
                dve.wait_ge(film_set, 2 + 4 * l)
                dve.tensor_tensor(film_s[:, l, :, :], emb_p[:, l, :, :],
                                  fcols[:, l, 0, :].unsqueeze(2).broadcast_to([P, KC, B]), ALU.mult)\
                   .then_inc(film_set, 1)
                dve.tensor_tensor(emb_q[:, l, :, :], emb_p[:, l, :, :],
                                  fcols[:, l, 1, :].unsqueeze(2).broadcast_to([P, KC, B]), ALU.mult)\
                   .then_inc(film_set, 1)
                dve.wait_ge(film_set, 4 + 4 * l)
                dve.scalar_tensor_tensor(film_t[:, l, :, :], emb_e[:, l, 1, :, :], 0.5, emb_q[:, l, :, :],
                                         ALU.mult, ALU.add).then_inc(film_set, 1)
            for w in (V0, K1, Q1, V1, O0, O1):
                dve.wait_ge(w_hi_set, 2 * w + 2)
                weight_lo(w)
            dve.wait_ge(w_lo_set, 16)
            dve.wait_ge(film_set, 9)
            dve.memset(qs[ROW_MASK:ROW_MAX, :, :].bitcast(F32), 1.0).then_inc(stack_set, 1)
            dve.memset(ks[ROW_MASK:ROW_MAX, :, :].bitcast(F32), 0.0).then_inc(stack_set, 1)
            dve.memset(ks[ROW_MAX:ROWS_SHIFTED, :, :].bitcast(F32), 1.0).then_inc(stack_set, 1)
            for h in range(LEAD):
                for part in range(2):
                    maxima(0, h, part)
                if h == HG:
                    piece("c", 0, 0)
            batches(dve, full_step, tail)

        @block.tensor
        def _(pe):
            free = [None]

            def take():
                if free[0] is not None:
                    for s, v in free[0]:
                        pe.wait_ge(s, v)

            def give(*readers):
                free[0] = [(S[name], at(name, b, n)) for name, b, n in readers]

            def split_product(dst, lhs, rhs, extra=None, stop_all=True):
                terms = [(a, c, b2) for c in range(KC) for a, b2 in ((0, 0), (0, 1), (1, 0))]
                for i, (a, c, b2) in enumerate(terms):
                    ins = pe.matmul(dst, lhs[a](c), rhs[b2](c), start=(i == 0),
                                    stop=(i == len(terms) - 1 and extra is None))
                if extra is not None:
                    for i, row in enumerate((bias_hi, bias_lo)):
                        ins = pe.matmul(dst, ones_row[:, :], row[:, extra], start=False, stop=(i == 1))
                return ins

            def weights(w, cols_of=slice(0, D)):
                return [lambda c: wh[:, w, c, cols_of], lambda c: wl[:, w, c, cols_of]]

            def tokens(hi, lo, t=None):
                s = slice(0, T) if t is None else slice(P * t, P * t + P)
                return [lambda c: hi[:, c, s], lambda c: lo[:, c, s]]

            def turn(src, c, blocks_of):
                for t in range(TT):
                    ins = pe.transpose(w_ps[:, P * t:P * t + P], blocks_of(src, t, c), ident[:, :])
                return ins

            token_block = lambda src, t, c: src[:, t, P * c:P * c + P]
            feature_block = lambda src, t, c: src[:, c, P * t:P * t + P]

            def piece(name, n, b):
                if name in ("ln_a", "ln_b", "ln_c", "ln_next", "z_a", "z_b", "z_c", "z_next", "softmax_q"):
                    return
                take()
                if name == "zt":
                    if n == 0:
                        pe.wait_ge(S["z_next"], at("z_next", b, 4))
                    turn(x_in, n, token_block).then_inc(S["zt_mm"], 1)
                    give(("zt_lo", b, n + 1))
                elif name == "qk":
                    mc, i = n // 2, n % 2
                    if n == 0:
                        pe.wait_ge(S["zt_hi"], at("zt_hi", b, 2))
                        pe.wait_ge(S["zt_lo"], at("zt_lo", b, 2))
                    split_product(w_ps[:, :], weights((Q0, K0)[i], slice(P * mc, P * mc + P)),
                                  tokens(zt_hi, zt_lo)).then_inc(S["qk_mm"], 1)
                    give(("qk_lo", b, n + 1))
                elif name == "v":
                    for t in (2 * n, 2 * n + 1):
                        ins = split_product(w_ps[:, D * (t % 2):D * (t % 2) + D], tokens(zt_hi, zt_lo, t),
                                            weights(V0), extra=slice(0, D))
                    ins.then_inc(S["v_mm"], 1)
                    give(("v_set", b, 2 * n + 2))
                elif name == "c":
                    pe.wait_ge(S["m_red"], at("m_red", b, 16 * n + 16))
                    pe.transpose(w_ps[0:HG * TT, 0:P], negmax[:, n % 2, :], ident[:, :]).then_inc(S["c_mm"], 1)
                    give(("c_lo", b, n + 1))
                elif name in ("film_a", "film_c"):
                    f = "f" + name[-1]
                    if n == 0:
                        z = "z_" + name[-1]
                        pe.wait_ge(S[z], at(z, b, 4))
                    turn(zn, n, token_block).then_inc(S[f + "_mm"], 1)
                    give((f + "_t", b, n + 1))
                elif name in ("out_a", "out_c"):
                    f, o, w = "f" + name[-1], "o" + name[-1], O0 if name == "out_a" else O1
                    if n == 0:
                        pe.wait_ge(S[f + "_hi"], at(f + "_hi", b, 2))
                        pe.wait_ge(S[f + "_lo"], at(f + "_lo", b, 2))
                    for t in (2 * n, 2 * n + 1):
                        ins = split_product(w_ps[:, D * (t % 2):D * (t % 2) + D], tokens(at_hi, at_lo, t),
                                            weights(w))
                    ins.then_inc(S[o + "_mm"], 1)
                    give((o + "_set", b, n + 1))
                elif name == "z1t":
                    if n == 0:
                        pe.wait_ge(S["z_b"], at("z_b", b, 4))
                    turn(zn, n, token_block).then_inc(S["z1_mm"], 1)
                    give(("z1_lo", b, n + 1))
                elif name == "k1":
                    if n == 0:
                        pe.wait_ge(S["z1_hi"], at("z1_hi", b, 2))
                        pe.wait_ge(S["z1_lo"], at("z1_lo", b, 2))
                    split_product(w_ps[:, :], weights(K1, slice(P * n, P * n + P)),
                                  tokens(at_hi, at_lo)).then_inc(S["k1_mm"], 1)
                    give(("k1_b", b, n + 1))
                elif name == "qv":
                    both = [lambda c: wh[:, Q1:V1 + 1, c, :], lambda c: wl[:, Q1:V1 + 1, c, :]]
                    split_product(w_ps[:, :], tokens(at_hi, at_lo, n),
                                  both, extra=slice(D, 3 * D)).then_inc(S["qv_mm"], 1)
                    give(("q1_sub", b, n + 1))
                elif name == "k1t":
                    pe.wait_ge(S["k1_n"], at("k1_n", b, n + 1))
                    turn(k1, n, feature_block).then_inc(S["kt_mm"], 1)
                    give(("kt_set", b, n + 1))
                elif name == "q1t":
                    pe.wait_ge(S["q1_exp"], at("q1_exp", b, 1))
                    turn(q1, n, token_block).then_inc(S["qt_mm"], 1)
                    give(("qt_set", b, n + 1))
                elif name == "attn":
                    pe.wait_ge(S["kt_set"], at("kt_set", b, 2))
                    pe.wait_ge(S["v1_set"], at("v1_set", b, 4))
                    for c in range(KC):
                        for t in range(TT):
                            ins = pe.matmul(w_ps[:, P * c:P * c + P], v1[:, t, P * c:P * c + P],
                                            yk[:, t, P * c:P * c + P], start=(t == 0), stop=(t == TT - 1))
                    ins.then_inc(S["at_mm"], 1)
                    give(("at_set", b, 1))
                elif name == "y1":
                    if n == 0:
                        pe.wait_ge(S["at_set"], at("at_set", b, 1))
                        pe.wait_ge(S["qt_set"], at("qt_set", b, 2))
                    for t in (2 * n, 2 * n + 1):
                        for c in range(KC):
                            o = D * (t % 2) + P * c
                            ins = pe.matmul(w_ps[:, o:o + P], q1t[:, c, P * t:P * t + P], attn[:, c, :],
                                            start=True, stop=True)
                    ins.then_inc(S["y1_mm"], 1)
                    give(("y1_set", b, 2 * n + 2))

            def maxima(b, h, part):
                if part == 0 and h % HG == 0:
                    pe.wait_ge(fill[h // HG], 160 * (b + 1))
                for t in (2 * part, 2 * part + 1):
                    if not (isinstance(b, int) and 64 * b + TT * h + t < 2):
                        pe.wait_ge(S["m_red"], at("m_red", b, TT * h + t - 1))
                    pe.matmul(m_ps[t % 2][:, :], qs[0:ROWS_SCORE, h, P * t:P * t + P],
                              ks[0:ROWS_SCORE, h, :], start=True, stop=True).then_inc(S["m_mm"], 1)

            def scores(b, k, half):
                if half == 0 and k % HG == 0:
                    g = k // HG
                    pe.wait_ge(c_in[g % 2], 32 * (2 * b + g // 2 + 1))
                if not (isinstance(b, int) and b == 0 and k == 0):
                    pe.wait_ge(S["exp"], at("exp", b, 2 * k + half - 1))
                for j in range(2):
                    c = 2 * half + j
                    ins = pe.matmul(s_ps[half][:, T * j:T * j + T], ks[0:ROWS_SHIFTED, k, P * c:P * c + P],
                                    qs[0:ROWS_SHIFTED, k, :], start=True, stop=True)
                ins.then_inc(S["s_mm"], 1)

            def products(b, k, part):
                g, j = k // HG, k % HG
                if part == 0:
                    if j == 0 and not (isinstance(b, int) and b == 0 and g == 0):
                        pe.wait_ge(S["y_set"], at("y_set", b, g))
                    if k == 0:
                        pe.wait_ge(S["v_set"], at("v_set", b, 4))
                pe.wait_ge(S["exp"], at("exp", b, 2 * k + part + 1))
                for c in (2 * part, 2 * part + 1):
                    for t in range(TT):
                        ins = pe.matmul(y_v[:, j, t, :], probs[:, k % 2, c, P * t:P * t + P],
                                        v_aug[:, c, k, :], start=(j == 0 and c == 0 and t == 0),
                                        stop=(c == TT - 1), skip_group_check=True)
                if part == 1:
                    ins.then_inc(S["pv"], 1)

            def step(b, k, first, last):
                i = (k + LEAD) % H
                nb = b + (k + LEAD) // H
                for place in range(4):
                    for name, n, bb in pieces(k, place, b, first, last):
                        piece(name, n, bb)
                    if place < 2 and not (last and k + LEAD >= H):
                        maxima(nb, i, place)
                    if place >= 2:
                        scores(b, k, place - 2)
                        if k > 0:
                            products(b, k - 1, place - 2)
                        elif not first:
                            products(b - 1, H - 1, place - 2)

            def full_step(b, k, first, last):
                if k == 0:
                    free[0] = None
                step(b, k, first, last)

            def tail(b):
                for part in range(2):
                    products(b, H - 1, part)
                for name, n in LAST_ONLY:
                    piece(name, n, b)

            pe.wait_ge(const_set, 7)
            pe.wait_ge(ones_set, 2)
            pe.wait_ge(vec_in, 16 * 13)
            pe.transpose(w_ps[:, 0:56], vrows[:, :], ident[0:56, 0:56]).then_inc(cols_mm, 1)
            pe.wait_ge(hid_rows, 1)
            pe.transpose(w_ps[:, 56:56 + B * TT], hrows[:, :], ident[0:B * TT, 0:B * TT]).then_inc(cols_mm, 1)
            pe.wait_ge(cols_set, 2)
            piece("zt", 0, 0)
            piece("zt", 1, 0)
            pe.wait_ge(perm_set, 4)
            pe.wait_ge(w_in[1], 32)
            for n in range(6):
                i, mc = n // 2, n % 2
                o = slice(P * mc, P * mc + P)
                for c in range(KC):
                    w = wperm[:, i, c, o] if i < 2 else wraw[:, K1, c, o]
                    nb = NB0 if i < 2 else NB1
                    pe.matmul(m_ps[0][:, n:n + 1], w, cols[:, nb + c:nb + c + 1], start=(c == 0), stop=False)
                bias = bperm[:, i, o] if i < 2 else brow[:, 3, o]
                pe.matmul(m_ps[0][:, n:n + 1], bias, one1[:, :], start=False, stop=True).then_inc(bias_mm, 1)
            pe.wait_ge(w_lo_set, 4)
            for n in range(4):
                piece("qk", n, 0)
            pe.wait_ge(w_in[2], 32)
            for w, nb, ps, off in ((V0, NB0, m_ps[1], 0), (Q1, NB1, s_ps[0], 0), (V1, NB1, s_ps[0], 512)):
                for c in range(KC):
                    ins = pe.matmul(ps[0:1, off:off + D], cols[:, nb + c:nb + c + 1], wraw[:, w, c, :],
                                    start=(c == 0), stop=(c == KC - 1))
                ins.then_inc(bias_mm, 1)
            pe.wait_ge(cond_set, 3)
            pe.wait_ge(emb_in, 32)
            cond_v = cond_s[:, :].rearrange("p (b k) -> p k b", k=EC)
            for l in range(2):
                for f in range(2 * KC):
                    for c in range(EC):
                        o = (2 * KC * l + f) * B
                        ins = pe.matmul(s_ps[1][:, o:o + B], embw[:, l, c, P * f:P * f + P], cond_v[:, c, :],
                                        start=(c == 0), stop=(c == EC - 1))
            ins.then_inc(film_mm, 1)
            pe.wait_ge(film_set, 9)
            pe.wait_ge(bias_set, 10)
            for h in range(LEAD):
                for part in range(2):
                    maxima(0, h, part)
                if h == HG:
                    piece("c", 0, 0)
            pe.wait_ge(w_lo_set, 16)
            batches(pe, full_step, tail)


_NAMES = ['x', 'cond_2048', 'mask_BxS_ff1', 'mask_BxS_ik0'] + [
    'L0_cond_' + n for n in ('norm_w', 'norm_b', 'q_w', 'q_b', 'k_w', 'k_b', 'v_w', 'v_b', 'emb_w', 'emb_b',
                             'sb_norm_w', 'sb_norm_b', 'out_w', 'out_b')] + [
    'L1_cond_' + n for n in ('norm_scale', 'norm_bias', 'Wq', 'bq', 'Wk', 'bk', 'Wv', 'bv', 'film_emb_W',
                             'film_emb_b', 'film_norm_scale', 'film_norm_bias', 'film_out_W', 'film_out_b')]


def kernel(**inputs):
    import numpy as _np
    import concourse.bacc as _bacc
    from concourse import mybir as _mybir
    from concourse.bass_utils import run_bass_kernel_spmd as _run

    nc = _bacc.Bacc("TRN2", target_bir_lowering=False, num_devices=1)
    arrays, args = {}, []
    for name in _NAMES:
        a = _np.ascontiguousarray(inputs[name])
        arrays[f"in_{name}"] = a
        args.append(nc.dram_tensor(f"in_{name}", a.shape, _mybir.dt.from_np(a.dtype), kind="ExternalInput").ap())
    result = nc.dram_tensor("out_0", inputs['x'].shape, _mybir.dt.float32, kind="ExternalOutput").ap()
    film_seq_kernel(nc, *args, result)
    r = _run(nc, [arrays], core_ids=[0])
    return r.results[0]["out_0"]
```

```python
import concourse.bass as bass
from concourse import mybir
from contextlib import ExitStack

F32 = mybir.dt.float32
F32R = mybir.dt.float32r
BF16 = mybir.dt.bfloat16
I32 = mybir.dt.int32
ALU = mybir.AluOpType
ACT = mybir.ActivationFunctionType
AX = mybir.AxisListType

P = 128
LN_EPS = 1e-5
MASK_PENALTY = 1e6
HIDDEN_KEY = -1e30
RSQRT_GUESS = 1597463007.0
NEWTON_STEPS = 3

ROW_MASK = 64
ROW_MAX = 96
ROWS_SCORE = 96
ROWS_SHIFTED = 98

PLACES = {
    0: [[], [("v", 0)], [], [("v", 1)]],
    1: [[("ye", 3), ("ln_next", 0)], [("yt", 3)], [("ln_a", 0)], [("z_next", 0)]],
    2: [[("c", 1)], [("zt", 0), ("z_a", 0)], [("zt", 1)], []],
    3: [[("film_a", 0)], [("film_a", 1)], [("qk", 0)], [("qk", 1)]],
    4: [[("out_a", 0)], [("out_a", 1)], [("qk", 2), ("ln_b", 0)], [("qk", 3)]],
    5: [[("ye", 0)], [("yt", 0)], [("z_b", 0)], []],
    6: [[("c", 2)], [("z1t", 0)], [("z1t", 1)], []],
    7: [[("k1", 0)], [("k1", 1)], [("qv", 0)], [("qv", 1)]],
    8: [[("qv", 2)], [("qv", 3)], [], [("softmax_q", 0)]],
    9: [[("ye", 1)], [("yt", 1)], [], []],
    10: [[("c", 3)], [("k1t", 0)], [("k1t", 1)], [("q1t", 0)]],
    11: [[("q1t", 1)], [("attn", 0)], [], []],
    12: [[("y1", 0)], [("y1", 1)], [("ln_c", 0)], []],
    13: [[("ye", 2)], [("yt", 2)], [("z_c", 0)], []],
    14: [[("c", 0)], [("film_c", 0)], [("film_c", 1)], []],
    15: [[("out_c", 0)], [("out_c", 1)], [], []],
}
NEXT = ("zt", "qk", "ln_next", "z_next")
OWN = ("v", "c", "ye", "yt")
NO_PRODUCT = ("ye", "ln_a", "ln_b", "ln_c", "ln_next", "z_a", "z_b", "z_c", "z_next", "softmax_q")
WITH_PRODUCT = [piece for k in range(16) for place in PLACES[k] for piece in place if piece[0] not in NO_PRODUCT]
BANK = {piece: i % 2 for i, piece in enumerate(WITH_PRODUCT)}


def film_seq_kernel(nc, x, cond_2048, mask_BxS_ff1, mask_BxS_ik0,
                    norm_w0, norm_b0, q_w0, q_b0, k_w0, k_b0, v_w0, v_b0, emb_w0, emb_b0,
                    film_w0, film_b0, out_w0, out_b0,
                    norm_w1, norm_b1, q_w1, q_b1, k_w1, k_b1, v_w1, v_b1, emb_w1, emb_b1,
                    film_w1, film_b1, out_w1, out_b1, out):
    B, T, D = x.shape
    E = cond_2048.shape[1]
    H, DH = 16, 16
    TT = T // P
    KC = D // P
    EC = E // P
    HG = 4
    G = H // HG
    M_HEAD = 32
    LEAD = 6
    assert T == 512 and D == H * DH == 256 and B == 4 and 2 * D == E

    ctx = ExitStack()
    with ctx:
        def sb(name, shape, dt=F32, scope=ctx):
            return scope.enter_context(nc.sbuf_tensor(name, shape, dt))

        def sem(name):
            return ctx.enter_context(nc.semaphore(name))

        wh = sb("w_hi", [P, 8, KC, D], F32R)
        wl = sb("w_lo", [P, 8, KC, D], F32R)
        Q0, K0, V0, K1, Q1, V1, O0, O1 = range(8)
        ident = sb("ident", [P, P])
        blocks = sb("blocks", [P, P], BF16)
        ones_row = sb("ones_row", [1, P], F32R)
        cols = sb("cols", [P, 56])
        own_key = sb("own_key", [P, B * TT])
        bias_cols = sb("bias_cols", [P, 6])
        bias_hi = sb("bias_hi", [1, 3 * D], F32R)
        bias_lo = sb("bias_lo", [1, 3 * D], F32R)
        film_s = sb("film_s", [P, 2, KC, B])
        film_t = sb("film_t", [P, 2, KC, B])
        outb = sb("outb", [P, 2, D])
        film_now = sb("film_now", [P, 2, 2, KC])
        mcol_now = sb("mcol_now", [P, TT])
        own_now = sb("own_now", [P, TT])
        x_in = sb("x_in", [P, TT, D])
        mrow = sb("mrow", [1, T])
        mrow_hi = sb("mrow_hi", [1, T], F32R)
        mrow_lo = sb("mrow_lo", [1, T], F32R)
        zt_hi = sb("zt_hi", [P, KC, T], F32R)
        zt_lo = sb("zt_lo", [P, KC, T], F32R)
        qk_hi = sb("qk_hi", [P, 2, KC, T], F32R)
        qk_lo = sb("qk_lo", [P, 2, KC, T], F32R)
        v_aug = sb("v_aug", [P, TT, H * (DH + 1) + M_HEAD - DH - 1])
        probs = sb("probs", [P, 2, TT, T])
        negmax = sb("negmax", [P, 2, HG * TT])
        crow_hi = sb("crow_hi", [HG * TT, P], F32R)
        crow_lo = sb("crow_lo", [HG * TT, P], F32R)
        recip = sb("recip", [P, HG * TT])
        y0 = sb("y0", [P, TT, D])
        yk = sb("yk", [P, TT, D])
        zn = sb("zn", [P, TT, D])
        x_res = sb("x_res", [P, TT, D])
        film_u = sb("film_u", [P, T])
        at_hi = sb("at_hi", [P, KC, T], F32R)
        at_lo = sb("at_lo", [P, KC, T], F32R)
        q1 = sb("q1_sb", [P, TT, D])
        v1 = sb("v1_sb", [P, TT, D])
        k1 = sb("k1_sb", [P, KC, T])
        film_h = k1
        yt_sb = sb("yt_sb", [P, T])
        q1t = k1
        hide = sb("hide", [P, T])
        attn = sb("attn_sb", [P, KC, P])
        q1max = sb("q1max", [P, TT, H])
        q1sum = sb("q1sum", [P, TT * H])
        q1rec = sb("q1rec", [P, TT * H])
        k1max = sb("k1max", [P, KC])
        k1sum = sb("k1sum", [P, KC])
        k1rec = sb("k1rec", [P, KC])
        three_halves = sb("three_halves", [P, TT])
        ln = {n: dict(stats=sb(f"stats_{n}", [P, TT, 6]), sum=sb(f"sum_{n}", [P, TT, 2]),
                      diff=sb(f"diff_{n}", [P, TT]), mean=sb(f"mean_{n}", [P, TT]),
                      var=sb(f"var_{n}", [P, TT]), nhalf=sb(f"nhalf_{n}", [P, TT]), y=sb(f"rstd_{n}", [P, TT]),
                      t=sb(f"newton_{n}", [P, TT])) for n in ("next", "last")}

        s_ps, m_ps, y_ps, w_ps = [
            [ctx.enter_context(nc.psum_tensor(f"{name}_ps{i}", [P, T], F32)) for i in range(2)]
            for name in ("s", "m", "y", "w")]
        VW = DH + 1
        v_heads = v_aug[:, :, 0:H * VW].rearrange("p t (h d) -> p t h d", d=VW)

        vec_in, bias_in, outb_in, emb_in = sem("vec_in"), sem("bias_in"), sem("outb_in"), sem("emb_in")
        w_in = [sem(f"w_in{i}") for i in range(4)]
        const_set, ones_set, cols_mm, cols_set = sem("const_set"), sem("ones_set"), sem("cols_mm"), sem("cols_set")
        hid_rows, perm_set, bias_mm, bias_set = sem("hid_rows"), sem("perm_set"), sem("bias_mm"), sem("bias_set")
        cond_set, film_mm, film_set = sem("cond_set"), sem("film_mm"), sem("film_set")
        w_hi_set, w_lo_set, stack_set = sem("w_hi_set"), sem("w_lo_set"), sem("stack_set")

        PER = {}

        def batch_sem(name, per):
            s = sem(name)
            PER[name] = per
            return s

        def at(name, b, n):
            return PER[name] * b + n

        S = {name: batch_sem(name, per) for name, per in dict(
            x_in=16, mrow_in=16, mrow_shift=1, mrow_hi=1, mrow_lo=1, mcol=1, own=1, film_now=2,
            bn_next=12, newton_next=4 * NEWTON_STEPS, z_next=4,
            bn_a=12, newton_a=4 * NEWTON_STEPS, z_a=4,
            bn_b=12, newton_b=4 * NEWTON_STEPS, z_b=4,
            bn_c=12, newton_c=4 * NEWTON_STEPS, z_c=4,
            zt_mm=2, zt_hi=2, zt_lo=2, qk_mm=4, qk_hi=4, qk_lo=4, v_mm=2, v_set=4,
            m_mm=64, m_red=64, c_mm=4, c_hi=4, c_lo=4,
            s_mm=64, exp=64, pv=64, y_ev=4, yt_mm=4, y_rec=4, y_set=4,
            res_in=16, res_b=1, hide_in=16, hide_set=1,
            fa_mm=2, fa_u=2, fa_t=2, fa_h=2, fa_hi=2, fa_lo=2,
            fc_mm=2, fc_u=2, fc_t=2, fc_h=2, fc_hi=2, fc_lo=2,
            oa_mm=2, oa_set=2, res_c=1, z1_mm=2, z1_hi=2, z1_lo=2,
            k1_mm=2, k1_b=2, k1_max=2, k1_exp=2, k1_rec=2, k1_n=2,
            qv_mm=4, v1_set=4, q1_max=4, q1_sub=4, q1_exp=1, q1_sum=1, q1_rec=1,
            kt_mm=2, kt_set=2, qt_mm=2, qt_set=2, at_mm=1, at_set=1, y1_mm=2, y1_set=4,
            oc_mm=2, oc_set=2, stored=16).items()}
        c_in = [sem("c_in0"), sem("c_in1")]
        fill = [sem(f"fill{g}") for g in range(G)]

        prep = ExitStack()
        wraw = sb("wraw", [P, 8, KC, D], F32, prep)
        wperm = sb("wperm", [P, 2, KC, D], F32, prep)
        embw = sb("embw", [P, 2, EC, 2 * D], F32, prep)
        vrows = sb("vrows", [56, P], F32, prep)
        hrows_i = sb("hrows_i", [B * TT, P], I32, prep)
        hrows = sb("hrows", [B * TT, P], F32, prep)
        brow = sb("brow", [1, 6, D], F32, prep)
        bperm = sb("bperm", [1, 2, D], F32, prep)
        one1 = sb("one1", [1, 1], F32, prep)
        cond_t = sb("cond_t", [P, B * EC], F32, prep)
        cond_h = sb("cond_h", [P, B * EC], F32, prep)
        cond_s = sb("cond_s", [P, B * EC], F32, prep)
        emb_e = sb("emb_e", [P, 2, 2, KC, B], F32, prep)
        emb_p = sb("emb_p", [P, 2, KC, B], F32, prep)
        emb_q = sb("emb_q", [P, 2, KC, B], F32, prep)
        prep.close()
        qs = sb("q_stack", [P, H, T], F32R)
        ks = sb("k_stack", [P, H, T], F32R)

        NW0, NB0, NW1, NB1, FW0, FB0, FW1, FB1 = range(0, 16, 2)
        EB = 16
        CD = 24
        MC = 40
        fcols = cols[:, FW0:FW0 + 8].rearrange("p (l w c) -> p l w c", l=2, w=2)

        def scale_col(w, c):
            n = NW0 if w in (Q0, K0, V0) else NW1
            return cols[:, n + c:n + c + 1]

        def tiles(ap):
            return ap.rearrange("(t p) d -> p t d", p=P)

        def regroup(ap):
            return ap.rearrange("p (g h d) -> p g d h", g=G, h=HG)

        block = ctx.enter_context(nc.Block())

        def batch_of(name, n, b, first, last):
            if name in NEXT or (name == "c" and n == 0):
                return None if last else b + 1
            if name in OWN and not (name in ("ye", "yt") and n == G - 1):
                return b
            return None if first else b - 1

        def pieces(k, place, b, first, last):
            for name, n in PLACES[k][place]:
                bb = batch_of(name, n, b, first, last)
                if bb is not None:
                    yield name, n, bb

        LAST_ONLY = [(name, n) for k in range(H) for place in PLACES[k] for name, n in place
                     if name not in NEXT + OWN or (name in ("ye", "yt") and n == G - 1)]

        def batches(eng, step, tail):
            for k in range(H):
                step(0, k, True, False)
            with eng.Fori(1, B - 1) as b:
                for k in range(H):
                    step(b, k, False, False)
            for k in range(H):
                step(B - 1, k, False, True)
            tail(B - 1)

        @block.sync
        def _(sp):
            def words(ap):
                return ap.bitcast(F32)

            row = 0
            for v, n in ((norm_w0, KC), (norm_b0, KC), (norm_w1, KC), (norm_b1, KC), (film_w0, KC),
                         (film_b0, KC), (film_w1, KC), (film_b1, KC), (emb_b0, EC), (emb_b1, EC)):
                sp.dma_start(vrows[row:row + n, :], v.rearrange("(c p) -> c p", p=P)).then_inc(vec_in, 16)
                row += n
            sp.dma_start(vrows[CD:CD + B * EC, :], cond_2048.rearrange("b (k p) -> (b k) p", p=P)).then_inc(vec_in, 16)
            sp.dma_start(vrows[MC:MC + B * TT, :], mask_BxS_ff1.rearrange("b (t p) -> (b t) p", p=P)).then_inc(vec_in, 16)
            sp.dma_start(hrows_i[:, :], mask_BxS_ik0.rearrange("b (t p) -> (b t) p", p=P)).then_inc(vec_in, 16)

            for i, v in enumerate((q_b0, k_b0, v_b0, k_b1, q_b1, v_b1)):
                sp.dma_start(brow[:, i, :], v.rearrange("(a n) -> a n", a=1)).then_inc(bias_in, 16)
            for i, w in enumerate((q_w0, k_w0, v_w0, k_w1, q_w1, v_w1, out_w0, out_w1)):
                sp.dma_start(wraw[:, i, :, :], w.rearrange("(c p) n -> p c n", p=P)).then_inc(w_in[i // 2], 16)
            for i, w in enumerate((emb_w0, emb_w1)):
                sp.dma_start(embw[:, i, :, :], w.rearrange("(c p) n -> p c n", p=P)).then_inc(emb_in, 16)
            for i, v in enumerate((out_b0, out_b1)):
                sp.dma_start(outb[:, i, :], v.rearrange("(a n) -> a n", a=1).broadcast_to([P, D])).then_inc(outb_in, 16)

            def fill_group(b, g):
                mc, part = g // 2, slice(64 * (g % 2), 64 * (g % 2) + 64)
                slots = slice(HG * g, HG * g + HG)
                for stack, i, order in ((qs, 0, (qk_hi, qk_hi, qk_lo, qk_lo)),
                                        (ks, 1, (qk_hi, qk_lo, qk_hi, qk_lo))):
                    for r, src in enumerate(order):
                        sp.dma_start(words(stack[DH * r:DH * r + DH, slots, :]), words(src[part, i, mc, :]))\
                          .then_inc(fill[g], 16)
                for r, src in enumerate((mrow_hi, mrow_lo)):
                    sp.dma_start(words(ks[ROW_MASK + r:ROW_MASK + r + 1, slots, :]),
                                 words(src[:, :]).unsqueeze(1).broadcast_to([1, HG, T])).then_inc(fill[g], 16)

            def shift_rows(b, g):
                sp.wait_ge(S["c_lo"], at("c_lo", b, g + 1))
                for r, src in enumerate((crow_hi, crow_lo)):
                    dst = qs[ROW_MAX + r:ROW_MAX + r + 1, HG * g:HG * g + HG, :]
                    sp.dma_start(words(dst).rearrange("a h (t p) -> a (h t) p", p=P), words(src[:, :]))\
                      .then_inc(c_in[g % 2], 16)

            def step(b, k, first, last):
                if k in (0, 5, 9, 13) and not (last and k > 0):
                    h = k + LEAD
                    sp.wait_ge(S["m_red"], at("m_red", b, TT * h + 1))
                    fill_group(*{0: (b, 3), 5: (b + 1, 0), 9: (b + 1, 1), 13: (b + 1, 2)}[k])
                if k in (2, 6, 10):
                    shift_rows(b, (k + 2) // 4)
                if not last and k == 14:
                    shift_rows(b + 1, 0)

            sp.wait_ge(stack_set, 3)
            for g in range(3):
                sp.wait_ge(S["mrow_lo"], 1)
                sp.wait_ge(S["qk_lo"], 2 * (g // 2) + 2)
                fill_group(0, g)
            shift_rows(0, 0)

            def tail(b):
                sp.wait_ge(S["stored"], at("stored", b, 16))

            batches(sp, step, tail)

        def newton(pool, which, name, b):
            t = ln[which]
            s, done = S[name], 0

            def after(ins):
                nonlocal done
                done += 1
                ins.then_inc(s, 1)
                pool.wait_ge(s, at(name, b, done))

            for _ in range(NEWTON_STEPS):
                after(pool.tensor_tensor(t["t"][:, :], t["y"][:, :], t["y"][:, :], ALU.mult))
                after(pool.tensor_tensor(t["t"][:, :], t["t"][:, :], t["nhalf"][:, :], ALU.mult))
                after(pool.tensor_tensor(t["t"][:, :], t["t"][:, :], three_halves[:, :], ALU.add))
                after(pool.tensor_tensor(t["y"][:, :], t["y"][:, :], t["t"][:, :], ALU.mult))

        NEWTON = 4 * NEWTON_STEPS
        STATS = TT + 8
        LN_OF = {"next": ("next", x_in, x_in), "a": ("last", y0, zn), "b": ("last", x_res, zn),
                 "c": ("last", yk, zn)}

        @block.gpsimd
        def _(pool):
            pool.memset(ident[:, :], 0.0).then_inc(const_set, 1)
            pool.memset(blocks[:, :], 1.0).then_inc(const_set, 1)
            pool.memset(one1[:, :], 1.0).then_inc(const_set, 1)
            pool.wait_ge(const_set, 3)
            pool.affine_select(out=ident[:, :], in_=ident[:, :], compare_op=ALU.not_equal, fill=1.0,
                               base=0, pattern=[[-1, P]], channel_multiplier=1).then_inc(const_set, 1)
            bview = blocks[:, :].rearrange("p (n e) -> p n e", e=DH)
            pool.affine_select(out=bview, in_=bview, compare_op=ALU.is_ge, fill=0.0,
                               base=0, pattern=[[-DH, P // DH], [0, DH]], channel_multiplier=1).then_inc(const_set, 1)
            pool.wait_ge(const_set, 5)
            pool.affine_select(out=bview, in_=bview, compare_op=ALU.is_ge, fill=0.0,
                               base=DH - 1, pattern=[[DH, P // DH], [0, DH]], channel_multiplier=-1).then_inc(const_set, 1)
            pool.memset(v_aug[:, :, :], 1.0).then_inc(const_set, 1)

            def piece(name, n, b):
                if name.startswith("ln_"):
                    which = name[3:]
                    pool.wait_ge(S[f"bn_{which}"], at(f"bn_{which}", b, STATS))
                    newton(pool, LN_OF[which][0], f"newton_{which}", b)
                    if which == "a":
                        pool.wait_ge(S["res_in"], at("res_in", b, 16))
                        if isinstance(b, int) and b == 0:
                            pool.wait_ge(outb_in, 32)
                        pool.tensor_tensor(x_res[:, :, :], x_res[:, :, :],
                                           outb[:, 0:1, :].broadcast_to([P, TT, D]), ALU.add)\
                            .then_inc(S["res_b"], 1)
                if name == "z_b":
                    pool.wait_ge(S["z_b"], at("z_b", b, 4))
                    pool.tensor_tensor(x_res[:, :, :], x_res[:, :, :],
                                       outb[:, 1:2, :].broadcast_to([P, TT, D]), ALU.add)\
                        .then_inc(S["res_c"], 1)
                if name in ("film_a", "film_c"):
                    f = "f" + name[-1]
                    pool.wait_ge(S[f + "_hi"], at(f + "_hi", b, n + 1))
                    pool.tensor_tensor(at_lo[:, n, :], film_h[:, n, :], at_hi[:, n, :].bitcast(F32),
                                       ALU.subtract).then_inc(S[f + "_lo"], 1)

            def step(b, k, first, last):
                for place in range(4):
                    for name, n, bb in pieces(k, place, b, first, last):
                        piece(name, n, bb)

            def tail(b):
                for name, n in LAST_ONLY:
                    piece(name, n, b)

            pool.wait_ge(ones_set, 2)
            piece("ln_next", 0, 0)
            batches(pool, step, tail)

        @block.scalar
        def _(act):
            act.dma_start(x_in[:, :, :], tiles(x[0])).then_inc(S["x_in"], 16)
            act.dma_start(mrow[:, :], mask_BxS_ff1[0:1, :]).then_inc(S["mrow_in"], 16)
            act.wait_ge(cols_set, 1)
            act.activation(cond_t[:, :], cols[:, CD:CD + B * EC], ACT.Tanh, scale=0.5).then_inc(cond_set, 1)

            def weight_hi(w):
                for c in range(KC):
                    src = wperm[:, w, c, :] if w in (Q0, K0) else wraw[:, w, c, :]
                    if w in (O0, O1):
                        act.activation(wh[:, w, c, :], src, ACT.Copy).then_inc(w_hi_set, 1)
                    else:
                        act.activation(wh[:, w, c, :], src, ACT.Copy, scale=scale_col(w, c)).then_inc(w_hi_set, 1)

            act.wait_ge(perm_set, 2)
            weight_hi(Q0)
            weight_hi(K0)

            def piece(name, n, b):
                if name not in NO_PRODUCT:
                    w_now = w_ps[BANK[name, n]]
                if name == "zt":
                    if n == 0 and not (isinstance(b, int) and b == 0):
                        act.wait_ge(S["v_mm"], at("v_mm", b - 1, 2))
                    act.wait_ge(S["zt_mm"], at("zt_mm", b, n + 1))
                    act.activation(zt_hi[:, n, :], w_now[:, :], ACT.Copy).then_inc(S["zt_hi"], 1)
                elif name == "qk":
                    mc, i = n // 2, n % 2
                    if i == 0 and not (isinstance(b, int) and b == 0):
                        act.wait_ge(fill[2 * mc], 160 * b)
                        act.wait_ge(fill[2 * mc + 1], 160 * b)
                    act.wait_ge(S["qk_mm"], at("qk_mm", b, n + 1))
                    act.activation(qk_hi[:, i, mc, :], w_now[:, :], ACT.Identity,
                                   bias=bias_cols[:, 2 * i + mc:2 * i + mc + 1]).then_inc(S["qk_hi"], 1)
                elif name == "v":
                    act.wait_ge(S["v_mm"], at("v_mm", b, n + 1))
                    if n == 0:
                        act.wait_ge(S["mcol"], at("mcol", b, 1))
                    for t in (2 * n, 2 * n + 1):
                        if not (isinstance(b, int) and b == 0):
                            act.wait_ge(S["pv"], at("pv", b - 1, TT * (H - 1) + t + 1))
                        act.activation(v_heads[:, t, :, 0:DH],
                                       w_now[:, D * (t % 2):D * (t % 2) + D].rearrange("p (h d) -> p h d", h=H),
                                       ACT.Copy, scale=mcol_now[:, t:t + 1]).then_inc(S["v_set"], 1)
                elif name in ("film_a", "film_c"):
                    f, layer = "f" + name[-1], 0 if name == "film_a" else 1
                    act.wait_ge(S[f + "_mm"], at(f + "_mm", b, n + 1))
                    if n == 0 and layer == 0:
                        act.wait_ge(S["film_now"], at("film_now", b, 2))
                    if n == 1:
                        act.wait_ge(S[f + "_h"], at(f + "_h", b, 1))
                    for which, func, dst in (("_u", ACT.Identity, film_u[:, :]), ("_t", ACT.Tanh, film_h[:, n, :])):
                        act.activation(dst, w_now[:, :], func, scale=film_now[:, layer, 0, n:n + 1],
                                       bias=film_now[:, layer, 1, n:n + 1]).then_inc(S[f + which], 1)
                    act.wait_ge(S[f + "_h"], at(f + "_h", b, n + 1))
                    act.activation(at_hi[:, n, :], film_h[:, n, :], ACT.Copy).then_inc(S[f + "_hi"], 1)
                elif name == "z1t":
                    act.wait_ge(S["z1_mm"], at("z1_mm", b, n + 1))
                    act.activation(at_hi[:, n, :], w_now[:, :], ACT.Copy).then_inc(S["z1_hi"], 1)
                elif name == "k1":
                    act.wait_ge(S["k1_max"], at("k1_max", b, n + 1))
                    act.activation(k1[:, n, :], k1[:, n, :], ACT.Exp, bias=k1max[:, n:n + 1],
                                   accum_out=k1sum[:, n:n + 1]).then_inc(S["k1_exp"], 1)
                elif name == "qv":
                    act.wait_ge(S["qv_mm"], at("qv_mm", b, n + 1))
                    if n == 0:
                        act.wait_ge(S["own"], at("own", b, 1))
                    act.activation(v1[:, n, :], w_now[:, D:2 * D], ACT.Copy, scale=own_now[:, n:n + 1])\
                        .then_inc(S["v1_set"], 1)
                elif name == "softmax_q":
                    act.wait_ge(S["q1_sub"], at("q1_sub", b, 4))
                    act.activation(q1[:, :, :], q1[:, :, :], ACT.Exp).then_inc(S["q1_exp"], 1)
                elif name == "k1t":
                    act.wait_ge(S["kt_mm"], at("kt_mm", b, n + 1))
                    act.activation(yk[:, :, P * n:P * n + P], w_now[:, :].rearrange("p (t f) -> p t f", t=TT),
                                   ACT.Copy).then_inc(S["kt_set"], 1)
                elif name == "ye":
                    act.wait_ge(S["pv"], at("pv", b, TT * HG * (n + 1)))
                    if not (isinstance(b, int) and b == 0 and n == 0):
                        act.wait_ge(S["yt_mm"], at("yt_mm", b, n))
                    act.activation(yt_sb[:, :], y_ps[n % 2][:, :], ACT.Copy).then_inc(S["y_ev"], 1)
                elif name == "q1t":
                    act.wait_ge(S["qt_mm"], at("qt_mm", b, n + 1))
                    act.activation(q1t[:, n, :], w_now[:, :], ACT.Copy).then_inc(S["qt_set"], 1)

            def load_batch(b):
                if not isinstance(b, int) or b > 0:
                    act.wait_ge(S["zt_mm"], at("zt_mm", b - 1, 2))
                act.dma_start(x_in[:, :, :], tiles(x[b])).then_inc(S["x_in"], 16)

            def load_mask(b):
                if not isinstance(b, int) or b > 0:
                    act.wait_ge(fill[G - 1], 160 * b)
                act.dma_start(mrow[:, :], mask_BxS_ff1[bass.ds(b, 1), :]).then_inc(S["mrow_in"], 16)

            def load_last(b):
                act.dma_start(x_res[:, :, :], tiles(x[b])).then_inc(S["res_in"], 16)
                act.dma_start(hide[:, :].bitcast(I32), mask_BxS_ik0[bass.ds(b, 1), :].broadcast_to([P, T])).then_inc(S["hide_in"], 16)

            def store(b):
                act.wait_ge(S["oc_set"], at("oc_set", b, 2))
                act.dma_start(tiles(out[b]), x_res[:, :, :]).then_inc(S["stored"], 16)

            def exponentials(b, k, c):
                act.wait_ge(S["s_mm"], at("s_mm", b, TT * k + c + 1))
                if not (isinstance(b, int) and H * b + k < 2):
                    act.wait_ge(S["pv"], at("pv", b, TT * (k - 2) + c + 1))
                act.activation(probs[:, k % 2, c, :], s_ps[c % 2][:, :], ACT.Exp).then_inc(S["exp"], 1)

            def step(b, k, first, last):
                if k == 0:
                    if not last:
                        load_batch(b + 1)
                    if not first:
                        load_last(b - 1)
                if k == 2 and not last:
                    load_mask(b + 1)
                for place in range(4):
                    exponentials(b, k, place)
                    for name, n, bb in pieces(k, place, b, first, last):
                        piece(name, n, bb)
                if k == H - 1 and not first:
                    store(b - 1)
                if k == H - 1 and not first:
                    act.wait_ge(S["stored"], at("stored", b - 1, 16))

            def tail(b):
                load_last(b)
                for name, n in LAST_ONLY:
                    piece(name, n, b)
                store(b)

            piece("zt", 0, 0)
            piece("zt", 1, 0)
            act.wait_ge(bias_set, 1)
            for n in range(4):
                piece("qk", n, 0)
            act.wait_ge(w_in[1], 32)
            act.wait_ge(w_in[2], 32)
            act.wait_ge(w_in[3], 32)
            for w in (V0, K1, Q1, V1, O0, O1):
                weight_hi(w)
            batches(act, step, tail)

        @block.vector
        def _(dve):
            nm = nc.vector

            def statistics(which, b, wait):
                scratch, src, _ = LN_OF[which]
                t = ln[scratch]
                s, name, done = S[f"bn_{which}"], f"bn_{which}", 0

                def then(ins):
                    nonlocal done
                    done += 1
                    ins.then_inc(s, 1)

                def settled():
                    dve.wait_ge(s, at(name, b, done))

                wait()
                for i in range(TT):
                    then(dve.bn_stats(t["stats"][:, i, :], src[:, i, :]))
                settled()
                even, odd = t["stats"][:, :, 1:3], t["stats"][:, :, 4:6]
                then(dve.tensor_tensor(t["sum"][:, :, :], even, odd, ALU.add))
                then(dve.tensor_tensor(t["diff"][:, :], even[:, :, 0], odd[:, :, 0], ALU.subtract))
                settled()
                then(dve.tensor_scalar(t["mean"][:, :], t["sum"][:, :, 0], 0.5, None, ALU.mult))
                then(dve.tensor_scalar(t["var"][:, :], t["sum"][:, :, 1], 1.0 / D, LN_EPS, ALU.mult, ALU.add))
                then(dve.scalar_tensor_tensor(t["diff"][:, :], t["diff"][:, :], 0.25, t["diff"][:, :],
                                              ALU.mult, ALU.mult))
                settled()
                then(dve.tensor_tensor(t["var"][:, :], t["var"][:, :], t["diff"][:, :], ALU.add))
                settled()
                then(dve.tensor_scalar(t["nhalf"][:, :], t["var"][:, :], -0.5, None, ALU.mult))
                then(dve.tensor_scalar(t["y"][:, :].bitcast(I32), t["var"][:, :].bitcast(I32), -0.5,
                                       RSQRT_GUESS, ALU.mult, ALU.add))

            def normalise(which, b):
                scratch, src, dst = LN_OF[which]
                t = ln[scratch]
                dve.wait_ge(S[f"newton_{which}"], at(f"newton_{which}", b, NEWTON))
                for i in range(TT):
                    dve.tensor_scalar(dst[:, i, :], src[:, i, :], t["mean"][:, i:i + 1], t["y"][:, i:i + 1],
                                      ALU.subtract, ALU.mult).then_inc(S[f"z_{which}"], 1)

            dve.memset(three_halves[:, :], 1.5).then_inc(ones_set, 1)
            dve.memset(ones_row[:, :].bitcast(F32), 1.0).then_inc(ones_set, 1)
            dve.wait_ge(vec_in, 16 * 13)
            dve.tensor_scalar(hrows[:, :], hrows_i[:, :], 1.0, None, ALU.is_equal).then_inc(hid_rows, 1)
            dve.wait_ge(cols_mm, 2)
            dve.tensor_copy(cols[:, :], w_ps[0][:, 0:56]).then_inc(cols_set, 1)
            dve.tensor_scalar(own_key[:, :], w_ps[0][:, 56:56 + B * TT], -1.0, 1.0, ALU.mult, ALU.add)\
               .then_inc(cols_set, 1)
            statistics("next", 0, lambda: dve.wait_ge(S["x_in"], 16))
            dve.wait_ge(w_in[0], 32)
            dve.tensor_copy(wperm[:, Q0, :, :].rearrange("p c (g d h) -> p (c g) d h", g=G, d=DH),
                            wraw[:, Q0, :, :].rearrange("p c (g h d) -> p (c g) d h", g=G, h=HG)).then_inc(perm_set, 1)
            dve.tensor_copy(wperm[:, K0, :, :].rearrange("p c (g d h) -> p (c g) d h", g=G, d=DH),
                            wraw[:, K0, :, :].rearrange("p c (g h d) -> p (c g) d h", g=G, h=HG)).then_inc(perm_set, 1)
            dve.wait_ge(bias_in, 16 * 6)
            for i in range(2):
                dve.tensor_copy(bperm[:, i, :].rearrange("p (g d h) -> p g d h", g=G, d=DH),
                                regroup(brow[:, i, :])).then_inc(perm_set, 1)
            normalise("next", 0)

            def weight_lo(w):
                for c in range(KC):
                    src = wperm[:, w, c, :] if w in (Q0, K0) else wraw[:, w, c, :]
                    if w in (O0, O1):
                        dve.tensor_tensor(wl[:, w, c, :], src, wh[:, w, c, :].bitcast(F32), ALU.subtract)\
                           .then_inc(w_lo_set, 1)
                    else:
                        dve.scalar_tensor_tensor(wl[:, w, c, :], src, scale_col(w, c),
                                                 wh[:, w, c, :].bitcast(F32), ALU.mult, ALU.subtract)\
                           .then_inc(w_lo_set, 1)

            dve.wait_ge(cols_set, 1)
            for w in (Q0, K0):
                dve.wait_ge(w_hi_set, 2 * w + 2)
                weight_lo(w)

            def piece(name, n, b):
                if name not in NO_PRODUCT:
                    w_now = w_ps[BANK[name, n]]
                if name.startswith("ln_"):
                    which = name[3:]
                    ready = {"next": lambda: dve.wait_ge(S["x_in"], at("x_in", b, 16)),
                             "a": lambda: dve.wait_ge(S["y_set"], at("y_set", b, G)),
                             "b": lambda: dve.wait_ge(S["oa_set"], at("oa_set", b, 2)),
                             "c": lambda: dve.wait_ge(S["y1_set"], at("y1_set", b, 4))}[which]
                    statistics(which, b, ready)
                elif name in ("z_a", "z_b", "z_c", "z_next"):
                    normalise(name[2:], b)
                    if name == "z_a":
                        dve.tensor_copy(film_now[:, :, 0, :].unsqueeze(3), film_s[:, :, :, bass.ds(b, 1)]).then_inc(S["film_now"], 1)
                        dve.tensor_copy(film_now[:, :, 1, :].unsqueeze(3), film_t[:, :, :, bass.ds(b, 1)]).then_inc(S["film_now"], 1)
                        dve.tensor_copy(own_now[:, :], own_key[:, bass.ds(b * TT, TT)]).then_inc(S["own"], 1)
                        dve.wait_ge(S["hide_in"], at("hide_in", b, 16))
                        dve.tensor_scalar(hide[:, :], hide[:, :].bitcast(I32), 1.0, HIDDEN_KEY, ALU.is_equal, ALU.mult)\
                           .then_inc(S["hide_set"], 1)
                elif name == "zt":
                    dve.wait_ge(S["zt_hi"], at("zt_hi", b, n + 1))
                    dve.tensor_tensor(zt_lo[:, n, :], w_now[:, :], zt_hi[:, n, :].bitcast(F32), ALU.subtract)\
                       .then_inc(S["zt_lo"], 1)
                elif name == "qk":
                    mc, i = n // 2, n % 2
                    dve.wait_ge(S["qk_hi"], at("qk_hi", b, n + 1))
                    dve.scalar_tensor_tensor(qk_lo[:, i, mc, :], w_now[:, :],
                                             bias_cols[:, 2 * i + mc:2 * i + mc + 1],
                                             qk_hi[:, i, mc, :].bitcast(F32), ALU.add, ALU.subtract)\
                       .then_inc(S["qk_lo"], 1)
                elif name == "c":
                    dve.wait_ge(S["c_mm"], at("c_mm", b, n + 1))
                    if not (isinstance(b, int) and b == 0 and n == 0):
                        prev = 2 * b + (n - 1) // 2 + 1
                        dve.wait_ge(c_in[(n - 1) % 2], 32 * prev)
                    dve.tensor_copy(crow_hi[:, :], w_now[0:HG * TT, 0:P]).then_inc(S["c_hi"], 1)
                    dve.wait_ge(S["c_hi"], at("c_hi", b, n + 1))
                    dve.tensor_tensor(crow_lo[:, :], w_now[0:HG * TT, 0:P], crow_hi[:, :].bitcast(F32),
                                      ALU.subtract).then_inc(S["c_lo"], 1)
                elif name == "yt":
                    dve.wait_ge(S["yt_mm"], at("yt_mm", b, n + 1))
                    heads = w_now[:, :].rearrange("p (t h d) -> p t h d", h=HG, d=M_HEAD)
                    dve.reciprocal(recip[:, :].rearrange("p (t h) -> p t h", h=HG), heads[:, :, :, DH])\
                       .then_inc(S["y_rec"], 1)
                    dve.wait_ge(S["y_rec"], at("y_rec", b, n + 1))
                    dst = y0[:, :, HG * DH * n:HG * DH * (n + 1)].rearrange("p t (h d) -> p t h d", h=HG)
                    dve.tensor_tensor(dst, heads[:, :, :, 0:DH],
                                      recip[:, :].rearrange("p (t h) -> p t h", h=HG).unsqueeze(3)
                                      .broadcast_to([P, TT, HG, DH]), ALU.mult).then_inc(S["y_set"], 1)
                elif name in ("film_a", "film_c"):
                    f = "f" + name[-1]
                    dve.wait_ge(S[f + "_t"], at(f + "_t", b, n + 1))
                    dve.scalar_tensor_tensor(film_h[:, n, :], film_h[:, n, :], 1.0, film_u[:, :],
                                             ALU.add, ALU.mult).then_inc(S[f + "_h"], 1)
                elif name == "out_a":
                    dve.wait_ge(S["oa_mm"], at("oa_mm", b, n + 1))
                    dve.wait_ge(S["res_b"], at("res_b", b, 1))
                    xr = x_res[:, 2 * n:2 * n + 2, :].rearrange("p t d -> p (t d)")
                    dve.tensor_tensor(xr, w_now[:, :], xr, ALU.add).then_inc(S["oa_set"], 1)
                elif name == "z1t":
                    dve.wait_ge(S["z1_hi"], at("z1_hi", b, n + 1))
                    dve.tensor_tensor(at_lo[:, n, :], w_now[:, :], at_hi[:, n, :].bitcast(F32), ALU.subtract)\
                       .then_inc(S["z1_lo"], 1)
                elif name == "k1":
                    dve.wait_ge(S["k1_mm"], at("k1_mm", b, n + 1))
                    dve.wait_ge(S["hide_set"], at("hide_set", b, 1))
                    dve.scalar_tensor_tensor(k1[:, n, :], w_now[:, :], bias_cols[:, 4 + n:5 + n], hide[:, :],
                                             ALU.add, ALU.add).then_inc(S["k1_b"], 1)
                    dve.wait_ge(S["k1_b"], at("k1_b", b, n + 1))
                    dve.tensor_reduce(k1max[:, n:n + 1], k1[:, n, :], AX.X, ALU.max, negate=True)\
                       .then_inc(S["k1_max"], 1)
                elif name == "qv":
                    dve.wait_ge(S["v1_set"], at("v1_set", b, n + 1))
                    qv = w_now[:, 0:D].rearrange("p (h d) -> p h d", h=H)
                    dve.tensor_reduce(q1max[:, n, :], qv, AX.X, ALU.max).then_inc(S["q1_max"], 1)
                    dve.wait_ge(S["q1_max"], at("q1_max", b, n + 1))
                    dve.tensor_tensor(q1[:, n, :].rearrange("p (h d) -> p h d", h=H), qv,
                                      q1max[:, n, :].unsqueeze(2).broadcast_to([P, H, DH]), ALU.subtract)\
                       .then_inc(S["q1_sub"], 1)
                elif name == "softmax_q":
                    for c in range(KC):
                        dve.wait_ge(S["k1_exp"], at("k1_exp", b, c + 1))
                        dve.reciprocal(k1rec[:, c:c + 1], k1sum[:, c:c + 1]).then_inc(S["k1_rec"], 1)
                        dve.wait_ge(S["k1_rec"], at("k1_rec", b, c + 1))
                        dve.tensor_scalar(k1[:, c, :], k1[:, c, :], k1rec[:, c:c + 1], None, ALU.mult)\
                           .then_inc(S["k1_n"], 1)
                    dve.wait_ge(S["q1_exp"], at("q1_exp", b, 1))
                    dve.tensor_reduce(q1sum[:, :], q1[:, :, :].rearrange("p t (h d) -> p (t h) d", h=H),
                                      AX.X, ALU.add).then_inc(S["q1_sum"], 1)
                    dve.wait_ge(S["q1_sum"], at("q1_sum", b, 1))
                    dve.reciprocal(q1rec[:, :], q1sum[:, :]).then_inc(S["q1_rec"], 1)
                elif name == "attn":
                    dve.wait_ge(S["at_mm"], at("at_mm", b, 1))
                    dve.tensor_tensor(attn[:, :, :], w_now[:, 0:KC * P].rearrange("p (c e) -> p c e", c=KC),
                                      blocks[:, :].unsqueeze(1).broadcast_to([P, KC, P]), ALU.mult)\
                       .then_inc(S["at_set"], 1)
                elif name == "y1":
                    dve.wait_ge(S["y1_mm"], at("y1_mm", b, n + 1))
                    dve.wait_ge(S["q1_rec"], at("q1_rec", b, 1))
                    for t in (2 * n, 2 * n + 1):
                        dve.tensor_tensor(yk[:, t, :].rearrange("p (h d) -> p h d", h=H),
                                          w_now[:, D * (t % 2):D * (t % 2) + D].rearrange("p (h d) -> p h d", h=H),
                                          q1rec[:, H * t:H * t + H].unsqueeze(2).broadcast_to([P, H, DH]),
                                          ALU.mult).then_inc(S["y1_set"], 1)
                elif name == "out_c":
                    dve.wait_ge(S["oc_mm"], at("oc_mm", b, n + 1))
                    dve.wait_ge(S["res_c"], at("res_c", b, 1))
                    xr = x_res[:, 2 * n:2 * n + 2, :].rearrange("p t d -> p (t d)")
                    dve.tensor_tensor(xr, w_now[:, :], xr, ALU.add).then_inc(S["oc_set"], 1)

            def mask_row(b):
                dve.wait_ge(S["mrow_in"], at("mrow_in", b, 16))
                dve.tensor_scalar(mrow[:, :], mrow[:, :], -1.0, MASK_PENALTY, ALU.add, ALU.mult)\
                   .then_inc(S["mrow_shift"], 1)
                dve.wait_ge(S["mrow_shift"], at("mrow_shift", b, 1))
                dve.tensor_copy(mrow_hi[:, :], mrow[:, :]).then_inc(S["mrow_hi"], 1)
                dve.wait_ge(S["mrow_hi"], at("mrow_hi", b, 1))
                dve.tensor_tensor(mrow_lo[:, :], mrow[:, :], mrow_hi[:, :].bitcast(F32), ALU.subtract)\
                   .then_inc(S["mrow_lo"], 1)

            def mask_cols(b):
                dve.wait_ge(cols_set, 2)
                if not (isinstance(b, int) and b == 0):
                    dve.wait_ge(S["v_set"], at("v_set", b - 1, 4))
                dve.tensor_copy(mcol_now[:, :], cols[:, bass.ds(b * TT + MC, TT)]).then_inc(S["mcol"], 1)

            def maximum(b, h, t):
                g, j = h // HG, h % HG
                if j == 0 and t == 0 and not (isinstance(b, int) and G * b + g < 2):
                    dve.wait_ge(S["c_mm"], at("c_mm", b, g - 1))
                dve.wait_ge(S["m_mm"], at("m_mm", b, TT * h + t + 1))
                dve.tensor_reduce(negmax[:, g % 2, TT * j + t:TT * j + t + 1], m_ps[t % 2][:, :], AX.X,
                                  ALU.max, negate=True).then_inc(S["m_red"], 1)

            def step(b, k, first, last):
                for place in range(TT):
                    if not (last and k + LEAD >= H):
                        maximum(b + (k + LEAD) // H, (k + LEAD) % H, place)
                    for name, n, bb in pieces(k, place, b, first, last):
                        piece(name, n, bb)

            def full_step(b, k, first, last):
                if k == 0:
                    mask_cols(b)
                step(b, k, first, last)
                if k == 3 and not last:
                    mask_row(b + 1)

            def tail(b):
                for name, n in LAST_ONLY:
                    piece(name, n, b)

            mask_row(0)
            piece("zt", 0, 0)
            piece("zt", 1, 0)
            dve.wait_ge(bias_mm, 6)
            dve.tensor_copy(bias_cols[:, :], m_ps[0][:, 0:6]).then_inc(bias_set, 1)
            for n in range(4):
                piece("qk", n, 0)
                if n == 0:
                    dve.wait_ge(w_lo_set, 4)
            for w, (ps, off, wd) in enumerate(((m_ps[1], 0, D), (s_ps[0], 0, D), (y_ps[0], 0, D))):
                dve.wait_ge(bias_mm, 7 + w)
                dve.tensor_tensor(brow[:, (2, 4, 5)[w], :], ps[0:1, off:off + wd], brow[:, (2, 4, 5)[w], :], ALU.add)\
                   .then_inc(bias_set, 1)
                dve.wait_ge(bias_set, 2 + 3 * w)
                dve.tensor_copy(bias_hi[:, D * w:D * w + D], brow[:, (2, 4, 5)[w], :]).then_inc(bias_set, 1)
                dve.wait_ge(bias_set, 3 + 3 * w)
                dve.tensor_tensor(bias_lo[:, D * w:D * w + D], brow[:, (2, 4, 5)[w], :],
                                  bias_hi[:, D * w:D * w + D].bitcast(F32), ALU.subtract).then_inc(bias_set, 1)
            dve.wait_ge(cond_set, 1)
            dve.tensor_scalar(cond_h[:, :], cols[:, CD:CD + B * EC], 0.5, None, ALU.mult).then_inc(cond_set, 1)
            dve.wait_ge(cond_set, 2)
            dve.scalar_tensor_tensor(cond_s[:, :], cond_t[:, :], 1.0, cond_h[:, :], ALU.add, ALU.mult)\
               .then_inc(cond_set, 1)
            dve.wait_ge(film_mm, 1)
            dve.tensor_tensor(emb_e[:, :, :, :, :].rearrange("p l w c b -> p (l w c) b"),
                              s_ps[1][:, 0:32].rearrange("p (f b) -> p f b", b=B),
                              cols[:, EB:EB + 2 * EC].unsqueeze(2).broadcast_to([P, 2 * EC, B]),
                              ALU.add).then_inc(film_set, 1)
            dve.wait_ge(film_set, 1)
            for l in range(2):
                dve.tensor_scalar(emb_p[:, l, :, :], emb_e[:, l, 0, :, :], 1.0, 0.5, ALU.add, ALU.mult)\
                   .then_inc(film_set, 1)
                dve.wait_ge(film_set, 2 + 4 * l)
                dve.tensor_tensor(film_s[:, l, :, :], emb_p[:, l, :, :],
                                  fcols[:, l, 0, :].unsqueeze(2).broadcast_to([P, KC, B]), ALU.mult)\
                   .then_inc(film_set, 1)
                dve.tensor_tensor(emb_q[:, l, :, :], emb_p[:, l, :, :],
                                  fcols[:, l, 1, :].unsqueeze(2).broadcast_to([P, KC, B]), ALU.mult)\
                   .then_inc(film_set, 1)
                dve.wait_ge(film_set, 4 + 4 * l)
                dve.scalar_tensor_tensor(film_t[:, l, :, :], emb_e[:, l, 1, :, :], 0.5, emb_q[:, l, :, :],
                                         ALU.mult, ALU.add).then_inc(film_set, 1)
            for w in (V0, K1, Q1, V1, O0, O1):
                dve.wait_ge(w_hi_set, 2 * w + 2)
                weight_lo(w)
            dve.wait_ge(w_lo_set, 16)
            dve.wait_ge(film_set, 9)
            dve.memset(qs[ROW_MASK:ROW_MAX, :, :].bitcast(F32), 1.0).then_inc(stack_set, 1)
            dve.memset(ks[ROW_MASK:ROW_MAX, :, :].bitcast(F32), 0.0).then_inc(stack_set, 1)
            dve.memset(ks[ROW_MAX:ROWS_SHIFTED, :, :].bitcast(F32), 1.0).then_inc(stack_set, 1)
            for h in range(LEAD):
                for t in range(TT):
                    maximum(0, h, t)
                if h == HG:
                    piece("c", 0, 0)
            batches(dve, full_step, tail)

        @block.tensor
        def _(pe):
            free = [None, None]

            def split_product(dst, lhs, rhs, extra=None, stop_all=True):
                terms = [(a, c, b2) for c in range(KC) for a, b2 in ((0, 0), (0, 1), (1, 0))]
                for i, (a, c, b2) in enumerate(terms):
                    ins = pe.matmul(dst, lhs[a](c), rhs[b2](c), start=(i == 0),
                                    stop=(i == len(terms) - 1 and extra is None))
                if extra is not None:
                    for i, row in enumerate((bias_hi, bias_lo)):
                        ins = pe.matmul(dst, ones_row[:, :], row[:, extra], start=False, stop=(i == 1))
                return ins

            def weights(w, cols_of=slice(0, D)):
                return [lambda c: wh[:, w, c, cols_of], lambda c: wl[:, w, c, cols_of]]

            def tokens(hi, lo, t=None):
                s = slice(0, T) if t is None else slice(P * t, P * t + P)
                return [lambda c: hi[:, c, s], lambda c: lo[:, c, s]]

            def turn(dst, src, c, blocks_of):
                for t in range(TT):
                    ins = pe.transpose(dst[:, P * t:P * t + P], blocks_of(src, t, c), ident[:, :])
                return ins

            token_block = lambda src, t, c: src[:, t, P * c:P * c + P]
            feature_block = lambda src, t, c: src[:, c, P * t:P * t + P]

            def piece(name, n, b):
                if name in NO_PRODUCT:
                    return
                bank = BANK[name, n]
                w_now = w_ps[bank]
                if free[bank] is not None:
                    pe.wait_ge(*free[bank])

                def give(reader, b, n):
                    free[bank] = (S[reader], at(reader, b, n))

                if name == "zt":
                    if n == 0:
                        pe.wait_ge(S["z_next"], at("z_next", b, 4))
                    turn(w_now, x_in, n, token_block).then_inc(S["zt_mm"], 1)
                    give("zt_lo", b, n + 1)
                elif name == "qk":
                    mc, i = n // 2, n % 2
                    if n == 0:
                        pe.wait_ge(S["zt_hi"], at("zt_hi", b, 2))
                        pe.wait_ge(S["zt_lo"], at("zt_lo", b, 2))
                    split_product(w_now[:, :], weights((Q0, K0)[i], slice(P * mc, P * mc + P)),
                                  tokens(zt_hi, zt_lo)).then_inc(S["qk_mm"], 1)
                    give("qk_lo", b, n + 1)
                elif name == "v":
                    for t in (2 * n, 2 * n + 1):
                        ins = split_product(w_now[:, D * (t % 2):D * (t % 2) + D], tokens(zt_hi, zt_lo, t),
                                            weights(V0), extra=slice(0, D))
                    ins.then_inc(S["v_mm"], 1)
                    give("v_set", b, 2 * n + 2)
                elif name == "c":
                    pe.wait_ge(S["m_red"], at("m_red", b, 16 * n + 16))
                    pe.transpose(w_now[0:HG * TT, 0:P], negmax[:, n % 2, :], ident[:, :]).then_inc(S["c_mm"], 1)
                    give("c_lo", b, n + 1)
                elif name in ("film_a", "film_c"):
                    f = "f" + name[-1]
                    if n == 0:
                        z = "z_" + name[-1]
                        pe.wait_ge(S[z], at(z, b, 4))
                    turn(w_now, zn, n, token_block).then_inc(S[f + "_mm"], 1)
                    give(f + "_t", b, n + 1)
                elif name in ("out_a", "out_c"):
                    f, o, w = "f" + name[-1], "o" + name[-1], O0 if name == "out_a" else O1
                    if n == 0:
                        pe.wait_ge(S[f + "_hi"], at(f + "_hi", b, 2))
                        pe.wait_ge(S[f + "_lo"], at(f + "_lo", b, 2))
                    for t in (2 * n, 2 * n + 1):
                        ins = split_product(w_now[:, D * (t % 2):D * (t % 2) + D], tokens(at_hi, at_lo, t),
                                            weights(w))
                    ins.then_inc(S[o + "_mm"], 1)
                    give(o + "_set", b, n + 1)
                elif name == "z1t":
                    if n == 0:
                        pe.wait_ge(S["z_b"], at("z_b", b, 4))
                    turn(w_now, zn, n, token_block).then_inc(S["z1_mm"], 1)
                    give("z1_lo", b, n + 1)
                elif name == "k1":
                    if n == 0:
                        pe.wait_ge(S["z1_hi"], at("z1_hi", b, 2))
                        pe.wait_ge(S["z1_lo"], at("z1_lo", b, 2))
                    split_product(w_now[:, :], weights(K1, slice(P * n, P * n + P)),
                                  tokens(at_hi, at_lo)).then_inc(S["k1_mm"], 1)
                    give("k1_b", b, n + 1)
                elif name == "qv":
                    both = [lambda c: wh[:, Q1:V1 + 1, c, :], lambda c: wl[:, Q1:V1 + 1, c, :]]
                    split_product(w_now[:, :], tokens(at_hi, at_lo, n),
                                  both, extra=slice(D, 3 * D)).then_inc(S["qv_mm"], 1)
                    give("q1_sub", b, n + 1)
                elif name == "k1t":
                    pe.wait_ge(S["k1_n"], at("k1_n", b, n + 1))
                    turn(w_now, k1, n, feature_block).then_inc(S["kt_mm"], 1)
                    give("kt_set", b, n + 1)
                elif name == "q1t":
                    pe.wait_ge(S["q1_exp"], at("q1_exp", b, 1))
                    turn(w_now, q1, n, token_block).then_inc(S["qt_mm"], 1)
                    give("qt_set", b, n + 1)
                elif name == "attn":
                    pe.wait_ge(S["kt_set"], at("kt_set", b, 2))
                    pe.wait_ge(S["v1_set"], at("v1_set", b, 4))
                    for c in range(KC):
                        for t in range(TT):
                            ins = pe.matmul(w_now[:, P * c:P * c + P], v1[:, t, P * c:P * c + P],
                                            yk[:, t, P * c:P * c + P], start=(t == 0), stop=(t == TT - 1))
                    ins.then_inc(S["at_mm"], 1)
                    give("at_set", b, 1)
                elif name == "y1":
                    if n == 0:
                        pe.wait_ge(S["at_set"], at("at_set", b, 1))
                        pe.wait_ge(S["qt_set"], at("qt_set", b, 2))
                    for t in (2 * n, 2 * n + 1):
                        for c in range(KC):
                            o = D * (t % 2) + P * c
                            ins = pe.matmul(w_now[:, o:o + P], q1t[:, c, P * t:P * t + P], attn[:, c, :],
                                            start=True, stop=True)
                    ins.then_inc(S["y1_mm"], 1)
                    give("y1_set", b, 2 * n + 2)
                elif name == "yt":
                    pe.wait_ge(S["y_ev"], at("y_ev", b, n + 1))
                    for t in range(TT):
                        ins = pe.transpose(w_now[:, P * t:P * t + P], yt_sb[:, P * t:P * t + P], ident[:, :])
                    ins.then_inc(S["yt_mm"], 1)
                    give("y_set", b, n + 1)

            def maxima_scores(b, h, t):
                if t == 0 and h % HG == 0:
                    pe.wait_ge(fill[h // HG], 160 * (b + 1))
                if not (isinstance(b, int) and 64 * b + TT * h + t < 2):
                    pe.wait_ge(S["m_red"], at("m_red", b, TT * h + t - 1))
                pe.matmul(m_ps[t % 2][:, :], qs[0:ROWS_SCORE, h, P * t:P * t + P],
                          ks[0:ROWS_SCORE, h, :], start=True, stop=True).then_inc(S["m_mm"], 1)

            def scores(b, k, c):
                if c == 0 and k % HG == 0:
                    g = k // HG
                    pe.wait_ge(c_in[g % 2], 32 * (2 * b + g // 2 + 1))
                if not (isinstance(b, int) and 64 * b + TT * k + c < 2):
                    pe.wait_ge(S["exp"], at("exp", b, TT * k + c - 1))
                pe.matmul(s_ps[c % 2][:, :], ks[0:ROWS_SHIFTED, k, P * c:P * c + P],
                          qs[0:ROWS_SHIFTED, k, :], start=True, stop=True).then_inc(S["s_mm"], 1)

            def products(b, k, c):
                g, j = k // HG, k % HG
                if c == 0 and j == 0 and not (isinstance(b, int) and G * b + g < 2):
                    pe.wait_ge(S["y_ev"], at("y_ev", b, g - 1))
                if k == 0:
                    pe.wait_ge(S["v_set"], at("v_set", b, c + 1))
                pe.wait_ge(S["exp"], at("exp", b, TT * k + c + 1))
                pe.matmul(y_ps[g % 2][M_HEAD * j:M_HEAD * j + M_HEAD, :], v_aug[:, c, VW * k:VW * k + M_HEAD],
                          probs[:, k % 2, c, :], start=(c == 0), stop=(c == TT - 1)).then_inc(S["pv"], 1)

            def step(b, k, first, last):
                for place in range(TT):
                    if not (last and k + LEAD >= H):
                        maxima_scores(b + (k + LEAD) // H, (k + LEAD) % H, place)
                    scores(b, k, place)
                    for name, n, bb in pieces(k, place, b, first, last):
                        piece(name, n, bb)
                    if k > 0:
                        products(b, k - 1, place)
                    elif not first:
                        products(b - 1, H - 1, place)

            def full_step(b, k, first, last):
                if k == 0:
                    free[0] = free[1] = None
                step(b, k, first, last)

            def tail(b):
                for c in range(TT):
                    products(b, H - 1, c)
                for name, n in LAST_ONLY:
                    piece(name, n, b)

            pe.wait_ge(const_set, 7)
            pe.wait_ge(ones_set, 2)
            pe.wait_ge(vec_in, 16 * 13)
            pe.transpose(w_ps[0][:, 0:56], vrows[:, :], ident[0:56, 0:56]).then_inc(cols_mm, 1)
            pe.wait_ge(hid_rows, 1)
            pe.transpose(w_ps[0][:, 56:56 + B * TT], hrows[:, :], ident[0:B * TT, 0:B * TT]).then_inc(cols_mm, 1)
            pe.wait_ge(cols_set, 2)
            piece("zt", 0, 0)
            piece("zt", 1, 0)
            pe.wait_ge(perm_set, 4)
            pe.wait_ge(w_in[1], 32)
            for n in range(6):
                i, mc = n // 2, n % 2
                o = slice(P * mc, P * mc + P)
                for c in range(KC):
                    w = wperm[:, i, c, o] if i < 2 else wraw[:, K1, c, o]
                    nb = NB0 if i < 2 else NB1
                    pe.matmul(m_ps[0][:, n:n + 1], w, cols[:, nb + c:nb + c + 1], start=(c == 0), stop=False)
                bias = bperm[:, i, o] if i < 2 else brow[:, 3, o]
                pe.matmul(m_ps[0][:, n:n + 1], bias, one1[:, :], start=False, stop=True).then_inc(bias_mm, 1)
            pe.wait_ge(w_lo_set, 4)
            for n in range(4):
                piece("qk", n, 0)
            pe.wait_ge(w_in[2], 32)
            for w, nb, ps, off in ((V0, NB0, m_ps[1], 0), (Q1, NB1, s_ps[0], 0), (V1, NB1, y_ps[0], 0)):
                for c in range(KC):
                    ins = pe.matmul(ps[0:1, off:off + D], cols[:, nb + c:nb + c + 1], wraw[:, w, c, :],
                                    start=(c == 0), stop=(c == KC - 1))
                ins.then_inc(bias_mm, 1)
            pe.wait_ge(cond_set, 3)
            pe.wait_ge(emb_in, 32)
            cond_v = cond_s[:, :].rearrange("p (b k) -> p k b", k=EC)
            for l in range(2):
                for f in range(2 * KC):
                    for c in range(EC):
                        o = (2 * KC * l + f) * B
                        ins = pe.matmul(s_ps[1][:, o:o + B], embw[:, l, c, P * f:P * f + P], cond_v[:, c, :],
                                        start=(c == 0), stop=(c == EC - 1))
            ins.then_inc(film_mm, 1)
            pe.wait_ge(film_set, 9)
            pe.wait_ge(bias_set, 10)
            for h in range(LEAD):
                for t in range(TT):
                    maxima_scores(0, h, t)
                if h == HG:
                    piece("c", 0, 0)
            pe.wait_ge(w_lo_set, 16)
            batches(pe, full_step, tail)


_NAMES = ['x', 'cond_2048', 'mask_BxS_ff1', 'mask_BxS_ik0'] + [
    'L0_cond_' + n for n in ('norm_w', 'norm_b', 'q_w', 'q_b', 'k_w', 'k_b', 'v_w', 'v_b', 'emb_w', 'emb_b',
                             'sb_norm_w', 'sb_norm_b', 'out_w', 'out_b')] + [
    'L1_cond_' + n for n in ('norm_scale', 'norm_bias', 'Wq', 'bq', 'Wk', 'bk', 'Wv', 'bv', 'film_emb_W',
                             'film_emb_b', 'film_norm_scale', 'film_norm_bias', 'film_out_W', 'film_out_b')]


def kernel(**inputs):
    import numpy as _np
    import concourse.bacc as _bacc
    from concourse import mybir as _mybir
    from concourse.bass_utils import run_bass_kernel_spmd as _run

    nc = _bacc.Bacc("TRN2", target_bir_lowering=False, num_devices=1)
    arrays, args = {}, []
    for name in _NAMES:
        a = _np.ascontiguousarray(inputs[name])
        arrays[f"in_{name}"] = a
        args.append(nc.dram_tensor(f"in_{name}", a.shape, _mybir.dt.from_np(a.dtype), kind="ExternalInput").ap())
    result = nc.dram_tensor("out_0", inputs['x'].shape, _mybir.dt.float32, kind="ExternalOutput").ap()
    film_seq_kernel(nc, *args, result)
    r = _run(nc, [arrays], core_ids=[0])
    return r.results[0]["out_0"]
```

```python
import concourse.bass as bass
from concourse import mybir
from contextlib import ExitStack

F32 = mybir.dt.float32
F32R = mybir.dt.float32r
BF16 = mybir.dt.bfloat16
I32 = mybir.dt.int32
ALU = mybir.AluOpType
ACT = mybir.ActivationFunctionType
AX = mybir.AxisListType

P = 128
LN_EPS = 1e-5
MASK_PENALTY = 1e6
HIDDEN_KEY = -1e30
RSQRT_GUESS = 1597463007.0
NEWTON_STEPS = 3

ROW_MASK = 64
ROW_MAX = 96
ROWS_SCORE = 96
ROWS_SHIFTED = 98

PLACES = {
    0: [[], [("v", 0), ("ye", 3)], [], [("v", 1), ("yt", 3)]],
    1: [[("ln_a", 0)], [("ls_a", 0), ("ln_next", 0)], [], [("ls_next", 0)]],
    2: [[], [], [("z_a", 0)], [("c", 1), ("film_a", 0), ("z_next", 0)]],
    3: [[("film_a", 1)], [("hi_a", 0), ("hi_a", 1), ("zt", 0)], [], [("zt", 1)]],
    4: [[("out_a", 0)], [("out_a", 1), ("ln_b", 0)], [("ls_b", 0)], [("ye", 0), ("qk", 0)]],
    5: [[("yt", 0)], [("qk", 1)], [("w_late", 3)], [("z_b", 0), ("w_late", 4), ("qk", 2)]],
    6: [[], [("z1t", 0), ("c", 2), ("z1t", 1)], [], []],
    7: [[("k1", 0)], [("k1", 1), ("film_rows", 0)], [("w_late", 5)], [("qk", 3), ("k1e", 0)]],
    8: [[("qv", 0), ("k1e", 1)], [("qv", 1)], [("w_late", 6), ("k1n", 0)], [("qv", 2), ("ye", 1), ("film_rows", 1)]],
    9: [[("qv", 3)], [("w_late", 7), ("yt", 1)], [], [("softmax_q", 0)]],
    10: [[("k1t", 1), ("k1t", 0)], [("c", 3)], [("q1t", 0)], [("bias_rows", 0), ("q1t", 1)]],
    11: [[("attn", 0)], [("film_turn", 0)], [], [("y1", 0)]],
    12: [[("y1", 1), ("ln_c", 0)], [("ls_c", 0)], [("bias_rows", 1)], [("ye", 2)]],
    13: [[("z_c", 0), ("yt", 2)], [("film_c", 0), ("film_c", 1)], [], [("hi_c", 0)]],
    14: [[("hi_c", 1), ("c", 0)], [], [("bias_turn", 0)], []],
    15: [[("out_c", 0)], [("out_c", 1)], [], []],
}
NEXT = ("zt", "qk", "ln_next", "ls_next", "z_next")
OWN = ("v", "c", "ye", "yt")
PREPARE = ("w_late", "film_rows", "film_turn", "bias_rows", "bias_turn")
NO_PRODUCT = ("w_late", "ye", "hi_a", "hi_c", "k1e", "k1n", "ls_a", "ls_b", "ls_c", "ls_next",
              "ln_a", "ln_b", "ln_c", "ln_next", "z_a", "z_b", "z_c", "z_next", "softmax_q")
WITH_PRODUCT = [piece for k in range(16) for place in PLACES[k] for piece in place if piece[0] not in NO_PRODUCT]
W_BANKS = 3
BANK = {piece: i % W_BANKS for some in (True, False)
        for i, piece in enumerate(piece for piece in WITH_PRODUCT if (piece[0] in PREPARE) == some)}


def film_seq_kernel(nc, x, cond_2048, mask_BxS_ff1, mask_BxS_ik0,
                    norm_w0, norm_b0, q_w0, q_b0, k_w0, k_b0, v_w0, v_b0, emb_w0, emb_b0,
                    film_w0, film_b0, out_w0, out_b0,
                    norm_w1, norm_b1, q_w1, q_b1, k_w1, k_b1, v_w1, v_b1, emb_w1, emb_b1,
                    film_w1, film_b1, out_w1, out_b1, out):
    B, T, D = x.shape
    E = cond_2048.shape[1]
    H, DH = 16, 16
    TT = T // P
    KC = D // P
    EC = E // P
    HG = 4
    G = H // HG
    PV_PLACE = 2
    M_BANKS = 5 - W_BANKS
    M_HEAD = 32
    LEAD = 6
    assert T == 512 and D == H * DH == 256 and B == 4 and 2 * D == E

    ctx = ExitStack()
    with ctx:
        def sb(name, shape, dt=F32, scope=ctx):
            return scope.enter_context(nc.sbuf_tensor(name, shape, dt))

        def sem(name):
            return ctx.enter_context(nc.semaphore(name))

        wh = sb("w_hi", [P, 8, KC, D], F32R)
        wl = sb("w_lo", [P, 8, KC, D], F32R)
        Q0, K0, V0, K1, Q1, V1, O0, O1 = range(8)
        ident = sb("ident", [P, P])
        blocks = sb("blocks", [P, P], BF16)
        ones_row = sb("ones_row", [1, P], F32R)
        cols = sb("cols", [P, 56])
        own_key = sb("own_key", [P, B * TT])
        bias_cols = sb("bias_cols", [P, 6])
        bias_hi = sb("bias_hi", [1, 3 * D], F32R)
        bias_lo = sb("bias_lo", [1, 3 * D], F32R)
        film_s = sb("film_s", [P, 2, KC, B])
        film_t = sb("film_t", [P, 2, KC, B])
        outb = sb("outb", [P, 2, D])
        film_now = sb("film_now", [P, 2, 2, KC])
        mcol_now = sb("mcol_now", [P, TT])
        own_now = sb("own_now", [P, TT])
        x_in = sb("x_in", [P, TT, D])
        mrow = sb("mrow", [1, T])
        mrow_hi = sb("mrow_hi", [1, T], F32R)
        mrow_lo = sb("mrow_lo", [1, T], F32R)
        zt_hi = sb("zt_hi", [P, KC, T], F32R)
        zt_lo = sb("zt_lo", [P, KC, T], F32R)
        qk_hi = sb("qk_hi", [P, 2, KC, T], F32R)
        qk_lo = sb("qk_lo", [P, 2, KC, T], F32R)
        v_aug = sb("v_aug", [P, TT, H * (DH + 1) + M_HEAD - DH - 1])
        probs = sb("probs", [P, 2, TT, T])
        negmax = sb("negmax", [P, 2, HG * TT])
        crow_hi = sb("crow_hi", [HG * TT, P], F32R)
        crow_lo = sb("crow_lo", [HG * TT, P], F32R)
        recip = sb("recip", [P, HG * TT])
        y0 = sb("y0", [P, TT, D])
        yt_sb = sb("yt_sb", [P, T])
        attn = sb("attn_sb", [P, KC, P])
        q1max = sb("q1max", [P, TT, H])
        q1sum = sb("q1sum", [P, TT * H])
        q1rec = sb("q1rec", [P, TT * H])
        k1max = sb("k1max", [P, KC])
        k1sum = sb("k1sum", [P, KC])
        k1rec = sb("k1rec", [P, KC])
        three_halves = sb("three_halves", [P, TT])
        ln = {n: dict(stats=sb(f"stats_{n}", [P, TT, 6]), sum=sb(f"sum_{n}", [P, TT, 2]),
                      diff=sb(f"diff_{n}", [P, TT]), nmean=sb(f"nmean_{n}", [P, TT]), shift=sb(f"shift_{n}", [P, TT]),
                      var=sb(f"var_{n}", [P, TT]), nhalf=sb(f"nhalf_{n}", [P, TT]), y=sb(f"rstd_{n}", [P, TT]),
                      t=sb(f"newton_{n}", [P, TT])) for n in ("next", "last")}

        s_ps, m_ps, y_ps, w_ps = [
            [ctx.enter_context(nc.psum_tensor(f"{name}_ps{i}", [P, T], F32)) for i in range(count)]
            for name, count in (("s", 2), ("m", M_BANKS), ("y", 1), ("w", W_BANKS))]
        BANKS = [(bank, None) for bank in w_ps] + [(bank, "m_red") for bank in m_ps] + [
            (bank, "exp") for bank in s_ps]
        M_COUNT = H * TT
        M_BANK = [i % M_BANKS for i in range(M_COUNT - 1)] + [1]
        M_AGO = [next(a for a in range(1, M_COUNT) if M_BANK[i - a] == M_BANK[i]) for i in range(M_COUNT)]
        VW = DH + 1
        v_heads = v_aug[:, :, 0:H * VW].rearrange("p t (h d) -> p t h d", d=VW)

        vec_in, bias_in, outb_in, emb_in = sem("vec_in"), sem("bias_in"), sem("outb_in"), sem("emb_in")
        wqk_in, wv_in, w_late_in, bias_late_in, norm_in = (
            sem("wqk_in"), sem("wv_in"), sem("w_late_in"), sem("bias_late_in"), sem("norm_in"))
        ident_set, const_set, ones_set = sem("ident_set"), sem("const_set"), sem("ones_set")
        cols_mm, cols_set = sem("cols_mm"), sem("cols_set")
        hid_rows, perm_set, bias_mm, bias_set = sem("hid_rows"), sem("perm_set"), sem("bias_mm"), sem("bias_set")
        cond_set, film_mm, film_set = sem("cond_set"), sem("film_mm"), sem("film_set")
        w_hi_set, w_lo_set, stack_set = sem("w_hi_set"), sem("w_lo_set"), sem("stack_set")

        PER = {}

        def batch_sem(name, per):
            s = sem(name)
            PER[name] = per
            return s

        def at(name, b, n):
            return PER[name] * b + n

        S = {name: batch_sem(name, per) for name, per in dict(
            x_in=16, mrow_in=16, mrow_shift=1, mrow_hi=1, mrow_lo=1, mcol=1, own=1, film_now=2,
            bn_next=12, newton_next=4 * NEWTON_STEPS + 1, z_next=4,
            bn_a=12, newton_a=4 * NEWTON_STEPS + 1, z_a=4,
            bn_b=12, newton_b=4 * NEWTON_STEPS + 1, z_b=4,
            bn_c=12, newton_c=4 * NEWTON_STEPS + 1, z_c=4,
            zt_mm=2, zt_hi=2, zt_lo=2, qk_mm=4, qk_hi=4, qk_lo=4, v_mm=2, v_set=4,
            m_mm=64, m_red=64, c_mm=4, c_hi=4, c_lo=4,
            s_mm=64, exp=64, pv=64, y_ev=4, yt_mm=4, y_rec=4, y_set=4,
            res_in=16, res_b=1, hide_in=16, hide_set=1,
            fa_mm=2, fa_u=2, fa_t=2, fa_h=2, fa_hi=2, fa_lo=2,
            fc_mm=2, fc_u=2, fc_t=2, fc_h=2, fc_hi=2, fc_lo=2,
            oa_mm=2, oa_set=2, res_c=1, z1_mm=2, z1_hi=2, z1_lo=2,
            k1_mm=2, k1_b=2, k1_max=2, k1_exp=2, k1_rec=2, k1_n=2,
            qv_mm=4, v1_set=4, q1_max=4, q1_sub=4, q1_exp=1, q1_sum=1, q1_rec=1,
            kt_mm=2, kt_set=2, qt_mm=2, qt_set=2, at_mm=1, at_set=1, y1_mm=2, y1_set=4,
            oc_mm=2, oc_set=2, stored=16).items()}
        c_in = [sem("c_in0"), sem("c_in1")]
        fill = [sem(f"fill{g}") for g in range(G)]

        early = ExitStack()
        wraw = sb("wraw", [P, 3, KC, D], F32, early)
        wperm = sb("wperm", [P, 2, KC, D], F32, early)
        nrows = sb("nrows", [8, P], F32, early)
        vrows = sb("vrows", [48, P], F32, early)
        hrows_i = sb("hrows_i", [B * TT, P], I32, early)
        hrows = sb("hrows", [B * TT, P], F32, early)
        brow = sb("brow", [1, 3, D], F32, early)
        bperm = sb("bperm", [1, 2, D], F32, early)
        early.close()
        qs, ks = [None] * G, [None] * G
        for g in reversed(range(G)):
            qs[g] = sb(f"q_stack{g}", [P, HG, T], F32R)
            ks[g] = sb(f"k_stack{g}", [P, HG, T], F32R)
        late = ExitStack()
        wraw_late = sb("wraw_late", [P, 5, KC, D], F32, late)
        embw = sb("embw", [P, 2, EC, 2 * D], F32, late)
        brow_late = sb("brow_late", [1, 3, D], F32, late)
        emb_rows = sb("emb_rows", [B, 2, 2 * D], F32, late)
        cond_t = sb("cond_t", [P, B * EC], F32, late)
        cond_h = sb("cond_h", [P, B * EC], F32, late)
        cond_s = sb("cond_s", [P, B * EC], F32, late)
        emb_e = sb("emb_e", [P, 2, 2, KC, B], F32, late)
        emb_p = sb("emb_p", [P, 2, KC, B], F32, late)
        emb_q = sb("emb_q", [P, 2, KC, B], F32, late)
        late.close()
        yk = sb("yk", [P, TT, D])
        zn = sb("zn", [P, TT, D])
        x_res = sb("x_res", [P, TT, D])
        film_u = (sb("film_u", [P, T]), yt_sb)
        at_hi = sb("at_hi", [P, KC, T], F32R)
        at_lo = sb("at_lo", [P, KC, T], F32R)
        q1 = sb("q1_sb", [P, TT, D])
        v1 = sb("v1_sb", [P, TT, D])
        k1 = sb("k1_sb", [P, KC, T])
        film_h = k1
        q1t = k1
        hide = sb("hide", [P, T])

        NW0, NB0, NW1, NB1, FW0, FB0, FW1, FB1 = range(0, 16, 2)
        EB = 16
        CD = EB + 2 * EC
        MC = CD + B * EC
        fcols = cols[:, FW0:FW0 + 8].rearrange("p (l w c) -> p l w c", l=2, w=2)

        def scale_col(w, c):
            n = NW0 if w in (Q0, K0, V0) else NW1
            return cols[:, n + c:n + c + 1]

        def raw(w, c):
            return wperm[:, w, c, :] if w in (Q0, K0) else wraw[:, w, c, :] if w == V0 else wraw_late[:, w - K1, c, :]

        def tiles(ap):
            return ap.rearrange("(t p) d -> p t d", p=P)

        def regroup(ap):
            return ap.rearrange("p (g h d) -> p g d h", g=G, h=HG)

        FILM_STEPS = 11

        block = ctx.enter_context(nc.Block())

        def batch_of(name, n, b, first, last):
            if name in PREPARE:
                return b if first else None
            if name in NEXT or (name == "c" and n == 0):
                return None if last else b + 1
            if name in OWN and not (name in ("ye", "yt") and n == G - 1):
                return b
            return None if first else b - 1

        def pieces(k, place, b, first, last):
            for name, n in PLACES[k][place]:
                bb = batch_of(name, n, b, first, last)
                if bb is not None:
                    yield name, n, bb

        LAST_ONLY = [(name, n) for k in range(H) for place in PLACES[k] for name, n in place
                     if name not in NEXT + OWN + PREPARE or (name in ("ye", "yt") and n == G - 1)]

        TAIL_TURN = {}
        for piece_of_tail in LAST_ONLY:
            if piece_of_tail[0] not in NO_PRODUCT:
                TAIL_TURN[piece_of_tail] = (len(TAIL_TURN) + 1) % len(BANKS)

        START_TURN = {("zt", 0): 0, ("zt", 1): 1, ("qk", 0): 2, ("qk", 1): W_BANKS + M_BANKS,
                      ("qk", 2): 0, ("qk", 3): 1}

        def turn_of(name, n, b, in_tail):
            if in_tail:
                return TAIL_TURN[name, n]
            if name in ("zt", "qk") and isinstance(b, int) and b == 0:
                return START_TURN[name, n]
            return BANK[name, n]

        def bank_of(name, n, b, in_tail):
            return None if name in NO_PRODUCT else BANKS[turn_of(name, n, b, in_tail)][0]

        def batches(eng, step, prepared, tail):
            for k in range(H):
                step(0, k, True, False)
            prepared()
            with eng.Fori(1, B - 1) as b:
                for k in range(H):
                    step(b, k, False, False)
            for k in range(H):
                step(B - 1, k, False, True)
            tail(B - 1)

        @block.sync
        def _(sp):
            def words(ap):
                return ap.bitcast(F32)

            for i, v in enumerate((norm_w0, norm_b0, norm_w1, norm_b1)):
                sp.dma_start(nrows[KC * i:KC * i + KC, :], v.rearrange("(c p) -> c p", p=P)).then_inc(norm_in, 16)
            row = 0
            for v, n in ((film_w0, KC), (film_b0, KC), (film_w1, KC), (film_b1, KC), (emb_b0, EC), (emb_b1, EC)):
                sp.dma_start(vrows[row:row + n, :], v.rearrange("(c p) -> c p", p=P)).then_inc(vec_in, 16)
                row += n
            sp.dma_start(vrows[CD - 8:CD - 8 + B * EC, :], cond_2048.rearrange("b (k p) -> (b k) p", p=P))\
              .then_inc(vec_in, 16)
            sp.dma_start(vrows[MC - 8:MC - 8 + B * TT, :], mask_BxS_ff1.rearrange("b (t p) -> (b t) p", p=P))\
              .then_inc(vec_in, 16)
            sp.dma_start(hrows_i[:, :], mask_BxS_ik0.rearrange("b (t p) -> (b t) p", p=P)).then_inc(vec_in, 16)
            sp.dma_start(wraw[:, V0, :, :], v_w0.rearrange("(c p) n -> p c n", p=P)).then_inc(wv_in, 16)
            for i, w in enumerate((k_w1, q_w1, v_w1, out_w0, out_w1)):
                sp.dma_start(wraw_late[:, i, :, :], w.rearrange("(c p) n -> p c n", p=P)).then_inc(w_late_in, 16)
            for i, w in enumerate((emb_w0, emb_w1)):
                sp.dma_start(embw[:, i, :, :], w.rearrange("(c p) n -> p c n", p=P)).then_inc(emb_in, 16)
            for i, v in enumerate((out_b0, out_b1)):
                sp.dma_start(outb[:, i, :], v.rearrange("(a n) -> a n", a=1).broadcast_to([P, D])).then_inc(outb_in, 16)

            def fill_group(b, g, at_start=False):
                mc, part = g // 2, slice(64 * (g % 2), 64 * (g % 2) + 64)
                if at_start:
                    sp.wait_ge(stack_set, 3 * g + 3)
                    sp.wait_ge(S["mrow_lo"], 1)
                for r, src in enumerate((mrow_hi, mrow_lo)):
                    sp.dma_start(words(ks[g][ROW_MASK + r:ROW_MASK + r + 1, :, :]),
                                 words(src[:, :]).unsqueeze(1).broadcast_to([1, HG, T])).then_inc(fill[g], 16)
                for stack, i, order in ((qs[g], 0, (qk_hi, qk_hi, qk_lo, qk_lo)),
                                        (ks[g], 1, (qk_hi, qk_lo, qk_hi, qk_lo))):
                    if at_start:
                        sp.wait_ge(S["qk_lo"], 2 * mc + i + 1)
                    for r, src in enumerate(order):
                        sp.dma_start(words(stack[DH * r:DH * r + DH, :, :]), words(src[part, i, mc, :]))\
                          .then_inc(fill[g], 16)

            def shift_rows(b, g):
                sp.wait_ge(S["c_lo"], at("c_lo", b, g + 1))
                for r, src in enumerate((crow_hi, crow_lo)):
                    dst = qs[g][ROW_MAX + r:ROW_MAX + r + 1, :, :]
                    sp.dma_start(words(dst).rearrange("a h (t p) -> a (h t) p", p=P), words(src[:, :]))\
                      .then_inc(c_in[g % 2], 16)

            def step(b, k, first, last):
                if k in (0, 7, 9, 13) and not (last and k > 0):
                    h = k + LEAD
                    sp.wait_ge(S["m_red"], at("m_red", b, TT * h + 1))
                    if first and k == 0:
                        sp.wait_ge(stack_set, 12)
                    fill_group(*{0: (b, 3), 7: (b + 1, 0), 9: (b + 1, 1), 13: (b + 1, 2)}[k])
                if k in (2, 6, 10):
                    shift_rows(b, (k + 2) // 4)
                if not last and k == 14:
                    shift_rows(b + 1, 0)

            for g in range(3):
                fill_group(0, g, True)
            shift_rows(0, 0)

            def tail(b):
                sp.wait_ge(S["stored"], at("stored", b + 1, 16))

            batches(sp, step, lambda: None, tail)

        def newton(pool, which, name, b):
            t = ln[which]
            s, done = S[name], 0

            def after(ins):
                nonlocal done
                done += 1
                ins.then_inc(s, 1)
                pool.wait_ge(s, at(name, b, done))

            for _ in range(NEWTON_STEPS):
                after(pool.tensor_tensor(t["t"][:, :], t["y"][:, :], t["y"][:, :], ALU.mult))
                after(pool.tensor_tensor(t["t"][:, :], t["t"][:, :], t["nhalf"][:, :], ALU.mult))
                after(pool.tensor_tensor(t["t"][:, :], t["t"][:, :], three_halves[:, :], ALU.add))
                after(pool.tensor_tensor(t["y"][:, :], t["y"][:, :], t["t"][:, :], ALU.mult))
            pool.tensor_tensor(t["shift"][:, :], t["nmean"][:, :], t["y"][:, :], ALU.mult).then_inc(s, 1)

        def newton_fused(dve, which, name, b):
            t = ln[which]
            s, done = S[name], 0

            def after(ins, count=1):
                nonlocal done
                done += count
                ins.then_inc(s, count)
                dve.wait_ge(s, at(name, b, done))

            for _ in range(NEWTON_STEPS):
                after(dve.tensor_tensor(t["t"][:, :], t["y"][:, :], t["y"][:, :], ALU.mult))
                after(dve.tensor_tensor(t["t"][:, :], t["t"][:, :], t["nhalf"][:, :], ALU.mult))
                after(dve.scalar_tensor_tensor(t["y"][:, :], t["t"][:, :], 1.5, t["y"][:, :],
                                               ALU.add, ALU.mult), 2)
            dve.tensor_tensor(t["shift"][:, :], t["nmean"][:, :], t["y"][:, :], ALU.mult).then_inc(s, 1)

        NEWTON = 4 * NEWTON_STEPS + 1
        STATS = TT + 8
        LN_OF = {"next": ("next", x_in, x_in), "a": ("last", y0, zn), "b": ("last", x_res, zn),
                 "c": ("last", yk, zn)}

        @block.gpsimd
        def _(pool):
            pool.memset(ident[:, :], 0.0).then_inc(ident_set, 1)
            pool.wait_ge(ident_set, 1)
            pool.affine_select(out=ident[:, :], in_=ident[:, :], compare_op=ALU.not_equal, fill=1.0,
                               base=0, pattern=[[-1, P]], channel_multiplier=1).then_inc(ident_set, 1)
            for i, v in enumerate((q_b0, k_b0, v_b0)):
                pool.dma_start(brow[:, i, :], v.rearrange("(a n) -> a n", a=1)).then_inc(bias_in, 16)

            def piece(name, n, b, in_tail=False):
                if name.startswith("ls_"):
                    which = name[3:]
                    pool.wait_ge(S[f"bn_{which}"], at(f"bn_{which}", b, STATS))
                    if not in_tail:
                        newton(pool, LN_OF[which][0], f"newton_{which}", b)
                if name == "z_a":
                    pool.wait_ge(S["res_in"], at("res_in", b, 16))
                    if isinstance(b, int) and b == 0:
                        pool.wait_ge(outb_in, 32)
                    pool.tensor_tensor(x_res[:, :, :], x_res[:, :, :],
                                       outb[:, 0:1, :].broadcast_to([P, TT, D]), ALU.add)\
                        .then_inc(S["res_b"], 1)
                if name == "z_b":
                    pool.wait_ge(S["z_b"], at("z_b", b, 4))
                    pool.tensor_tensor(x_res[:, :, :], x_res[:, :, :],
                                       outb[:, 1:2, :].broadcast_to([P, TT, D]), ALU.add)\
                        .then_inc(S["res_c"], 1)
                if name in ("hi_a", "hi_c") and not in_tail:
                    f = "f" + name[-1]
                    pool.wait_ge(S[f + "_hi"], at(f + "_hi", b, n + 1))
                    pool.tensor_tensor(at_lo[:, n, :], film_h[:, n, :], at_hi[:, n, :].bitcast(F32),
                                       ALU.subtract).then_inc(S[f + "_lo"], 1)

            def step(b, k, first, last):
                for place in range(4):
                    for name, n, bb in pieces(k, place, b, first, last):
                        piece(name, n, bb)

            def tail(b):
                for name, n in LAST_ONLY:
                    piece(name, n, b, True)

            def stack_rows(g):
                for i, (rows, value) in enumerate(((qs[g][ROW_MASK:ROW_MAX, :, :], 1.0),
                                                   (ks[g][ROW_MASK:ROW_MAX, :, :], 0.0),
                                                   (ks[g][ROW_MAX:ROWS_SHIFTED, :, :], 1.0))):
                    pool.memset(rows.bitcast(F32), value).then_inc(stack_set, 1)
                    pool.wait_ge(stack_set, 3 * g + i + 1)

            pool.wait_ge(ones_set, 2)
            piece("ls_next", 0, 0)
            pool.wait_ge(S["newton_next"], NEWTON)
            stack_rows(0)
            pool.memset(v_aug[:, :, :], 1.0).then_inc(const_set, 1)
            pool.memset(blocks[:, :], 1.0).then_inc(const_set, 1)
            for i, v in enumerate((k_b1, q_b1, v_b1)):
                pool.dma_start(brow_late[:, i, :], v.rearrange("(a n) -> a n", a=1)).then_inc(bias_late_in, 16)
            pool.wait_ge(const_set, 2)
            stack_rows(1)
            bview = blocks[:, :].rearrange("p (n e) -> p n e", e=DH)
            pool.affine_select(out=bview, in_=bview, compare_op=ALU.is_ge, fill=0.0,
                               base=0, pattern=[[-DH, P // DH], [0, DH]], channel_multiplier=1).then_inc(const_set, 1)
            pool.wait_ge(const_set, 3)
            pool.affine_select(out=bview, in_=bview, compare_op=ALU.is_ge, fill=0.0,
                               base=DH - 1, pattern=[[DH, P // DH], [0, DH]], channel_multiplier=-1).then_inc(const_set, 1)
            pool.wait_ge(const_set, 4)
            pool.wait_ge(w_lo_set, 6)
            pool.wait_ge(bias_set, 5)
            pool.wait_ge(cols_set, 3)
            stack_rows(2)
            stack_rows(3)
            batches(pool, step, lambda: None, tail)

        @block.scalar
        def _(act):
            act.dma_start(x_in[:, :, :], tiles(x[0])).then_inc(S["x_in"], 16)
            for i, w in enumerate((q_w0, k_w0)):
                act.dma_start(wraw[:, i, :, :], w.rearrange("(c p) n -> p c n", p=P)).then_inc(wqk_in, 16)
            act.dma_start(mrow[:, :], mask_BxS_ff1[0:1, :]).then_inc(S["mrow_in"], 16)

            def weight_hi(w):
                for c in range(KC):
                    if w in (O0, O1):
                        act.activation(wh[:, w, c, :], raw(w, c), ACT.Copy).then_inc(w_hi_set, 1)
                    else:
                        act.activation(wh[:, w, c, :], raw(w, c), ACT.Copy, scale=scale_col(w, c)).then_inc(w_hi_set, 1)

            def piece(name, n, b, in_tail=False):
                w_now = bank_of(name, n, b, in_tail)
                if name == "zt":
                    if n == 0 and not (isinstance(b, int) and b == 0):
                        act.wait_ge(S["v_mm"], at("v_mm", b - 1, 2))
                    act.wait_ge(S["zt_mm"], at("zt_mm", b, n + 1))
                    act.activation(zt_hi[:, n, :], w_now[:, :], ACT.Copy).then_inc(S["zt_hi"], 1)
                elif name == "qk":
                    mc, i = n // 2, n % 2
                    if i == 0 and not (isinstance(b, int) and b == 0):
                        act.wait_ge(fill[2 * mc], 160 * b)
                        act.wait_ge(fill[2 * mc + 1], 160 * b)
                    act.wait_ge(S["qk_mm"], at("qk_mm", b, n + 1))
                    act.activation(qk_hi[:, i, mc, :], w_now[:, :], ACT.Identity,
                                   bias=bias_cols[:, 2 * i + mc:2 * i + mc + 1]).then_inc(S["qk_hi"], 1)
                elif name == "v":
                    act.wait_ge(S["v_mm"], at("v_mm", b, n + 1))
                    if n == 0:
                        act.wait_ge(S["mcol"], at("mcol", b, 1))
                    for t in (2 * n, 2 * n + 1):
                        if not (isinstance(b, int) and b == 0):
                            act.wait_ge(S["pv"], at("pv", b - 1, HG * (H - TT + t + 1)))
                        act.activation(v_heads[:, t, :, 0:DH],
                                       w_now[:, D * (t % 2):D * (t % 2) + D].rearrange("p (h d) -> p h d", h=H),
                                       ACT.Copy, scale=mcol_now[:, t:t + 1]).then_inc(S["v_set"], 1)
                elif name in ("film_a", "film_c"):
                    f, layer = "f" + name[-1], 0 if name == "film_a" else 1
                    act.wait_ge(S[f + "_mm"], at(f + "_mm", b, n + 1))
                    if n == 0 and layer == 0:
                        act.wait_ge(S["film_now"], at("film_now", b, 2))
                    for which, func, dst in (("_u", ACT.Identity, film_u[n][:, :]), ("_t", ACT.Tanh, film_h[:, n, :])):
                        act.activation(dst, w_now[:, :], func, scale=film_now[:, layer, 0, n:n + 1],
                                       bias=film_now[:, layer, 1, n:n + 1]).then_inc(S[f + which], 1)
                elif name in ("hi_a", "hi_c"):
                    f = "f" + name[-1]
                    act.wait_ge(S[f + "_h"], at(f + "_h", b, n + 1))
                    act.activation(at_hi[:, n, :], film_h[:, n, :], ACT.Copy).then_inc(S[f + "_hi"], 1)
                elif name == "z1t":
                    act.wait_ge(S["z1_mm"], at("z1_mm", b, n + 1))
                    act.activation(at_hi[:, n, :], w_now[:, :], ACT.Copy).then_inc(S["z1_hi"], 1)
                elif name == "w_late":
                    act.wait_ge(w_late_in, 80)
                    weight_hi(n)
                elif name == "k1e":
                    act.wait_ge(S["k1_max"], at("k1_max", b, n + 1))
                    act.activation(k1[:, n, :], k1[:, n, :], ACT.Exp, bias=k1max[:, n:n + 1],
                                   accum_out=k1sum[:, n:n + 1]).then_inc(S["k1_exp"], 1)
                elif name == "qv":
                    act.wait_ge(S["qv_mm"], at("qv_mm", b, n + 1))
                    if n == 0:
                        act.wait_ge(S["own"], at("own", b, 1))
                    act.activation(v1[:, n, :], w_now[:, D:2 * D], ACT.Copy, scale=own_now[:, n:n + 1])\
                        .then_inc(S["v1_set"], 1)
                elif name == "softmax_q":
                    act.wait_ge(S["q1_sub"], at("q1_sub", b, 4))
                    act.activation(q1[:, :, :], q1[:, :, :], ACT.Exp).then_inc(S["q1_exp"], 1)
                elif name in ("z_a", "z_b", "z_c", "z_next"):
                    which = name[2:]
                    scratch, src, dst = LN_OF[which]
                    t = ln[scratch]
                    act.wait_ge(S[f"newton_{which}"], at(f"newton_{which}", b, NEWTON))
                    for i in range(TT):
                        act.activation(dst[:, i, :], src[:, i, :], ACT.Identity, scale=t["y"][:, i:i + 1],
                                       bias=t["shift"][:, i:i + 1]).then_inc(S[f"z_{which}"], 1)
                elif name == "k1n":
                    for c in range(KC):
                        act.wait_ge(S["k1_rec"], at("k1_rec", b, c + 1))
                        act.activation(k1[:, c, :], k1[:, c, :], ACT.Copy, scale=k1rec[:, c:c + 1])\
                           .then_inc(S["k1_n"], 1)
                elif name == "k1t":
                    act.wait_ge(S["kt_mm"], at("kt_mm", b, n + 1))
                    act.activation(yk[:, :, P * n:P * n + P], w_now[:, :].rearrange("p (t f) -> p t f", t=TT),
                                   ACT.Copy).then_inc(S["kt_set"], 1)
                elif name == "ye":
                    act.wait_ge(S["pv"], at("pv", b, TT * HG * (n + 1)))
                    if not (isinstance(b, int) and b == 0 and n == 0):
                        act.wait_ge(S["yt_mm"], at("yt_mm", b, n))
                    act.activation(yt_sb[:, :], y_ps[0][:, :], ACT.Copy).then_inc(S["y_ev"], 1)
                elif name == "q1t":
                    act.wait_ge(S["qt_mm"], at("qt_mm", b, n + 1))
                    act.activation(q1t[:, n, :], w_now[:, :], ACT.Copy).then_inc(S["qt_set"], 1)

            def load_batch(b):
                if not isinstance(b, int) or b > 0:
                    act.wait_ge(S["zt_mm"], at("zt_mm", b - 1, 2))
                act.dma_start(x_in[:, :, :], tiles(x[b])).then_inc(S["x_in"], 16)

            def load_mask(b):
                if not isinstance(b, int) or b > 0:
                    act.wait_ge(fill[G - 1], 160 * b)
                act.dma_start(mrow[:, :], mask_BxS_ff1[bass.ds(b, 1), :]).then_inc(S["mrow_in"], 16)

            def load_last(b):
                act.wait_ge(S["stored"], at("stored", b, 16))
                act.dma_start(x_res[:, :, :], tiles(x[b])).then_inc(S["res_in"], 16)
                act.dma_start(hide[:, :].bitcast(I32), mask_BxS_ik0[bass.ds(b, 1), :].broadcast_to([P, T]))\
                   .then_inc(S["hide_in"], 16)

            def store(b):
                act.wait_ge(S["oc_set"], at("oc_set", b, 2))
                act.dma_start(tiles(out[b]), x_res[:, :, :]).then_inc(S["stored"], 16)

            def exponentials(b, k, j):
                act.wait_ge(S["s_mm"], at("s_mm", b, HG * k + j + 1))
                if not (isinstance(b, int) and H * b + k < 2):
                    act.wait_ge(S["pv"], at("pv", b, HG * (k - 2) + j + 1))
                act.activation(probs[:, k % 2, j, :], s_ps[j % 2][:, :], ACT.Exp).then_inc(S["exp"], 1)

            def step(b, k, first, last):
                if k == 0:
                    if not last:
                        load_batch(b + 1)
                if k == 1 and not first:
                    load_last(b - 1)
                if k == 2 and not last:
                    load_mask(b + 1)
                for place in range(4):
                    exponentials(b, k, place)
                    for name, n, bb in pieces(k, place, b, first, last):
                        piece(name, n, bb)
                if k == H - 1 and not first:
                    store(b - 1)

            def tail(b):
                for name, n in LAST_ONLY:
                    piece(name, n, b, True)
                    if name == "ye":
                        load_last(b)
                store(b)

            act.wait_ge(cols_set, 1)
            for w in (Q0, K0):
                act.wait_ge(perm_set, w + 1)
                weight_hi(w)
            piece("z_next", 0, 0)
            piece("zt", 0, 0)
            piece("zt", 1, 0)
            act.wait_ge(bias_set, 2)
            for n in range(4):
                piece("qk", n, 0)
            act.wait_ge(wv_in, 16)
            weight_hi(V0)
            act.wait_ge(cols_set, 2)
            act.activation(cond_t[:, :], cols[:, CD:CD + B * EC], ACT.Tanh, scale=0.5).then_inc(cond_set, 1)

            def prepared():
                act.wait_ge(w_lo_set, 16)
                act.wait_ge(film_set, FILM_STEPS)
                act.wait_ge(bias_set, 10)
                act.sem_inc(S["stored"], 16)

            batches(act, step, prepared, tail)

        @block.vector
        def _(dve):
            def statistics(which, b, part, wait=None):
                scratch, src, _ = LN_OF[which]
                t = ln[scratch]
                s, name, done = S[f"bn_{which}"], f"bn_{which}", 0 if part == 0 else TT

                def then(ins):
                    nonlocal done
                    done += 1
                    ins.then_inc(s, 1)

                def settled():
                    dve.wait_ge(s, at(name, b, done))

                if part == 0:
                    for i in range(TT):
                        wait(i)
                        then(dve.bn_stats(t["stats"][:, i, :], src[:, i, :]))
                    return
                settled()
                even, odd = t["stats"][:, :, 1:3], t["stats"][:, :, 4:6]
                then(dve.tensor_tensor(t["sum"][:, :, :], even, odd, ALU.add))
                then(dve.tensor_tensor(t["diff"][:, :], even[:, :, 0], odd[:, :, 0], ALU.subtract))
                settled()
                then(dve.tensor_scalar(t["nmean"][:, :], t["sum"][:, :, 0], -0.5, None, ALU.mult))
                then(dve.tensor_scalar(t["var"][:, :], t["sum"][:, :, 1], 1.0 / D, LN_EPS, ALU.mult, ALU.add))
                then(dve.scalar_tensor_tensor(t["diff"][:, :], t["diff"][:, :], 0.25, t["diff"][:, :],
                                              ALU.mult, ALU.mult))
                settled()
                then(dve.tensor_tensor(t["var"][:, :], t["var"][:, :], t["diff"][:, :], ALU.add))
                settled()
                then(dve.tensor_scalar(t["nhalf"][:, :], t["var"][:, :], -0.5, None, ALU.mult))
                then(dve.tensor_scalar(t["y"][:, :].bitcast(I32), t["var"][:, :].bitcast(I32), -0.5,
                                       RSQRT_GUESS, ALU.mult, ALU.add))

            dve.memset(three_halves[:, :], 1.5).then_inc(ones_set, 1)
            dve.memset(ones_row[:, :].bitcast(F32), 1.0).then_inc(ones_set, 1)
            statistics("next", 0, 0, lambda i: dve.wait_ge(S["x_in"], 16))
            statistics("next", 0, 1)
            dve.wait_ge(cols_mm, 1)
            dve.tensor_copy(cols[:, 0:8], y_ps[0][:, 0:8]).then_inc(cols_set, 1)
            dve.wait_ge(wqk_in, 32)
            for w in (Q0, K0):
                dve.tensor_copy(wperm[:, w, :, :].rearrange("p c (g d h) -> p (c g) d h", g=G, d=DH),
                                wraw[:, w, :, :].rearrange("p c (g h d) -> p (c g) d h", g=G, h=HG))\
                   .then_inc(perm_set, 1)
            dve.wait_ge(bias_in, 16 * 3)
            for i in range(2):
                dve.tensor_copy(bperm[:, i, :].rearrange("p (g d h) -> p g d h", g=G, d=DH),
                                regroup(brow[:, i, :])).then_inc(perm_set, 1)

            def weight_lo(w):
                dve.wait_ge(w_hi_set, 2 * w + 2)
                for c in range(KC):
                    if w in (O0, O1):
                        dve.tensor_tensor(wl[:, w, c, :], raw(w, c), wh[:, w, c, :].bitcast(F32), ALU.subtract)\
                           .then_inc(w_lo_set, 1)
                    else:
                        dve.scalar_tensor_tensor(wl[:, w, c, :], raw(w, c), scale_col(w, c),
                                                 wh[:, w, c, :].bitcast(F32), ALU.mult, ALU.subtract)\
                           .then_inc(w_lo_set, 1)

            def split_bias(dst, rows, ps, done):
                dve.tensor_tensor(rows, ps, rows, ALU.add).then_inc(bias_set, 1)
                dve.wait_ge(bias_set, done + 1)
                dve.tensor_copy(bias_hi[:, dst], rows).then_inc(bias_set, 1)
                dve.wait_ge(bias_set, done + 2)
                dve.tensor_tensor(bias_lo[:, dst], rows, bias_hi[:, dst].bitcast(F32), ALU.subtract)\
                   .then_inc(bias_set, 1)

            weight_lo(Q0)
            weight_lo(K0)

            def piece(name, n, b, in_tail=False):
                w_now = bank_of(name, n, b, in_tail)
                if name.startswith("ln_"):
                    which = name[3:]
                    ready = {"next": lambda i: dve.wait_ge(S["x_in"], at("x_in", b, 16)),
                             "a": lambda i: dve.wait_ge(S["y_set"], at("y_set", b, G)),
                             "b": lambda i: dve.wait_ge(S["oa_set"], at("oa_set", b, i // 2 + 1)),
                             "c": lambda i: dve.wait_ge(S["y1_set"], at("y1_set", b, i + 1))}[which]
                    statistics(which, b, 0, ready)
                elif name.startswith("ls_"):
                    which = name[3:]
                    statistics(which, b, 1)
                    if in_tail:
                        dve.wait_ge(S[f"bn_{which}"], at(f"bn_{which}", b, STATS))
                        newton_fused(dve, LN_OF[which][0], f"newton_{which}", b)
                elif name in ("z_a", "z_b"):
                    if name == "z_a":
                        for i, of_all in enumerate((film_s, film_t)):
                            dve.tensor_copy(film_now[:, :, i, :].unsqueeze(3), of_all[:, :, :, bass.ds(b, 1)])\
                               .then_inc(S["film_now"], 1)
                        dve.tensor_copy(own_now[:, :], own_key[:, bass.ds(b * TT, TT)]).then_inc(S["own"], 1)
                    else:
                        dve.wait_ge(S["hide_in"], at("hide_in", b, 16))
                        dve.tensor_scalar(hide[:, :], hide[:, :].bitcast(I32), 1.0, HIDDEN_KEY, ALU.is_equal, ALU.mult)\
                           .then_inc(S["hide_set"], 1)
                elif name == "zt":
                    dve.wait_ge(S["zt_hi"], at("zt_hi", b, n + 1))
                    dve.tensor_tensor(zt_lo[:, n, :], w_now[:, :], zt_hi[:, n, :].bitcast(F32), ALU.subtract)\
                       .then_inc(S["zt_lo"], 1)
                elif name == "qk":
                    mc, i = n // 2, n % 2
                    dve.wait_ge(S["qk_hi"], at("qk_hi", b, n + 1))
                    dve.scalar_tensor_tensor(qk_lo[:, i, mc, :], w_now[:, :],
                                             bias_cols[:, 2 * i + mc:2 * i + mc + 1],
                                             qk_hi[:, i, mc, :].bitcast(F32), ALU.add, ALU.subtract)\
                       .then_inc(S["qk_lo"], 1)
                elif name == "c":
                    dve.wait_ge(S["c_mm"], at("c_mm", b, n + 1))
                    if not (isinstance(b, int) and b == 0 and n == 0):
                        prev = 2 * b + (n - 1) // 2 + 1
                        dve.wait_ge(c_in[(n - 1) % 2], 32 * prev)
                    dve.tensor_copy(crow_hi[:, :], w_now[0:HG * TT, 0:P]).then_inc(S["c_hi"], 1)
                    dve.wait_ge(S["c_hi"], at("c_hi", b, n + 1))
                    dve.tensor_tensor(crow_lo[:, :], w_now[0:HG * TT, 0:P], crow_hi[:, :].bitcast(F32),
                                      ALU.subtract).then_inc(S["c_lo"], 1)
                elif name == "yt":
                    dve.wait_ge(S["yt_mm"], at("yt_mm", b, n + 1))
                    heads = w_now[:, :].rearrange("p (t h d) -> p t h d", h=HG, d=M_HEAD)
                    dve.reciprocal(recip[:, :].rearrange("p (t h) -> p t h", h=HG), heads[:, :, :, DH])\
                       .then_inc(S["y_rec"], 1)
                    dve.wait_ge(S["y_rec"], at("y_rec", b, n + 1))
                    dst = y0[:, :, HG * DH * n:HG * DH * (n + 1)].rearrange("p t (h d) -> p t h d", h=HG)
                    dve.tensor_tensor(dst, heads[:, :, :, 0:DH],
                                      recip[:, :].rearrange("p (t h) -> p t h", h=HG).unsqueeze(3)
                                      .broadcast_to([P, TT, HG, DH]), ALU.mult).then_inc(S["y_set"], 1)
                elif name in ("film_a", "film_c"):
                    f = "f" + name[-1]
                    dve.wait_ge(S[f + "_t"], at(f + "_t", b, n + 1))
                    dve.scalar_tensor_tensor(film_h[:, n, :], film_h[:, n, :], 1.0, film_u[n][:, :],
                                             ALU.add, ALU.mult).then_inc(S[f + "_h"], 1)
                elif name in ("hi_a", "hi_c") and in_tail:
                    f = "f" + name[-1]
                    dve.wait_ge(S[f + "_hi"], at(f + "_hi", b, n + 1))
                    dve.tensor_tensor(at_lo[:, n, :], film_h[:, n, :], at_hi[:, n, :].bitcast(F32),
                                      ALU.subtract).then_inc(S[f + "_lo"], 1)
                elif name == "out_a":
                    dve.wait_ge(S["oa_mm"], at("oa_mm", b, n + 1))
                    dve.wait_ge(S["res_b"], at("res_b", b, 1))
                    xr = x_res[:, 2 * n:2 * n + 2, :].rearrange("p t d -> p (t d)")
                    dve.tensor_tensor(xr, w_now[:, :], xr, ALU.add).then_inc(S["oa_set"], 1)
                elif name == "z1t":
                    dve.wait_ge(S["z1_hi"], at("z1_hi", b, n + 1))
                    dve.tensor_tensor(at_lo[:, n, :], w_now[:, :], at_hi[:, n, :].bitcast(F32), ALU.subtract)\
                       .then_inc(S["z1_lo"], 1)
                elif name == "k1":
                    dve.wait_ge(S["k1_mm"], at("k1_mm", b, n + 1))
                    dve.wait_ge(S["hide_set"], at("hide_set", b, 1))
                    dve.scalar_tensor_tensor(k1[:, n, :], w_now[:, :], bias_cols[:, 4 + n:5 + n], hide[:, :],
                                             ALU.add, ALU.add).then_inc(S["k1_b"], 1)
                    dve.wait_ge(S["k1_b"], at("k1_b", b, n + 1))
                    dve.tensor_reduce(k1max[:, n:n + 1], k1[:, n, :], AX.X, ALU.max, negate=True)\
                       .then_inc(S["k1_max"], 1)
                elif name == "qv":
                    dve.wait_ge(S["v1_set"], at("v1_set", b, n + 1))
                    qv = w_now[:, 0:D].rearrange("p (h d) -> p h d", h=H)
                    dve.tensor_reduce(q1max[:, n, :], qv, AX.X, ALU.max).then_inc(S["q1_max"], 1)
                    dve.wait_ge(S["q1_max"], at("q1_max", b, n + 1))
                    dve.tensor_tensor(q1[:, n, :].rearrange("p (h d) -> p h d", h=H), qv,
                                      q1max[:, n, :].unsqueeze(2).broadcast_to([P, H, DH]), ALU.subtract)\
                       .then_inc(S["q1_sub"], 1)
                elif name == "w_late":
                    weight_lo(n)
                elif name == "film_rows":
                    dve.wait_ge(film_mm, n + 1)
                    dve.tensor_copy(emb_rows[:, n, :], w_now[0:B, :]).then_inc(film_set, 1)
                elif name == "film_turn":
                    dve.wait_ge(film_mm, 3)
                    dve.tensor_tensor(emb_e[:, :, :, :, :].rearrange("p l w c b -> p (l w c) b"),
                                      w_now[:, 0:32].rearrange("p (f b) -> p f b", b=B),
                                      cols[:, EB:EB + 2 * EC].unsqueeze(2).broadcast_to([P, 2 * EC, B]),
                                      ALU.add).then_inc(film_set, 1)
                    dve.wait_ge(film_set, 3)
                    for l in range(2):
                        dve.tensor_scalar(emb_p[:, l, :, :], emb_e[:, l, 0, :, :], 1.0, 0.5, ALU.add, ALU.mult)\
                           .then_inc(film_set, 1)
                        dve.wait_ge(film_set, 4 + 4 * l)
                        dve.tensor_tensor(film_s[:, l, :, :], emb_p[:, l, :, :],
                                          fcols[:, l, 0, :].unsqueeze(2).broadcast_to([P, KC, B]), ALU.mult)\
                           .then_inc(film_set, 1)
                        dve.tensor_tensor(emb_q[:, l, :, :], emb_p[:, l, :, :],
                                          fcols[:, l, 1, :].unsqueeze(2).broadcast_to([P, KC, B]), ALU.mult)\
                           .then_inc(film_set, 1)
                        dve.wait_ge(film_set, 6 + 4 * l)
                        dve.scalar_tensor_tensor(film_t[:, l, :, :], emb_e[:, l, 1, :, :], 0.5, emb_q[:, l, :, :],
                                                 ALU.mult, ALU.add).then_inc(film_set, 1)
                elif name == "bias_rows":
                    dve.wait_ge(bias_late_in, 16 * 3)
                    dve.wait_ge(bias_mm, 4 + n)
                    if n == 0:
                        dve.tensor_tensor(brow_late[:, 0, :], w_now[0:1, 0:D], brow_late[:, 0, :], ALU.add)\
                           .then_inc(bias_set, 1)
                    else:
                        split_bias(slice(D, 3 * D), brow_late[:, 1:3, :].rearrange("a w d -> a (w d)"), w_now[0:1, :], 6)
                elif name == "bias_turn":
                    dve.wait_ge(bias_mm, 6)
                    dve.tensor_copy(bias_cols[:, 4:6], w_now[:, 0:2]).then_inc(bias_set, 1)
                elif name == "k1n":
                    for c in range(KC):
                        dve.wait_ge(S["k1_exp"], at("k1_exp", b, c + 1))
                        dve.reciprocal(k1rec[:, c:c + 1], k1sum[:, c:c + 1]).then_inc(S["k1_rec"], 1)
                elif name == "softmax_q":
                    dve.wait_ge(S["q1_exp"], at("q1_exp", b, 1))
                    dve.tensor_reduce(q1sum[:, :], q1[:, :, :].rearrange("p t (h d) -> p (t h) d", h=H),
                                      AX.X, ALU.add).then_inc(S["q1_sum"], 1)
                    dve.wait_ge(S["q1_sum"], at("q1_sum", b, 1))
                    dve.reciprocal(q1rec[:, :], q1sum[:, :]).then_inc(S["q1_rec"], 1)
                elif name == "attn":
                    dve.wait_ge(S["at_mm"], at("at_mm", b, 1))
                    dve.tensor_tensor(attn[:, :, :], w_now[:, 0:KC * P].rearrange("p (c e) -> p c e", c=KC),
                                      blocks[:, :].unsqueeze(1).broadcast_to([P, KC, P]), ALU.mult)\
                       .then_inc(S["at_set"], 1)
                elif name == "y1":
                    dve.wait_ge(S["y1_mm"], at("y1_mm", b, n + 1))
                    dve.wait_ge(S["q1_rec"], at("q1_rec", b, 1))
                    for t in (2 * n, 2 * n + 1):
                        dve.tensor_tensor(yk[:, t, :].rearrange("p (h d) -> p h d", h=H),
                                          w_now[:, D * (t % 2):D * (t % 2) + D].rearrange("p (h d) -> p h d", h=H),
                                          q1rec[:, H * t:H * t + H].unsqueeze(2).broadcast_to([P, H, DH]),
                                          ALU.mult).then_inc(S["y1_set"], 1)
                elif name == "out_c":
                    dve.wait_ge(S["oc_mm"], at("oc_mm", b, n + 1))
                    dve.wait_ge(S["res_c"], at("res_c", b, 1))
                    xr = x_res[:, 2 * n:2 * n + 2, :].rearrange("p t d -> p (t d)")
                    dve.tensor_tensor(xr, w_now[:, :], xr, ALU.add).then_inc(S["oc_set"], 1)

            def mask_row(b):
                dve.wait_ge(S["mrow_in"], at("mrow_in", b, 16))
                dve.tensor_scalar(mrow[:, :], mrow[:, :], -1.0, MASK_PENALTY, ALU.add, ALU.mult)\
                   .then_inc(S["mrow_shift"], 1)
                dve.wait_ge(S["mrow_shift"], at("mrow_shift", b, 1))
                dve.tensor_copy(mrow_hi[:, :], mrow[:, :]).then_inc(S["mrow_hi"], 1)
                dve.wait_ge(S["mrow_hi"], at("mrow_hi", b, 1))
                dve.tensor_tensor(mrow_lo[:, :], mrow[:, :], mrow_hi[:, :].bitcast(F32), ALU.subtract)\
                   .then_inc(S["mrow_lo"], 1)

            def mask_cols(b):
                dve.wait_ge(cols_set, 3)
                if not (isinstance(b, int) and b == 0):
                    dve.wait_ge(S["v_set"], at("v_set", b - 1, 4))
                dve.tensor_copy(mcol_now[:, :], cols[:, bass.ds(b * TT + MC, TT)]).then_inc(S["mcol"], 1)

            def maximum(b, h, t):
                g, j = h // HG, h % HG
                if j == 0 and t == 0 and not (isinstance(b, int) and G * b + g < 2):
                    dve.wait_ge(S["c_mm"], at("c_mm", b, g - 1))
                dve.wait_ge(S["m_mm"], at("m_mm", b, TT * h + t + 1))
                dve.tensor_reduce(negmax[:, g % 2, TT * j + t:TT * j + t + 1], m_ps[M_BANK[TT * h + t]][:, :], AX.X,
                                  ALU.max, negate=True).then_inc(S["m_red"], 1)

            def step(b, k, first, last):
                for place in range(TT):
                    if not (last and k + LEAD >= H):
                        maximum(b + (k + LEAD) // H, (k + LEAD) % H, place)
                    before = (k, place - 1) if place > 0 else (k - 1, TT - 1)
                    if before[0] >= 0:
                        for name, n, bb in pieces(*before, b, first, last):
                            piece(name, n, bb)

            def full_step(b, k, first, last):
                if k == 0:
                    mask_cols(b)
                step(b, k, first, last)
                if k == 3 and not last:
                    mask_row(b + 1)

            def tail(b):
                for name, n in LAST_ONLY:
                    piece(name, n, b, True)

            mask_row(0)
            dve.wait_ge(bias_mm, 1)
            dve.wait_ge(perm_set, 4)
            bp = bperm[:, :, :].rearrange("a w d -> a (w d)")
            dve.tensor_tensor(bp, m_ps[0][0:1, :], bp, ALU.add).then_inc(bias_set, 1)
            piece("zt", 0, 0)
            piece("zt", 1, 0)
            dve.wait_ge(bias_mm, 2)
            dve.tensor_copy(bias_cols[:, 0:4], m_ps[1][:, 0:4]).then_inc(bias_set, 1)
            for n in range(4):
                piece("qk", n, 0)
            dve.wait_ge(vec_in, 16 * 9)
            dve.tensor_scalar(hrows[:, :], hrows_i[:, :], 1.0, None, ALU.is_equal).then_inc(hid_rows, 1)
            dve.wait_ge(bias_mm, 3)
            split_bias(slice(0, D), brow[:, 2, :], m_ps[0][0:1, 0:D], 2)
            weight_lo(V0)
            dve.wait_ge(cols_mm, 3)
            dve.tensor_copy(cols[:, 8:56], y_ps[0][:, 8:56]).then_inc(cols_set, 1)
            dve.tensor_scalar(own_key[:, :], y_ps[0][:, 56:56 + B * TT], -1.0, 1.0, ALU.mult, ALU.add)\
               .then_inc(cols_set, 1)
            dve.wait_ge(cond_set, 1)
            dve.tensor_scalar(cond_h[:, :], cols[:, CD:CD + B * EC], 0.5, None, ALU.mult).then_inc(cond_set, 1)
            dve.wait_ge(cond_set, 2)
            dve.scalar_tensor_tensor(cond_s[:, :], cond_t[:, :], 1.0, cond_h[:, :], ALU.add, ALU.mult)\
               .then_inc(cond_set, 1)
            for h in range(LEAD):
                for t in range(TT):
                    maximum(0, h, t)
                if h == HG:
                    piece("c", 0, 0)
            def prepared():
                dve.wait_ge(bias_mm, 6)
                dve.wait_ge(film_mm, 3)

            batches(dve, full_step, prepared, tail)

        @block.tensor
        def _(pe):
            free = [None] * len(BANKS)

            def split_product(dst, lhs, rhs, bias=None):
                terms = [(a, c, b2) for c in range(KC) for a, b2 in ((0, 0), (0, 1), (1, 0))]
                for i, (a, c, b2) in enumerate(terms):
                    ins = pe.matmul(dst, lhs[a](c), rhs[b2](c), start=(i == 0),
                                    stop=(i == len(terms) - 1 and bias is None))
                if bias is not None:
                    for i, row in enumerate((bias_hi, bias_lo)):
                        ins = pe.matmul(dst, ones_row[:, :], row[:, bias], start=False, stop=(i == 1))
                return ins

            def shift_product(dst, nb, w_of):
                for c in range(KC):
                    ins = pe.matmul(dst, cols[:, nb + c:nb + c + 1], w_of(c), start=(c == 0), stop=(c == KC - 1))
                ins.then_inc(bias_mm, 1)

            def weights(w, cols_of=slice(0, D)):
                return [lambda c: wh[:, w, c, cols_of], lambda c: wl[:, w, c, cols_of]]

            def tokens(hi, lo, t=None):
                s = slice(0, T) if t is None else slice(P * t, P * t + P)
                return [lambda c: hi[:, c, s], lambda c: lo[:, c, s]]

            def turn(dst, src, c, blocks_of, arrived=None):
                for t in range(TT):
                    if arrived is not None:
                        pe.wait_ge(*arrived(t))
                    ins = pe.transpose(dst[:, P * t:P * t + P], blocks_of(src, t, c), ident[:, :])
                return ins

            token_block = lambda src, t, c: src[:, t, P * c:P * c + P]
            feature_block = lambda src, t, c: src[:, c, P * t:P * t + P]

            def piece(name, n, b, in_tail=False):
                if name in NO_PRODUCT:
                    return
                bank = turn_of(name, n, b, in_tail)
                w_now = bank_of(name, n, b, in_tail)
                if free[bank] is not None:
                    pe.wait_ge(*free[bank])

                def give(reader, b, n):
                    free[bank] = (S[reader], at(reader, b, n))

                if name == "zt":
                    turn(w_now, x_in, n, token_block,
                         (lambda t: (S["z_next"], at("z_next", b, t + 1))) if n == 0 else None)\
                        .then_inc(S["zt_mm"], 1)
                    give("zt_lo", b, n + 1)
                elif name == "qk":
                    mc, i = n // 2, n % 2
                    if n == 0:
                        pe.wait_ge(S["zt_hi"], at("zt_hi", b, 2))
                        pe.wait_ge(S["zt_lo"], at("zt_lo", b, 2))
                    split_product(w_now[:, :], weights((Q0, K0)[i], slice(P * mc, P * mc + P)),
                                  tokens(zt_hi, zt_lo)).then_inc(S["qk_mm"], 1)
                    give("qk_lo", b, n + 1)
                elif name == "v":
                    if isinstance(b, int) and b == 0:
                        pe.wait_ge(w_lo_set, 6)
                        pe.wait_ge(bias_set, 5)
                    for t in (2 * n, 2 * n + 1):
                        ins = split_product(w_now[:, D * (t % 2):D * (t % 2) + D], tokens(zt_hi, zt_lo, t),
                                            weights(V0), bias=slice(0, D))
                    ins.then_inc(S["v_mm"], 1)
                    give("v_set", b, 2 * n + 2)
                elif name == "c":
                    pe.wait_ge(S["m_red"], at("m_red", b, 16 * n + 16))
                    pe.transpose(w_now[0:HG * TT, 0:P], negmax[:, n % 2, :], ident[:, :]).then_inc(S["c_mm"], 1)
                    give("c_lo", b, n + 1)
                elif name in ("film_a", "film_c"):
                    f = "f" + name[-1]
                    z = "z_" + name[-1]
                    turn(w_now, zn, n, token_block, (lambda t: (S[z], at(z, b, t + 1))) if n == 0 else None)\
                        .then_inc(S[f + "_mm"], 1)
                    give(f + "_t", b, n + 1)
                elif name in ("out_a", "out_c"):
                    f, o, w = "f" + name[-1], "o" + name[-1], O0 if name == "out_a" else O1
                    if n == 0:
                        pe.wait_ge(S[f + "_hi"], at(f + "_hi", b, 2))
                        pe.wait_ge(S[f + "_lo"], at(f + "_lo", b, 2))
                    for t in (2 * n, 2 * n + 1):
                        ins = split_product(w_now[:, D * (t % 2):D * (t % 2) + D], tokens(at_hi, at_lo, t),
                                            weights(w))
                    ins.then_inc(S[o + "_mm"], 1)
                    give(o + "_set", b, n + 1)
                elif name == "z1t":
                    turn(w_now, zn, n, token_block, (lambda t: (S["z_b"], at("z_b", b, t + 1))) if n == 0 else None)\
                        .then_inc(S["z1_mm"], 1)
                    give("z1_lo", b, n + 1)
                elif name == "k1":
                    if n == 0:
                        pe.wait_ge(S["z1_hi"], at("z1_hi", b, 2))
                        pe.wait_ge(S["z1_lo"], at("z1_lo", b, 2))
                    split_product(w_now[:, :], weights(K1, slice(P * n, P * n + P)),
                                  tokens(at_hi, at_lo)).then_inc(S["k1_mm"], 1)
                    give("k1_b", b, n + 1)
                elif name == "qv":
                    both = [lambda c: wh[:, Q1:V1 + 1, c, :], lambda c: wl[:, Q1:V1 + 1, c, :]]
                    split_product(w_now[:, :], tokens(at_hi, at_lo, n),
                                  both, bias=slice(D, 3 * D)).then_inc(S["qv_mm"], 1)
                    give("q1_sub", b, n + 1)
                elif name == "k1t":
                    pe.wait_ge(S["k1_n"], at("k1_n", b, n + 1))
                    turn(w_now, k1, n, feature_block).then_inc(S["kt_mm"], 1)
                    give("kt_set", b, n + 1)
                elif name == "q1t":
                    pe.wait_ge(S["q1_exp"], at("q1_exp", b, 1))
                    turn(w_now, q1, n, token_block).then_inc(S["qt_mm"], 1)
                    give("qt_set", b, n + 1)
                elif name == "attn":
                    pe.wait_ge(S["kt_set"], at("kt_set", b, 2))
                    pe.wait_ge(S["v1_set"], at("v1_set", b, 4))
                    for c in range(KC):
                        for t in range(TT):
                            ins = pe.matmul(w_now[:, P * c:P * c + P], v1[:, t, P * c:P * c + P],
                                            yk[:, t, P * c:P * c + P], start=(t == 0), stop=(t == TT - 1))
                    ins.then_inc(S["at_mm"], 1)
                    give("at_set", b, 1)
                elif name == "y1":
                    if n == 0:
                        pe.wait_ge(S["at_set"], at("at_set", b, 1))
                        pe.wait_ge(S["qt_set"], at("qt_set", b, 2))
                    for t in (2 * n, 2 * n + 1):
                        for c in range(KC):
                            o = D * (t % 2) + P * c
                            ins = pe.matmul(w_now[:, o:o + P], q1t[:, c, P * t:P * t + P], attn[:, c, :],
                                            start=True, stop=True)
                    ins.then_inc(S["y1_mm"], 1)
                    give("y1_set", b, 2 * n + 2)
                elif name == "yt":
                    pe.wait_ge(S["y_ev"], at("y_ev", b, n + 1))
                    for t in range(TT):
                        ins = pe.transpose(w_now[:, P * t:P * t + P], yt_sb[:, P * t:P * t + P], ident[:, :])
                    ins.then_inc(S["yt_mm"], 1)
                    give("y_set", b, n + 1)
                elif name == "film_rows":
                    pe.wait_ge(cond_set, 3)
                    pe.wait_ge(emb_in, 32)
                    for c in range(EC):
                        ins = pe.matmul(w_now[0:B, :], cond_s[:, :].rearrange("p (b k) -> p k b", k=EC)[:, c, :],
                                        embw[:, n, c, :], start=(c == 0), stop=(c == EC - 1))
                    ins.then_inc(film_mm, 1)
                    free[bank] = (film_set, n + 1)
                elif name == "film_turn":
                    pe.wait_ge(film_set, 2)
                    for l in range(2):
                        for f in range(2 * KC):
                            o = (2 * KC * l + f) * B
                            ins = pe.transpose(w_now[:, o:o + B], emb_rows[:, l, P * f:P * f + P], ident[0:B, 0:B])
                    ins.then_inc(film_mm, 1)
                    free[bank] = (film_set, 3)
                elif name == "bias_rows":
                    pe.wait_ge(w_late_in, 80)
                    shift_product(w_now[0:1, 0:D] if n == 0 else w_now[0:1, :], NB1,
                                  lambda c: wraw_late[:, 0, c, :] if n == 0 else wraw_late[:, 1:3, c, :])
                    free[bank] = (bias_set, 6 + n)
                elif name == "bias_turn":
                    for c in range(KC):
                        ins = pe.transpose(w_now[:, c:c + 1], brow_late[0:1, 0, P * c:P * c + P], ident[0:1, 0:1])
                    ins.then_inc(bias_mm, 1)
                    free[bank] = (bias_set, 10)

            def maxima_scores(b, h, t):
                g, j = h // HG, h % HG
                if t == 0 and j == 0:
                    pe.wait_ge(fill[h // HG], 160 * (b + 1))
                i = TT * h + t
                if not (isinstance(b, int) and M_COUNT * b + i < M_AGO[i]):
                    pe.wait_ge(S["m_red"], at("m_red", b, i - M_AGO[i] + 1))
                pe.matmul(m_ps[M_BANK[TT * h + t]][:, :], qs[g][0:ROWS_SCORE, j, P * t:P * t + P],
                          ks[g][0:ROWS_SCORE, j, :], start=True, stop=True).then_inc(S["m_mm"], 1)

            def scores(b, k, j):
                g, c = k // TT, k % TT
                if c == 0 and j == 0:
                    pe.wait_ge(c_in[g % 2], 32 * (2 * b + g // 2 + 1))
                if not (isinstance(b, int) and 64 * b + HG * k + j < 2):
                    pe.wait_ge(S["exp"], at("exp", b, HG * k + j - 1))
                pe.matmul(s_ps[j % 2][:, :], ks[g][0:ROWS_SHIFTED, j, P * c:P * c + P],
                          qs[g][0:ROWS_SHIFTED, j, :], start=True, stop=True).then_inc(S["s_mm"], 1)

            def products(b, k):
                g, c = k // TT, k % TT
                if c == 0 and not (isinstance(b, int) and G * b + g < 1):
                    pe.wait_ge(S["y_ev"], at("y_ev", b, g))
                if g == 0:
                    pe.wait_ge(S["v_set"], at("v_set", b, c + 1))
                for j in range(HG):
                    pe.wait_ge(S["exp"], at("exp", b, HG * k + j + 1))
                    v = VW * (HG * g + j)
                    pe.matmul(y_ps[0][M_HEAD * j:M_HEAD * j + M_HEAD, :], v_aug[:, c, v:v + M_HEAD],
                              probs[:, k % 2, j, :], start=(c == 0), stop=(c == TT - 1)).then_inc(S["pv"], 1)

            def step(b, k, first, last):
                for place in range(TT):
                    if not (last and k + LEAD >= H):
                        maxima_scores(b + (k + LEAD) // H, (k + LEAD) % H, place)
                    scores(b, k, place)
                    if place == PV_PLACE and (k > 0 or not first):
                        products(*((b, k - 1) if k > 0 else (b - 1, H - 1)))
                    for name, n, bb in pieces(k, place, b, first, last):
                        piece(name, n, bb)

            def full_step(b, k, first, last):
                if k == 0:
                    for i in range(W_BANKS):
                        free[i] = (S["m_red"], at("m_red", b, TT * LEAD + 1))
                step(b, k, first, last)

            def tail(b):
                products(b, H - 1)
                for i, (_, reader) in enumerate(BANKS):
                    if reader is not None:
                        free[i] = (S[reader], at(reader, b, H * TT))
                for name, n in LAST_ONLY:
                    piece(name, n, b, True)

            pe.wait_ge(ident_set, 2)
            pe.wait_ge(norm_in, 16 * 4)
            pe.transpose(y_ps[0][:, 0:8], nrows[:, :], ident[0:8, 0:8]).then_inc(cols_mm, 1)
            pe.wait_ge(cols_set, 1)
            pe.wait_ge(perm_set, 2)
            shift_product(m_ps[0][0:1, :], NB0, lambda c: wperm[:, :, c, :])
            piece("zt", 0, 0)
            piece("zt", 1, 0)
            pe.wait_ge(bias_set, 1)
            for i in range(2):
                for c in range(KC):
                    ins = pe.transpose(m_ps[1][:, 2 * i + c:2 * i + c + 1], bperm[0:1, i, P * c:P * c + P],
                                       ident[0:1, 0:1])
            ins.then_inc(bias_mm, 1)
            pe.wait_ge(w_lo_set, 4)
            for n in range(4):
                piece("qk", n, 0)
            pe.wait_ge(wv_in, 16)
            shift_product(m_ps[0][0:1, 0:D], NB0, lambda c: wraw[:, V0, c, :])
            pe.wait_ge(vec_in, 16 * 9)
            pe.transpose(y_ps[0][:, 8:56], vrows[:, :], ident[0:48, 0:48]).then_inc(cols_mm, 1)
            pe.wait_ge(hid_rows, 1)
            pe.transpose(y_ps[0][:, 56:56 + B * TT], hrows[:, :], ident[0:B * TT, 0:B * TT]).then_inc(cols_mm, 1)
            pe.wait_ge(bias_set, 5)
            pe.wait_ge(cols_set, 3)
            for h in range(LEAD):
                for t in range(TT):
                    maxima_scores(0, h, t)
                if h == HG:
                    piece("c", 0, 0)
            def prepared():
                pe.wait_ge(w_lo_set, 16)
                pe.wait_ge(film_set, FILM_STEPS)
                pe.wait_ge(bias_set, 10)

            batches(pe, full_step, prepared, tail)


_NAMES = ['x', 'cond_2048', 'mask_BxS_ff1', 'mask_BxS_ik0'] + [
    'L0_cond_' + n for n in ('norm_w', 'norm_b', 'q_w', 'q_b', 'k_w', 'k_b', 'v_w', 'v_b', 'emb_w', 'emb_b',
                             'sb_norm_w', 'sb_norm_b', 'out_w', 'out_b')] + [
    'L1_cond_' + n for n in ('norm_scale', 'norm_bias', 'Wq', 'bq', 'Wk', 'bk', 'Wv', 'bv', 'film_emb_W',
                             'film_emb_b', 'film_norm_scale', 'film_norm_bias', 'film_out_W', 'film_out_b')]


def kernel(**inputs):
    import numpy as _np
    import concourse.bacc as _bacc
    from concourse import mybir as _mybir
    from concourse.bass_utils import run_bass_kernel_spmd as _run

    nc = _bacc.Bacc("TRN2", target_bir_lowering=False, num_devices=1)
    arrays, args = {}, []
    for name in _NAMES:
        a = _np.ascontiguousarray(inputs[name])
        arrays[f"in_{name}"] = a
        args.append(nc.dram_tensor(f"in_{name}", a.shape, _mybir.dt.from_np(a.dtype), kind="ExternalInput").ap())
    result = nc.dram_tensor("out_0", inputs['x'].shape, _mybir.dt.float32, kind="ExternalOutput").ap()
    film_seq_kernel(nc, *args, result)
    r = _run(nc, [arrays], core_ids=[0])
    return r.results[0]["out_0"]
```
